# Optimizing a Trainium2 kernel written in Bass

```python
import numpy as np
import jax
import jax.numpy as jnp

def _softmax(x, axis=-1):
    return jax.nn.softmax(x, axis=axis)

def _gelu(x):
    return jax.nn.gelu(x, approximate=True)

def _silu(x):
    return jax.nn.silu(x)

def _sigmoid(x):
    return jax.nn.sigmoid(x)

def _layernorm(x, axis=-1, eps=1e-05):
    m = jnp.mean(x, axis=axis, keepdims=True)
    v = jnp.var(x, axis=axis, keepdims=True)
    return (x - m) / jnp.sqrt(v + eps)

def _scatter_add(tgt, idx, src, axis=0):
    return tgt.at[idx].add(src)

def _segment_sum(src, seg, n):
    return jax.ops.segment_sum(src, seg, n)
kernel_name = 'mk_gnn_preln_d4_gnn_r8_addc15'

def setup_inputs(seed: int=0):
    np.random.seed(seed)
    _w = jnp.asarray

    def _rec_inputs():
        import jax
        import jax.numpy as jnp
        _gk = jax.random.key(seed)
        x = -0.0009044 + 1 * jax.random.normal(jax.random.fold_in(_gk, 1), (12500, 32), jnp.float32)
        src = jax.random.randint(jax.random.fold_in(_gk, 2), (200000,), 0, 12500, jnp.int32)
        dst = jnp.minimum((12500 * jax.random.uniform(jax.random.fold_in(_gk, 3), (200000,)) ** 2.0).astype(jnp.int32), 99999)
        _o = jnp.argsort(dst, stable=True)
        src = src[_o]
        dst = dst[_o]
        edge_attr_10 = jax.random.uniform(jax.random.fold_in(_gk, 12), (200000, 10), jnp.float32, 0.0, 1)
        edge_attr_3 = 0.00109039 + 0.999626 * jax.random.normal(jax.random.fold_in(_gk, 13), (200000, 3), jnp.float32)
        edge_attr_32 = 0.000196303 + 1.00016 * jax.random.normal(jax.random.fold_in(_gk, 14), (200000, 32), jnp.float32)
        edge_weight = jax.random.uniform(jax.random.fold_in(_gk, 16), (200000,), jnp.float32, 0.0, 0.999997)
        return (x, src, dst, edge_attr_10, edge_attr_3, edge_attr_32, edge_weight)
    x, src, dst, edge_attr_10, edge_attr_3, edge_attr_32, edge_weight = _rec_inputs()

    def _L0_gnn_setup():
        import jax, jax.numpy as jnp
        import numpy as np
        N_NODES = 6250
        N_EDGES = 100000
        X_DIM = 32
        E_DIM = 32
        HID = 64
        OUT = 32
        key = jax.random.key(seed)
        ks = jax.random.split(key, 6)
        x = jax.random.normal(ks[0], (N_NODES, X_DIM), dtype=jnp.float32)
        edge_index = jax.random.randint(ks[1], (2, N_EDGES), 0, N_NODES, dtype=jnp.int64)
        edge_attr = jax.random.normal(ks[2], (N_EDGES, E_DIM), dtype=jnp.float32)
        in_dim = 2 * X_DIM + E_DIM
        W1 = jax.random.normal(ks[3], (in_dim, HID), dtype=jnp.float32) * (1.0 / np.sqrt(in_dim))
        b1 = jnp.zeros((HID,), dtype=jnp.float32)
        W2 = jax.random.normal(ks[4], (HID, OUT), dtype=jnp.float32) * (1.0 / np.sqrt(HID))
        b2 = jnp.zeros((OUT,), dtype=jnp.float32)
        return {'x': x, 'edge_index': edge_index, 'edge_attr': edge_attr, 'W1': W1, 'b1': b1, 'W2': W2, 'b2': b2}
    _L0_gnn_all = _L0_gnn_setup()
    _L0_gnn_in = {k: v for k, v in _L0_gnn_all.items() if k in ('W1', 'b1', 'W2', 'b2')}
    del _L0_gnn_all

    def _L1_gnn_setup():
        import jax, jax.numpy as jnp
        import numpy as np
        N_NODES = 12500
        N_EDGES = 200000
        DIM1 = 32
        LEAKY_SLOPE = 0.01
        key = jax.random.key(seed)
        k1, k2, k3, k4 = jax.random.split(key, 4)
        h = jax.random.normal(k1, (N_NODES, DIM1), dtype=jnp.float32)
        attn_w = jax.random.normal(k2, (2 * DIM1,), dtype=jnp.float32) * (1.0 / np.sqrt(2 * DIM1))
        src = jax.random.randint(k3, (N_EDGES,), 0, N_NODES, dtype=jnp.int32)
        dst = jax.random.randint(k4, (N_EDGES,), 0, N_NODES, dtype=jnp.int32)
        return {'h': h, 'attn_w': attn_w, 'src': src, 'dst': dst}
    _L1_gnn_all = _L1_gnn_setup()
    _L1_gnn_in = {k: v for k, v in _L1_gnn_all.items() if k in ('attn_w',)}
    del _L1_gnn_all

    def _L2_gnn_setup():
        import jax, jax.numpy as jnp
        import numpy as np
        MUL = 16
        MOUT = 8
        TANH_GAIN = 1.593
        INV_SQRT3 = 0.5773502691896258
        PW_S = 0.17677669529663687
        PW_V = 0.25

        def _w3j_121():
            s2, s6 = (2 ** 0.5, 6 ** 0.5)
            M = np.zeros((5, 3, 3))
            M[0, 0, 1] = M[0, 1, 0] = 1 / s2
            M[1, 1, 2] = M[1, 2, 1] = 1 / s2
            M[2] = np.diag([-1.0, -1.0, 2.0]) / s6
            M[3, 0, 2] = M[3, 2, 0] = 1 / s2
            M[4] = np.diag([1.0, -1.0, 0.0]) / s2
            return jnp.asarray(np.transpose(M, (1, 0, 2)) / 5 ** 0.5, jnp.float32)
        W3J121 = _w3j_121()

        def _sph(edge_vec):
            n = edge_vec / jnp.linalg.norm(edge_vec, axis=1, keepdims=True)
            x, y, z = (n[:, 0], n[:, 1], n[:, 2])
            y1 = 3.0 ** 0.5 * n
            s15 = 15.0 ** 0.5
            y2 = jnp.stack([s15 * x * y, s15 * y * z, 5.0 ** 0.5 / 2 * (3 * z * z - 1), s15 * x * z, s15 / 2 * (x * x - y * y)], axis=1)
            return (y1, y2)

        def _forward(x, edge_src, edge_dst, edge_vec, emb, norm, W1, W2):
            N, E = (x.shape[0], edge_src.shape[0])
            xs = jnp.concatenate([x[edge_src, :8], x[edge_dst, :8]], axis=1)
            xv = jnp.concatenate([x[edge_src, 8:].reshape(E, 8, 3), x[edge_dst, 8:].reshape(E, 8, 3)], axis=1)
            y1, y2 = _sph(edge_vec)
            h = 2.0 ** 0.5 * jax.nn.relu(emb @ W1 / 10.0 ** 0.5)
            w = (h @ W2 / 16.0 ** 0.5).reshape(E, 7, MUL, MOUT)
            wa_s, wb_s, wa_g, wb_g, wc, wd, we = [w[:, i] for i in range(7)]
            s_out = PW_S * (jnp.einsum('eu,euw->ew', xs, wa_s) + INV_SQRT3 * jnp.einsum('eui,ei,euw->ew', xv, y1, wb_s))
            g_out = PW_S * (jnp.einsum('eu,euw->ew', xs, wa_g) + INV_SQRT3 * jnp.einsum('eui,ei,euw->ew', xv, y1, wb_g))
            v_out = PW_V * (INV_SQRT3 * jnp.einsum('eu,ek,euw->ewk', xs, y1, wc) + INV_SQRT3 * jnp.einsum('eui,euw->ewi', xv, wd) + jnp.einsum('eui,ea,iak,euw->ewk', xv, y2, W3J121, we))
            s_act = TANH_GAIN * jnp.tanh(s_out)
            gates = TANH_GAIN * jnp.tanh(g_out)
            edge_ftr = jnp.concatenate([s_act, (gates[:, :, None] * v_out).reshape(E, 24)], axis=1) * norm[:, None]
            return jax.ops.segment_sum(edge_ftr, edge_dst, num_segments=N)
        key = jax.random.key(seed)
        ks = jax.random.split(key, 8)
        N, E = (6250, 37500)
        return {'x': jax.random.normal(ks[0], (N, 32), jnp.float32), 'edge_src': jax.random.randint(ks[1], (E,), 0, N), 'edge_dst': jax.random.randint(ks[2], (E,), 0, N), 'edge_vec': jax.random.normal(ks[3], (E, 3), jnp.float32), 'emb': jax.random.uniform(ks[4], (E, 10), jnp.float32), 'norm': jax.random.uniform(ks[5], (E,), jnp.float32), 'W1': jax.random.normal(ks[6], (10, 16), jnp.float32), 'W2': jax.random.normal(ks[7], (16, 896), jnp.float32)}
    _L2_gnn_all = _L2_gnn_setup()
    _L2_gnn_in = {k: v for k, v in _L2_gnn_all.items() if k in ('W1', 'W2')}
    del _L2_gnn_all

    def _L3_gnn_setup():
        import jax, jax.numpy as jnp
        import numpy as np
        N_NODES = 12500
        N_EDGES = 200000
        EMB = 32
        HID = 64

        def gcn_conv(x, W, b, row, col, n_nodes):
            xw = x @ W
            ones = jnp.ones(row.shape[0], dtype=x.dtype)
            deg = jax.ops.segment_sum(ones, col, num_segments=n_nodes)
            dinv = jnp.where(deg > 0, jax.lax.rsqrt(deg), 0.0)
            norm = dinv[row] * dinv[col]
            msgs = norm[:, None] * xw[row]
            out = jax.ops.segment_sum(msgs, col, num_segments=n_nodes)
            return out + b
        key = jax.random.key(seed)
        k1, k2, k3, k4, k5, k6 = jax.random.split(key, 6)
        x = jax.random.normal(k1, (N_NODES, EMB), dtype=jnp.float32)
        edge_index = jax.random.randint(k2, (2, N_EDGES), 0, N_NODES, dtype=jnp.int64)
        W1 = jax.random.normal(k3, (EMB, HID), dtype=jnp.float32) / np.sqrt(EMB)
        b1 = jnp.zeros((HID,), dtype=jnp.float32)
        W2 = jax.random.normal(k4, (HID, EMB), dtype=jnp.float32) / np.sqrt(HID)
        b2 = jnp.zeros((EMB,), dtype=jnp.float32)
        return {'x': x, 'edge_index': edge_index, 'W1': W1, 'b1': b1, 'W2': W2, 'b2': b2}
    _L3_gnn_all = _L3_gnn_setup()
    _L3_gnn_in = {k: v for k, v in _L3_gnn_all.items() if k in ('W1', 'b1', 'W2', 'b2')}
    del _L3_gnn_all
    return {'x': x, 'src': src, 'dst': dst, 'edge_attr_10': edge_attr_10, 'edge_attr_3': edge_attr_3, 'edge_attr_32': edge_attr_32, 'edge_weight': edge_weight, 'L0_gnn_W1': _L0_gnn_in['W1'], 'L0_gnn_b1': _L0_gnn_in['b1'], 'L0_gnn_W2': _L0_gnn_in['W2'], 'L0_gnn_b2': _L0_gnn_in['b2'], 'L1_gnn_attn_w': _L1_gnn_in['attn_w'], 'L2_gnn_W1': _L2_gnn_in['W1'], 'L2_gnn_W2': _L2_gnn_in['W2'], 'L3_gnn_W1': _L3_gnn_in['W1'], 'L3_gnn_b1': _L3_gnn_in['b1'], 'L3_gnn_W2': _L3_gnn_in['W2'], 'L3_gnn_b2': _L3_gnn_in['b2']}

def reference(x, src, dst, edge_attr_10, edge_attr_3, edge_attr_32, edge_weight, L0_gnn_W1, L0_gnn_b1, L0_gnn_W2, L0_gnn_b2, L1_gnn_attn_w, L2_gnn_W1, L2_gnn_W2, L3_gnn_W1, L3_gnn_b1, L3_gnn_W2, L3_gnn_b2):
    import jax
    import jax.numpy as jnp

    def _L0_gnn_ref(x, edge_index, edge_attr, W1, b1, W2, b2):
        import jax, jax.numpy as jnp
        import numpy as np
        N_NODES = 6250
        N_EDGES = 100000
        X_DIM = 32
        E_DIM = 32
        HID = 64
        OUT = 32
        num_nodes = x.shape[0]
        rol, col = (edge_index[0], edge_index[1])
        e_feat = jnp.concatenate([x[rol], x[col], edge_attr], axis=-1)
        h = jax.nn.relu(e_feat @ W1 + b1)
        v = h @ W2 + b2
        x_cand = jax.ops.segment_max(v, col, num_segments=num_nodes)
        return jnp.maximum(x_cand, x[:, -v.shape[-1]:])

    def _L1_gnn_ref(h, attn_w, src, dst):
        import jax, jax.numpy as jnp
        import numpy as np
        N_NODES = 12500
        N_EDGES = 200000
        DIM1 = 32
        LEAKY_SLOPE = 0.01
        N, d = h.shape
        s_src = h @ attn_w[:d]
        s_dst = h @ attn_w[d:]
        e = s_src[src] + s_dst[dst]
        e = jnp.where(e >= 0, e, LEAKY_SLOPE * e)
        m = jax.ops.segment_max(e, dst, num_segments=N)
        ex = jnp.exp(e - m[dst])
        denom = jax.ops.segment_sum(ex, dst, num_segments=N)
        alpha = ex / denom[dst]
        out = jax.ops.segment_sum(h[src] * alpha[:, None], dst, num_segments=N)
        return out

    def _L2_gnn_ref(x, edge_src, edge_dst, edge_vec, emb, norm, W1, W2):
        import jax, jax.numpy as jnp
        import numpy as np
        MUL = 16
        MOUT = 8
        TANH_GAIN = 1.593
        INV_SQRT3 = 0.5773502691896258
        PW_S = 0.17677669529663687
        PW_V = 0.25

        def _w3j_121():
            s2, s6 = (2 ** 0.5, 6 ** 0.5)
            M = np.zeros((5, 3, 3))
            M[0, 0, 1] = M[0, 1, 0] = 1 / s2
            M[1, 1, 2] = M[1, 2, 1] = 1 / s2
            M[2] = np.diag([-1.0, -1.0, 2.0]) / s6
            M[3, 0, 2] = M[3, 2, 0] = 1 / s2
            M[4] = np.diag([1.0, -1.0, 0.0]) / s2
            return jnp.asarray(np.transpose(M, (1, 0, 2)) / 5 ** 0.5, jnp.float32)
        W3J121 = _w3j_121()

        def _sph(edge_vec):
            n = edge_vec / jnp.linalg.norm(edge_vec, axis=1, keepdims=True)
            x, y, z = (n[:, 0], n[:, 1], n[:, 2])
            y1 = 3.0 ** 0.5 * n
            s15 = 15.0 ** 0.5
            y2 = jnp.stack([s15 * x * y, s15 * y * z, 5.0 ** 0.5 / 2 * (3 * z * z - 1), s15 * x * z, s15 / 2 * (x * x - y * y)], axis=1)
            return (y1, y2)

        def _forward(x, edge_src, edge_dst, edge_vec, emb, norm, W1, W2):
            N, E = (x.shape[0], edge_src.shape[0])
            xs = jnp.concatenate([x[edge_src, :8], x[edge_dst, :8]], axis=1)
            xv = jnp.concatenate([x[edge_src, 8:].reshape(E, 8, 3), x[edge_dst, 8:].reshape(E, 8, 3)], axis=1)
            y1, y2 = _sph(edge_vec)
            h = 2.0 ** 0.5 * jax.nn.relu(emb @ W1 / 10.0 ** 0.5)
            w = (h @ W2 / 16.0 ** 0.5).reshape(E, 7, MUL, MOUT)
            wa_s, wb_s, wa_g, wb_g, wc, wd, we = [w[:, i] for i in range(7)]
            s_out = PW_S * (jnp.einsum('eu,euw->ew', xs, wa_s) + INV_SQRT3 * jnp.einsum('eui,ei,euw->ew', xv, y1, wb_s))
            g_out = PW_S * (jnp.einsum('eu,euw->ew', xs, wa_g) + INV_SQRT3 * jnp.einsum('eui,ei,euw->ew', xv, y1, wb_g))
            v_out = PW_V * (INV_SQRT3 * jnp.einsum('eu,ek,euw->ewk', xs, y1, wc) + INV_SQRT3 * jnp.einsum('eui,euw->ewi', xv, wd) + jnp.einsum('eui,ea,iak,euw->ewk', xv, y2, W3J121, we))
            s_act = TANH_GAIN * jnp.tanh(s_out)
            gates = TANH_GAIN * jnp.tanh(g_out)
            edge_ftr = jnp.concatenate([s_act, (gates[:, :, None] * v_out).reshape(E, 24)], axis=1) * norm[:, None]
            return jax.ops.segment_sum(edge_ftr, edge_dst, num_segments=N)
        return _forward(x, edge_src, edge_dst, edge_vec, emb, norm, W1, W2)

    def _L3_gnn_ref(x, edge_index, W1, b1, W2, b2):
        import jax, jax.numpy as jnp
        import numpy as np
        N_NODES = 12500
        N_EDGES = 200000
        EMB = 32
        HID = 64

        def gcn_conv(x, W, b, row, col, n_nodes):
            xw = x @ W
            ones = jnp.ones(row.shape[0], dtype=x.dtype)
            deg = jax.ops.segment_sum(ones, col, num_segments=n_nodes)
            dinv = jnp.where(deg > 0, jax.lax.rsqrt(deg), 0.0)
            norm = dinv[row] * dinv[col]
            msgs = norm[:, None] * xw[row]
            out = jax.ops.segment_sum(msgs, col, num_segments=n_nodes)
            return out + b
        n = x.shape[0]
        loops = jnp.arange(n, dtype=edge_index.dtype)
        row = jnp.concatenate([edge_index[0], loops])
        col = jnp.concatenate([edge_index[1], loops])
        h = jax.nn.relu(gcn_conv(x, W1, b1, row, col, n))
        h = jax.nn.relu(gcn_conv(h, W2, b2, row, col, n))
        return h
    edge_index = jnp.stack([src, dst])
    h = jnp.maximum(_layernorm(x, axis=-1), 0.0)
    x = x + _L0_gnn_ref(h, edge_index, edge_attr_32, L0_gnn_W1, L0_gnn_b1, L0_gnn_W2, L0_gnn_b2)
    h = jnp.maximum(_layernorm(x, axis=-1), 0.0)
    x = x + _L1_gnn_ref(h, L1_gnn_attn_w, src, dst)
    h = jnp.maximum(_layernorm(x, axis=-1), 0.0)
    x = x + _L2_gnn_ref(h, src, dst, edge_attr_3, edge_attr_10, edge_weight, L2_gnn_W1, L2_gnn_W2)
    h = jnp.maximum(_layernorm(x, axis=-1), 0.0)
    x = x + _L3_gnn_ref(h, edge_index, L3_gnn_W1, L3_gnn_b1, L3_gnn_W2, L3_gnn_b2)
    return x

_drawn_inputs = setup_inputs


def setup_inputs(seed=0):
    import zlib

    import numpy as np

    out = dict(_drawn_inputs(seed))
    spreads = {'L0_gnn_b1': (0.0, 0.1),
     'L0_gnn_b2': (0.0, 0.1),
     'L3_gnn_b1': (0.0, 0.282),
     'L3_gnn_b2': (0.0, 0.298)}
    factors = {'L1_gnn_attn_w': 5.1}
    for name, (base, spread) in spreads.items():
        noise = np.random.default_rng([zlib.crc32(name.encode()), seed]).standard_normal(out[name].shape)
        drawn = base * np.exp(spread * noise) if base else spread * noise
        out[name] = jnp.asarray(drawn.astype(out[name].dtype))
    for name, factor in factors.items():
        out[name] = (out[name] * factor).astype(out[name].dtype)
    return out
```

```python
from contextlib import ExitStack

import numpy as np
import concourse.bass as bass
from concourse import mybir

P = 128
N, E, F = 12500, 200000, 32
NP_REAL = 125
NT = N // NP_REAL
NPAD = P * NT
JC = 56
NCH = 28
J = JC * NCH
EP = P * J
HALF = NCH // 2
G = 4
NG = JC // G
ZW = 96
ZE = 90
AW = 34
RW = 33
HC = 14
BIG = 1.0e38
EPS = 1e-5
TANH_GAIN = 1.593
PW_S, PW_V = 0.17677669529663687, 0.25
ALPHA = 2.0 ** 0.5 / 10.0 ** 0.5 / 4.0
LEAKY = 0.01

ALU = mybir.AluOpType
ACT = mybir.ActivationFunctionType
AX = mybir.AxisListType
F32 = mybir.dt.float32
I32 = mybir.dt.int32
BF16 = mybir.dt.bfloat16


def after(eng, sem, value):
    if isinstance(value, int) and value <= 0:
        return
    eng.wait_ge(sem, value)


class Steps:

    def __init__(self, eng, sem, base=0):
        self.eng, self.sem, self.base, self.k = eng, sem, base, 0

    def done(self, ins):
        self.k += 1
        ins.then_inc(self.sem, 1)
        return self.k

    def settle(self):
        after(self.eng, self.sem, self.base + self.k)


def graph_kernel(nc, d, out):
    with ExitStack() as ctx:
        def sb(name, shape, dt=F32):
            return ctx.enter_context(nc.sbuf_tensor(name, shape, dt))

        sems = {}

        def sem(name):
            if name not in sems:
                sems[name] = ctx.enter_context(nc.semaphore(name))
            return sems[name]

        def dram(name, shape, dt=F32):
            return nc.dram_tensor(name, shape, dt).ap()

        spread = dram("spread", (EP + NPAD, F))
        spread1 = dram("spread1", (EP + NPAD, 1))
        end_table = dram("end_table", (NPAD, 1), I32)
        table = {0: dram("table0", (NPAD, F)), 1: dram("table1", (NPAD, AW)),
                 2: dram("table2", (NPAD, F)), 3: dram("table3", (NPAD, F)),
                 4: dram("table4", (NPAD, F))}
        width = {0: F, 1: RW, 2: F, 3: F, 4: F}
        rows = {k: dram(f"rows{k}", (EP + P, width[k])) for k in width}
        stash = dram("stash", (EP, AW))

        x = sb("x", [P, NT, F])
        prod_f = sb("prod", [P, 2 * 7 * 512])
        prod = prod_f[:, :].rearrange("p (b a e) -> p b a e", b=2, a=7)
        h = prod_f[:, 0:NT * F].rearrange("p (t f) -> p t f", f=F)
        zero = prod_f[:, NT * F:NT * F + J]
        hot = prod_f[:, 0:HC * (P + NT)].bitcast(BF16).rearrange("p (k w) -> p k w", w=P + NT)
        fetched = sb("fetched", [P, NT * RW])
        att = sb("att", [P, NT * AW])
        zin = sb("zin", [P, 2, JC * ZW])
        zout = sb("zout", [P, 2, JC * RW])
        keep = sb("keep", [P, J])
        pen = sb("pen", [P, J])
        ea = sb("ea", [P, 6, J])
        dst0 = sb("dst0", [P, 1], I32)
        idx = sb("idx", [P, 2, JC], I32)
        start_idx = sb("start_idx", [P, NT], I32)
        end_idx = sb("end_idx", [P, NT], I32)
        fix_idx = sb("fix_idx", [P, 1], I32)
        fix_end = sb("fix_end", [P, 1], I32)
        has = sb("has", [P, NT])
        nohas = sb("nohas", [P, NT])
        dinv = sb("dinv", [P, NT])
        n1 = sb("n1", [P, NT])
        n2 = sb("n2", [P, NT])
        n3 = sb("n3", [P, NT])
        c1 = sb("c1", [P, 1])
        c2 = sb("c2", [P, 1])
        c3 = sb("c3", [P, 1])
        krow = sb("krow", [RW, P])
        penkrow = sb("penkrow", [RW, P])
        bkrow = sb("bkrow", [1, P])
        kcols = sb("kcols", [P, RW])
        rowa = sb("rowa", [RW, P])
        rowb = sb("rowb", [RW, P])
        rowc = sb("rowc", [RW, P])
        carry_in = sb("carry_in", [P, F])
        carry = sb("carry", [P, RW])
        fix = sb("fix", [P, AW])
        ident = sb("ident", [P, P])
        before = sb("before", [P, P])
        dump = sb("dump", [P, 1])
        dump_n = sb("dump_n", [P, NT])
        plimit = sb("plimit", [P, 1])
        iota_f = sb("iota_f", [P, P])
        iota_b = sb("iota_b", [P, P], BF16)
        w01 = sb("w01", [3 * F, 64])
        w02 = sb("w02", [64, F])
        b01 = sb("b01", [64, 1])
        b02 = sb("b02", [P, F])
        aw = sb("aw", [P, 2 * F])
        w31 = sb("w31", [F, 64])
        w32 = sb("w32", [64, F])
        b31 = sb("b31", [64, 1])
        b32 = sb("b32", [P, F])
        w1rep = sb("w1rep", [ZE, P])
        sel = sb("sel", [ZE, 7, P])
        wa = sb("wa", [P, 4, 24])
        wd = sb("wd", [16, P])
        we = sb("we", [16, P])
        sumw = sb("sumw", [P, 8])
        tz = sb("tz", [ZW, 2, 512])
        hid = sb("hid", [P, 2, 512])
        dw = sb("dw", [P, 2, 512])
        qtemp = sb("qtemp", [P, 2 * JC * 16])
        eo = [t[:, 0:JC * 48].rearrange("p (j w) -> p j w", w=48) for t in (att, fetched)]

        bank = [ctx.enter_context(nc.psum_tensor(f"bank{i}", [P, 512], F32)) for i in range(8)]


        def zrow(b, w):
            return zin[:, b, 0:JC * w].rearrange("p (j w) -> p j w", w=w)

        def orow(b, w):
            return zout[:, b, 0:JC * w].rearrange("p (j w) -> p j w", w=w)

        def orow_flat(b, w):
            return zout[:, b, 0:JC * w]

        def hold(eng, semaphore, value):
            after(eng, semaphore, value)
            if not isinstance(value, int):
                eng.sem_inc(sem("gate"))

        def block_bank(b, g, a):
            return 2 + (7 * (b * NG + g) + a) % 4

        def chunks(eng, body):
            for b in range(2):
                body(0, b, b)
            with eng.Fori(1, HALF) as i:
                for b in range(2):
                    body(i, b, 2 * i + b)

        def cols(c):
            return slice(c * JC, (c + 1) * JC) if isinstance(c, int) else bass.ds(c * JC, JC)

        consts = [(w01[:, :], d["w01"]), (w02[:, :], d["w02"]), (b01[:, :], d["b01"]), (b02[:, :], d["b02"]),
                  (aw[:, :], d["aw"]), (w31[:, :], d["w31"]), (w32[:, :], d["w32"]), (b31[:, :], d["b31"]),
                  (b32[:, :], d["b32"]), (w1rep[:, :], d["w1rep"]), (sel[:, :, :], d["sel"]),
                  (wa[:, :, :], d["wa"]), (wd[:, :], d["wd"]), (we[:, :], d["we"]), (sumw[:, :], d["sumw"]),
                  (ident[:, :], d["ident"]), (before[:, :], d["before"]), (dump[:, :], d["dump"]), (dump_n[:, :], d["dump_n"]),
                  (plimit[:, :], d["plimit"]), (iota_f[:, :], d["iota"])]
        fetch = {k: fetched[:, 0:NT * width[k]].rearrange("p (t w) -> p t w", w=width[k])
                 for k in width}
        att3 = att[:, :].rearrange("p (t w) -> p t w", w=AW)
        scratch = att[:, 0:NT * F].rearrange("p (t w) -> p t w", w=F)
        dst_i, prev_i, next_i = (fetched[:, 0:J].bitcast(I32), fetched[:, J:2 * J].bitcast(I32),
                                 zout[:, :, :].rearrange("p b w -> p (b w)")[:, 0:J].bitcast(I32))

        block = ctx.enter_context(nc.Block())

        @block.sync
        def _(sp):
            for dst, src in ((dst_i, d["dst"][1:1 + EP]), (prev_i, d["dst"][0:EP]),
                             (next_i, d["dst"][2:2 + EP])):
                sp.dma_start(dst, src.rearrange("(p j) -> p j", j=J)).then_inc(sem("dst_loaded"), 16)
            sp.wait_ge(sem("x_cleared"), 1)
            sp.dma_start(x[0:NP_REAL], d["x"].rearrange("(p t) f -> p t f", t=NT)
                         ).then_inc(sem("x_loaded"), 16)
            for dst, src in consts:
                sp.dma_start(dst, src).then_inc(sem("consts_loaded"), 16)
            sp.wait_ge(sem("zero_ready"), 1)
            sp.dma_start(spread1[0:EP].rearrange("(p j) w -> p (j w)", j=J), zero[:, :]
                         ).then_inc(sem("filled"), 16)
            for k in range(F):
                sp.dma_start(spread[0:EP].rearrange("(p c j) w -> p c (j w)", p=P, c=F)[:, k], zero[:, :]
                             ).then_inc(sem("filled"), 16)
            for k in width:
                sp.dma_start(rows[k][EP:EP + P], zero[:, 0:width[k]]).then_inc(sem("filled"), 16)
            sp.wait_ge(sem("end_idx_ready"), 1)
            sp.dma_start(end_table.rearrange("(p t) w -> p (t w)", t=NT), end_idx[:, :]
                         ).then_inc(sem("end_table_stored"), 16)

            def store_table(k, tile):
                if k == 4:
                    sp.wait_ge(sem("out_copied3"), NT // G)
                else:
                    sp.wait_ge(sem("table_ready"), k + 1)
                sp.dma_start(table[k].rearrange("(p t) w -> p (t w)", t=NT), tile
                             ).then_inc(sem("table_stored"), 16)

            def load_idx(k, b, c):
                sp.dma_start(idx[:, b], d["src"][:, cols(c)]).then_inc(sem(f"idx_loaded{b}"), 16)

            def store_rows(k, i, b, c):
                hold(sp, sem("scanned"), NCH * k + c + 1)
                sp.dma_start(rows[k][0:EP].rearrange("(p j) w -> p (j w)", j=J)[
                    :, wcols(c, width[k])], orow_flat(b, width[k])).then_inc(sem(f"stored{b}"), 16)

            def wcols(c, w):
                return slice(c * JC * w, (c + 1) * JC * w) if isinstance(c, int) else bass.ds(c * JC * w, JC * w)

            def later_store(k, i, b, c):
                if b == 1:
                    store_rows(k, i, 0, c - 1)
                elif not isinstance(i, int):
                    store_rows(k, i - 1, 1, c - 1)

            def spread_rows(b, c):
                return spread[0:EP].rearrange("(p j) w -> p j w", j=J)[:, cols(c), :]

            store_table(0, h[:, :, :].rearrange("p t f -> p (t f)"))

            def body0(i, b, c):
                hold(sp, sem("transposed0"), NG * (c - 1))
                load_idx(0, b, c)
                sp.dma_start(zrow(b, ZW)[:, :, 2 * F:3 * F],
                             d["a32"].rearrange("(p j) w -> p j w", j=J)[:, cols(c), :]
                             ).then_inc(sem(f"loaded0_{b}"), 16)
                if isinstance(i, int) and b == 0:
                    sp.wait_ge(sem("spread"), 16 * NT * 1)
                sp.dma_start(zrow(b, ZW)[:, :, F:2 * F], spread_rows(b, c)
                             ).then_inc(sem(f"loaded0_{b}"), 16)
                later_store(0, i, b, c)
            chunks(sp, body0)
            store_rows(0, HALF - 1, 1, NCH - 1)

            store_table(1, att[:, :])

            def body1(i, b, c):
                hold(sp, sem("score_copied"), c - 1)
                if not (isinstance(i, int)):
                    sp.wait_ge(sem(f"stashed{b}"), 16 * i)
                load_idx(1, b, c)
                if b == 1:
                    stash_rows(i, 0, c - 1)
                elif not isinstance(i, int):
                    stash_rows(i - 1, 1, c - 1)

            def stash_rows(i, b, c):
                hold(sp, sem(f"gathered1_{b}"), 16 * JC * (i + 1))
                sp.dma_start(stash.rearrange("(p j) w -> p (j w)", j=J)[:, wcols(c, AW)],
                             zin[:, b, 0:JC * AW]).then_inc(sem(f"stashed{b}"), 16)
            chunks(sp, body1)
            stash_rows(HALF - 1, 1, NCH - 1)
            sp.wait_ge(sem("spread"), 16 * NT * 2)
            sp.wait_ge(sem("table_ready"), 2)
            sp.dma_start(ea[:, 1], spread1[0:EP].rearrange("(p j) w -> p (j w)", j=J)
                         ).then_inc(sem("spread1_loaded"), 16)
            for b in range(2):
                sp.wait_ge(sem(f"stashed{b}"), 16 * HALF)

            def body1b(i, b, c):
                if isinstance(i, int) and b == 0:
                    sp.wait_ge(sem("score_copied"), NCH)
                hold(sp, sem("weighted"), c - 1)
                sp.dma_start(zin[:, b, 0:JC * AW],
                             stash.rearrange("(p j) w -> p (j w)", j=J)[:, wcols(c, AW)]
                             ).then_inc(sem(f"loaded1_{b}"), 16)
                later_store(1, i, b, c)
            chunks(sp, body1b)
            store_rows(1, HALF - 1, 1, NCH - 1)

            sp.wait_ge(sem("scanned"), 2 * NCH)
            sp.dma_start(zin[:, :, :].rearrange("p b w -> p (b w)")[:, 0:3 * J],
                         d["a3"].rearrange("(p j) w -> p (j w)", j=J)).then_inc(sem("vec_loaded"), 16)
            sp.dma_start(ea[:, 3], d["wgt"].rearrange("(p j) -> p j", j=J)).then_inc(sem("vec_loaded"), 16)
            store_table(2, h[:, :, :].rearrange("p t f -> p (t f)"))
            sp.wait_ge(sem("vec_read"), 1)

            def body2(i, b, c):
                hold(sp, sem("transposed2"), NG * (c - 1))
                load_idx(2, b, c)
                sp.dma_start(zrow(b, ZE)[:, :, 80:90],
                             d["a10"].rearrange("(p j) w -> p j w", j=J)[:, cols(c), :]
                             ).then_inc(sem(f"loaded2_{b}"), 16)
                if isinstance(i, int) and b == 0:
                    sp.wait_ge(sem("spread"), 16 * NT * 3)
                sp.dma_start(zrow(b, ZE)[:, :, F:2 * F], spread_rows(b, c)
                             ).then_inc(sem(f"loaded2_{b}"), 16)
                later_store(2, i, b, c)
            chunks(sp, body2)
            store_rows(2, HALF - 1, 1, NCH - 1)

            for k in (3, 4):
                store_table(k, h[:, :, :].rearrange("p t f -> p (t f)"))

                def body3(i, b, c):
                    hold(sp, sem("scanned"), NCH * k + c - 1)
                    load_idx(k, b, c)
                    later_store(k, i, b, c)
                chunks(sp, body3)
                store_rows(k, HALF - 1, 1, NCH - 1)

            sp.wait_ge(sem("x_final"), 1)
            sp.dma_start(out.rearrange("(p t) f -> p t f", t=NT), x[0:NP_REAL]).then_inc(sem("out_stored"), 16)
            sp.wait_ge(sem("out_stored"), 16)

        @block.gpsimd
        def _(pool):
            def take(dst, src, index):
                return pool.indirect_dma_start(out=dst, out_offset=None, in_=src,
                                               in_offset=bass.IndirectOffsetOnAxis(ap=index, axis=0))

            def put(dst, index, src):
                return pool.indirect_dma_start(out=dst, out_offset=bass.IndirectOffsetOnAxis(ap=index, axis=0),
                                               in_=src, in_offset=None)

            def gather(k, w, row_width, used, also=None):
                pool.wait_ge(sem("table_stored"), 16 * (k + 1))

                def body(i, b, c):
                    hold(pool, sem(f"idx_loaded{b}"), 16 * (HALF * k + i + 1))
                    for j in range(JC):
                        take(zrow(b, row_width)[:, j, 0:w], table[k], idx[:, b, j:j + 1]
                             ).then_inc(sem(f"gathered{k}_{b}"), 16)
                chunks(pool, body)

            def fix_and_fetch(k):
                w = width[k]
                for b in range(2):
                    pool.wait_ge(sem(f"stored{b}"), 16 * HALF * (k + 1))
                take(fix[:, 0:w], rows[k], fix_idx[:, 0:1]).then_inc(sem("fix_fetched"), 16)
                pool.wait_ge(sem("fix_ready"), k + 1)
                put(rows[k], fix_idx[:, 0:1], fix[:, 0:w]).then_inc(sem("fix_stored"), 16)
                pool.wait_ge(sem("fix_stored"), 16 * (k + 1))
                for t in range(NT):
                    take(fetch[k][:, t, :], rows[k], end_idx[:, t:t + 1]).then_inc(sem("fetched"), 16)

            def spread_nodes(k, tile, where, first, w):
                pool.wait_ge(sem("table_ready"), k + 1)
                for t in range(NT):
                    put(where, start_idx[:, t:t + 1], tile(t)).then_inc(sem("spread"), 16)
                pool.wait_ge(sem("table_stored"), 16 * (k + 1))
                take(first, table[k], dst0[:, 0:1]).then_inc(sem("first"), 16)

            pool.wait_ge(sem("start_idx_ready"), 1)
            pool.wait_ge(sem("filled"), 16 * (1 + F + len(width)))
            pool.wait_ge(sem("end_table_stored"), 16)
            pool.wait_ge(sem("dst0_ready"), 1)
            take(fix_end[:, :], end_table, dst0[:, 0:1]).then_inc(sem("fix_end_fetched"), 16)
            spread_nodes(0, lambda t: h[:, t, :], spread, carry_in[:, :], F)
            gather(0, F, ZW, "input_used0")
            pool.wait_ge(sem("fix_idx_ready"), 1)
            fix_and_fetch(0)
            spread_nodes(1, lambda t: att3[:, t, F + 1:F + 2], spread1, fix[:, 0:AW], 1)
            gather(1, AW, AW, "score_copied")
            fix_and_fetch(1)
            spread_nodes(2, lambda t: h[:, t, :], spread, carry_in[:, :], F)
            pool.wait_ge(sem("vec_read"), 1)
            gather(2, F, ZE, "input_used2")
            fix_and_fetch(2)
            for k in (3, 4):
                gather(k, F, F, f"scanned{k}")
                fix_and_fetch(k)

        @block.scalar
        def _(act):
            def copy(dst, src):
                return act.activation(dst, src, ACT.Copy)

            def root(k):
                act.wait_ge(sem("recip"), k + 1)
                act.activation(n3[:, :], n2[:, :], ACT.Sqrt).then_inc(sem("rstd"), 1)

            act.wait_ge(sem("deg_recip"), 1)
            act.activation(dinv[:, :], dinv[:, :], ACT.Sqrt).then_inc(sem("dinv_ready"), 1)
            root(0)
            act.wait_ge(sem("consts_loaded"), 16 * len(consts))

            def body0(i, b, c):
                for s in range(NG + 2):
                    n = c * NG + s
                    if s < NG:
                        act.wait_ge(sem("transposed0"), n + 1)
                        after(act, sem("hidden0"), n - 1)
                        copy(tz[:, s % 2, :], bank[s % 2][0:ZW, :]).then_inc(sem("transposed_copied0"), 1)
                    if 1 <= s <= NG:
                        m, g = n - 1, s - 1
                        act.wait_ge(sem("hidden0"), m + 1)
                        after(act, sem("out0"), m - 1)
                        act.activation(hid[0:64, g % 2, :], bank[2 + g % 2][0:64, :], ACT.Relu,
                                       bias=b01[:, 0:1]).then_inc(sem("relu0"), 1)
                    if s >= 2:
                        m, g = n - 2, s - 2
                        act.wait_ge(sem("out0"), m + 1)
                        if g == 0:
                            after(act, sem("scanned"), c - 1)
                            if not isinstance(i, int):
                                act.wait_ge(sem(f"stored{b}"), 16 * (HALF * 0 + i))
                        copy(orow(b, F)[:, g * G:(g + 1) * G, :],
                             bank[4 + g % 2][:, 0:G * F].rearrange("p (j w) -> p j w", w=F)
                             ).then_inc(sem("out_copied0"), 1)
            chunks(act, body0)

            root(1)

            def body1(i, b, c):
                hold(act, sem(f"gathered1_{b}"), 16 * JC * (i + 1))
                copy(ea[:, 0, cols(c)], zrow(b, AW)[:, :, F]).then_inc(sem("score_copied"), 1)
            chunks(act, body1)
            act.wait_ge(sem("logits"), 1)
            act.activation(ea[:, 0], ea[:, 1], ACT.Exp).then_inc(sem("weights_ready"), 1)

            act.wait_ge(sem("norm2_ready"), 1)
            act.activation(ea[:, 5], ea[:, 4], ACT.Sqrt).then_inc(sem("rnorm_ready"), 1)
            root(2)

            def body2(i, b, c):
                for s in range(NG + 3):
                    n = c * NG + s
                    if 1 <= s <= NG:
                        m, g = n - 1, s - 1
                        act.wait_ge(sem("hidden2"), m + 1)
                        after(act, sem("product2"), 7 * (m - 1))
                        act.activation(hid[:, g % 2, :], bank[1][:, :], ACT.Relu).then_inc(sem("relu2"), 1)
                        act.wait_ge(sem("dw2"), m + 1)
                        copy(dw[:, g % 2, :], bank[1][:, :]).then_inc(sem("dw_copied2"), 1)
                    if s < NG:
                        act.wait_ge(sem("transposed2"), n + 1)
                        after(act, sem("block2"), 7 * (n - 1))
                        copy(tz[0:ZE, s % 2, :], bank[0][0:ZE, :]).then_inc(sem("transposed_copied2"), 1)
                    if s >= 3:
                        m, g = n - 3, s - 3
                        act.wait_ge(sem("out2"), m + 1)
                        if g == 0:
                            after(act, sem("combined2"), c - 1)
                        o = bank[6 + g % 2][:, 0:G * 48].rearrange("p (j w) -> p j w", w=48)
                        e = eo[b][:, g * G:(g + 1) * G]
                        act.activation(e[:, :, 0:16], o[:, :, 0:16], ACT.Tanh)
                        copy(e[:, :, 16:48], o[:, :, 16:48]).then_inc(sem("out_copied2"), 1)
            chunks(act, body2)

            root(3)

            for g in range(NT // G):
                act.wait_ge(sem("transposed3"), g + 1)
                after(act, sem("hidden3"), g - 1)
                copy(tz[0:F, g % 2, :], bank[g % 2][0:F, :]).then_inc(sem("transposed_copied3"), 1)
                act.wait_ge(sem("hidden3"), g + 1)
                after(act, sem("out3"), g - 1)
                act.activation(hid[0:64, g % 2, :], bank[2 + g % 2][0:64, :], ACT.Relu,
                               bias=b31[:, 0:1]).then_inc(sem("relu3"), 1)

        @block.tensor
        def _(pe):
            pe.wait_ge(sem("consts_loaded"), 16 * len(consts))

            def hist(i, b):
                hh = 2 * i + b
                pe.wait_ge(sem("hot"), hh + 1)
                for k in range(HC):
                    first = isinstance(i, int) and b == 0 and k == 0
                    ins = pe.matmul(bank[7][:, 0:NT], hot[:, b * HC + k, 0:P], hot[:, b * HC + k, P:P + NT],
                                    start=first, stop=False, skip_group_check=True)
                ins.then_inc(sem("hot_used"), 1)
            for b in range(2):
                hist(0, b)
            with pe.Fori(1, J // (2 * HC)) as i:
                for b in range(2):
                    hist(i, b)
            pe.wait_ge(sem("deg_scanned"), 1)
            pe.matmul(bank[6][:, 0:1], before[:, :], n1[:, NT - 1:NT], start=True, stop=True
                      ).then_inc(sem("base_ready"), 1)
            for m, (src, w) in enumerate(((kcols[:, 0:RW], RW), (fix[:, 0:RW], RW), (c3[:, :], 1))):
                pe.wait_ge(sem("marks_ready"), m + 1)
                pe.transpose(bank[m][0:w, 0:P], src, ident[:, :]).then_inc(sem("marks_turned"), 1)

            def turn_carry(k):
                w = width[k]
                pe.wait_ge(sem("scanned"), NCH * (k + 1))
                pe.transpose(bank[6][0:w, 0:P], carry[:, 0:w], ident[:, :]).then_inc(sem("carry_turned"), 1)
                pe.wait_ge(sem("carry_scanned"), k + 1)
                pe.transpose(bank[7][:, 0:w], rowc[0:w, :], ident[0:w, 0:w]).then_inc(sem("carry_turned"), 1)

            def body0(i, b, c):
                for s in range(NG + 2):
                    n = c * NG + s
                    if s < NG:
                        if s == 0:
                            pe.wait_ge(sem(f"gathered0_{b}"), 16 * JC * (i + 1))
                            pe.wait_ge(sem(f"loaded0_{b}"), 32 * (i + 1))
                            pe.wait_ge(sem("spread_done0"), c + 1)
                        after(pe, sem("transposed_copied0"), n - 1)
                        for j in range(G):
                            ins = pe.transpose(bank[s % 2][0:ZW, j * P:(j + 1) * P],
                                               zrow(b, ZW)[:, s * G + j, :], ident[:, :])
                        ins.then_inc(sem("transposed0"), 1)
                    if 1 <= s <= NG:
                        m, g = n - 1, s - 1
                        pe.wait_ge(sem("transposed_copied0"), m + 1)
                        after(pe, sem("relu0"), m - 1)
                        pe.matmul(bank[2 + g % 2][0:64, :], w01[:, :], tz[:, g % 2, :],
                                  start=True, stop=True).then_inc(sem("hidden0"), 1)
                    if s >= 2:
                        m, g = n - 2, s - 2
                        pe.wait_ge(sem("relu0"), m + 1)
                        after(pe, sem("out_copied0"), m - 1)
                        for j in range(G):
                            ins = pe.matmul(bank[4 + g % 2][:, j * F:(j + 1) * F],
                                            hid[0:64, g % 2, j * P:(j + 1) * P], w02[:, :],
                                            start=True, stop=True)
                        ins.then_inc(sem("out0"), 1)
            chunks(pe, body0)
            turn_carry(0)
            for m in range(2):
                pe.wait_ge(sem("max_end"), m + 1)
                pe.transpose(bank[0][0:1, 0:P], c1[:, :], ident[:, :]).then_inc(sem("max_turned"), 1)
                pe.wait_ge(sem("max_scanned"), m + 1)
                pe.transpose(bank[1][:, 0:1], rowc[0:1, :], ident[0:1, 0:1]).then_inc(sem("max_turned"), 1)
            turn_carry(1)

            def body2(i, b, c):
                for s in range(NG + 3):
                    n = c * NG + s
                    if s < NG:
                        if s == 0:
                            pe.wait_ge(sem(f"gathered2_{b}"), 16 * JC * (i + 1))
                            pe.wait_ge(sem(f"loaded2_{b}"), 32 * (i + 1))
                            pe.wait_ge(sem("ready2"), c + 1)
                        after(pe, sem("transposed_copied2"), n)
                        for j in range(G):
                            ins = pe.transpose(bank[0][0:ZE, j * P:(j + 1) * P],
                                               zrow(b, ZE)[:, s * G + j, :], ident[:, :])
                        ins.then_inc(sem("transposed2"), 1)
                    if 2 <= s < NG + 2:
                        m, g = n - 2, s - 2
                        for a in range(7):
                            if a == 4 and s <= NG:
                                pe_dw(n - 1, s - 1)
                            after(pe, sem("product2"), 7 * m + a - 3)
                            pe.matmul(bank[block_bank(b, g, a)][:, :], sel[:, a, :],
                                      tz[0:ZE, g % 2, :], start=True, stop=True).then_inc(sem("block2"), 1)
                            if a == 0 and s <= NG:
                                pe_hidden(n - 1, s - 1)
                    elif s == 1:
                        pe_hidden(n - 1, s - 1)
                        pe_dw(n - 1, s - 1)
                    if s >= 3:
                        m, g = n - 3, s - 3
                        pe.wait_ge(sem("product2"), 7 * m + 7)
                        after(pe, sem("out_copied2"), m - 1)
                        for j in range(G):
                            e = slice(j * P, (j + 1) * P)
                            for a in range(4):
                                pe.matmul(bank[6 + g % 2][:, j * 48:j * 48 + 24], prod[:, g % 2, a, e],
                                          wa[:, a, :], start=(a == 0), stop=(a == 3))
                            for q in range(3):
                                ins = pe.matmul(bank[6 + g % 2][:, j * 48 + 24 + 8 * q:j * 48 + 32 + 8 * q],
                                                prod[:, g % 2, 4 + q, e], sumw[:, :], start=True, stop=True)
                        ins.then_inc(sem("out2"), 1)

            def pe_hidden(m, g):
                pe.wait_ge(sem("transposed_copied2"), m + 1)
                after(pe, sem("dw_copied2"), m)
                pe.matmul(bank[1][:, :], w1rep[:, :], tz[0:ZE, g % 2, :], start=True, stop=True
                          ).then_inc(sem("hidden2"), 1)

            def pe_dw(m, g):
                pe.wait_ge(sem("relu2"), m + 1)
                pe.matmul(bank[1][:, :], wd[:, :], hid[0:16, g % 2, :], start=True, stop=True
                          ).then_inc(sem("dw2"), 1)
            pe.wait_ge(sem("weights2_ready"), 1)
            chunks(pe, body2)
            turn_carry(2)
            turn_carry(3)

            for g in range(NT // G):
                pe.wait_ge(sem("update3"), 1)
                after(pe, sem("transposed_copied3"), g - 1)
                for j in range(G):
                    ins = pe.transpose(bank[g % 2][0:F, j * P:(j + 1) * P], scratch[:, g * G + j, :], ident[:, :])
                ins.then_inc(sem("transposed3"), 1)
                pe.wait_ge(sem("transposed_copied3"), g + 1)
                after(pe, sem("relu3"), g - 1)
                pe.matmul(bank[2 + g % 2][0:64, :], w31[:, :], tz[0:F, g % 2, :], start=True, stop=True
                          ).then_inc(sem("hidden3"), 1)
                pe.wait_ge(sem("relu3"), g + 1)
                after(pe, sem("out_copied3"), g - 1)
                for j in range(G):
                    ins = pe.matmul(bank[4 + g % 2][:, j * F:(j + 1) * F], hid[0:64, g % 2, j * P:(j + 1) * P],
                                    w32[:, :], start=True, stop=True)
                ins.then_inc(sem("out3"), 1)
            turn_carry(4)

        @block.vector
        def _(dve):
            order = [0]

            def link(ins):
                order[0] += 1
                ins.then_inc(sem("dve_order"), 1)
                dve.wait_ge(sem("dve_order"), order[0])

            def mark(ins, name, value=1):
                ins.then_inc(sem(name), 1)
                dve.wait_ge(sem(name), value)

            def over(t, w=F):
                return t.unsqueeze(2).broadcast_to([P, t.shape[1], w])

            def along(t, n=NT):
                return t.unsqueeze(1).broadcast_to([P, n, t.shape[1]])

            tt, ts, stt = dve.tensor_tensor, dve.tensor_scalar, dve.scalar_tensor_tensor
            scan = dve.tensor_tensor_scan

            mark(dve.memset(x[:, :, :], 0.0), "x_cleared")
            mark(dve.memset(zero[:, :], 0.0), "zero_ready")

            dve.wait_ge(sem("dst_loaded"), 48)
            mark(dve.tensor_copy(dst0[:, :], dst_i[:, 0:1]), "dst0_ready")
            link(tt(keep[:, :], dst_i, prev_i, ALU.is_equal))
            link(tt(ea[:, 4], dst_i, next_i, ALU.is_equal))
            link(ts(pen[:, :], keep[:, :], -1.0, BIG, ALU.add, ALU.mult))
            link(ts(ea[:, 5], ea[:, 4], -1.0, BIG, ALU.add, ALU.mult))
            link(dve.tensor_copy(ea[:, 0], dst_i))
            link(ts(prev_i, ea[:, 0], 1.0 / NT, None, ALU.mult))
            link(dve.tensor_copy(ea[:, 1], prev_i))
            link(stt(ea[:, 2], ea[:, 1], -float(NT), ea[:, 0], ALU.mult, ALU.add))
            link(ts(ea[:, 3], ea[:, 2], 0.0, None, ALU.is_lt))
            link(tt(ea[:, 1], ea[:, 1], ea[:, 3], ALU.subtract))
            link(stt(ea[:, 2], ea[:, 3], float(NT), ea[:, 2], ALU.mult, ALU.add))
            link(ts(ea[:, 3], ea[:, 2], float(NT), None, ALU.is_ge))
            link(tt(ea[:, 1], ea[:, 1], ea[:, 3], ALU.add))
            link(stt(ea[:, 2], ea[:, 3], -float(NT), ea[:, 2], ALU.mult, ALU.add))
            link(dve.tensor_reduce(c2[:, :], keep[:, :], AX.X, ALU.min))
            link(dve.tensor_reduce(c3[:, :], ea[:, 4], AX.X, ALU.min))
            mark(ts(kcols[:, :], zero[:, 0:RW], c2[:, 0:1], None, ALU.add), "marks_ready", 1)
            mark(ts(fix[:, 0:RW], kcols[:, :], -1.0, BIG, ALU.add, ALU.mult), "marks_ready", 2)
            mark(ts(c3[:, :], c3[:, :], -1.0, BIG, ALU.add, ALU.mult), "marks_ready", 3)

            dve.wait_ge(sem("consts_loaded"), 16 * len(consts))
            link(dve.tensor_copy(iota_b[:, :], iota_f[:, :]))

            def hist(i, b):
                hh = 2 * i + b
                after(dve, sem("hot_used"), hh - 1)
                for k in range(HC):
                    col = (hh * HC + k)
                    at = slice(col, col + 1) if isinstance(col, int) else bass.ds(col, 1)
                    ts(hot[:, b * HC + k, 0:P], iota_b[:, :], ea[:, 1, at], None, ALU.is_equal)
                    ins = ts(hot[:, b * HC + k, P:P + NT], iota_b[:, 0:NT], ea[:, 2, at], None, ALU.is_equal)
                ins.then_inc(sem("hot"), 1)
            for b in range(2):
                hist(0, b)
            with dve.Fori(1, J // (2 * HC)) as i:
                for b in range(2):
                    hist(i, b)

            dve.wait_ge(sem("hot_used"), J // HC)
            link(dve.tensor_copy(n2[:, :], bank[7][:, 0:NT]))
            link(ts(has[:, :], n2[:, :], 0.0, None, ALU.is_gt))
            link(ts(nohas[:, :], has[:, :], -1.0, BIG, ALU.add, ALU.mult))
            link(ts(n3[:, :], n2[:, :], 1.0, None, ALU.add))
            mark(dve.reciprocal(dinv[:, :], n3[:, :]), "deg_recip")
            link(ts(n3[:, :], n2[:, :], 0.0, 1.0, ALU.mult, ALU.add))
            mark(scan(n1[:, :], n3[:, :], n2[:, :], 0.0, ALU.mult, ALU.add), "deg_scanned")
            dve.wait_ge(sem("base_ready"), 1)
            link(dve.tensor_copy(c1[:, :], bank[6][:, 0:1]))
            link(ts(n1[:, :], n1[:, :], c1[:, 0:1], None, ALU.add))
            mark(ts(end_idx[:, :], n1[:, :], -1.0, 0.0, ALU.add, ALU.max), "end_idx_ready")
            link(tt(n1[:, :], n1[:, :], n2[:, :], ALU.subtract))
            link(tt(n1[:, :], n1[:, :], dump_n[:, :], ALU.subtract))
            link(tt(n1[:, :], n1[:, :], has[:, :], ALU.mult))
            mark(tt(start_idx[:, :], n1[:, :], dump_n[:, :], ALU.add), "start_idx_ready")
            dve.wait_ge(sem("marks_turned"), 3)
            link(dve.tensor_copy(krow[:, :], bank[0][0:RW, 0:P]))
            link(dve.tensor_copy(penkrow[:, :], bank[1][0:RW, 0:P]))
            link(dve.tensor_copy(bkrow[:, :], bank[2][0:1, 0:P]))

            link(ts(wa[:, :, 0:16], wa[:, :, 0:16], ALPHA * PW_S, None, ALU.mult))
            link(ts(wa[:, 0:2, 16:24], wa[:, 0:2, 16:24], ALPHA * PW_V, None, ALU.mult))
            link(ts(wa[:, 2:4, 16:24], wa[:, 2:4, 16:24], ALPHA * PW_V * 1.5 ** 0.5, None, ALU.mult))
            link(ts(we[:, :], we[:, :], -ALPHA * PW_V * 1.5 ** 0.5 / 3.0, None, ALU.mult))
            mark(stt(wd[:, :], wd[:, :], ALPHA * PW_V / 3.0 ** 0.5, we[:, :], ALU.mult, ALU.add),
                 "weights2_ready")

            def fix_index():
                dve.wait_ge(sem("fix_end_fetched"), 16)
                link(dve.tensor_copy(c1[:, :], fix_end[:, :]))
                link(ts(c2[:, :], c1[:, :], plimit[:, 0:1], None, ALU.is_lt))
                link(tt(c2[:, :], c2[:, :], keep[:, 0:1], ALU.mult))
                link(tt(c1[:, :], c1[:, :], dump[:, :], ALU.subtract))
                link(tt(c1[:, :], c1[:, :], c2[:, :], ALU.mult))
                mark(tt(fix_idx[:, :], c1[:, :], dump[:, :], ALU.add), "fix_idx_ready")

            def norm_relu(k):
                link(dve.tensor_reduce(n1[:, :], x[:, :, :], AX.X, ALU.add))
                link(ts(n1[:, :], n1[:, :], -1.0 / F, None, ALU.mult))
                link(tt(h[:, :, :], x[:, :, :], over(n1[:, :]), ALU.add))
                link(tt(scratch, h[:, :, :], h[:, :, :], ALU.mult))
                link(dve.tensor_reduce(n1[:, :], scratch, AX.X, ALU.add))
                link(ts(n1[:, :], n1[:, :], 1.0 / F, EPS, ALU.mult, ALU.add))
                mark(dve.reciprocal(n2[:, :], n1[:, :]), "recip", k + 1)
                dve.wait_ge(sem("rstd"), k + 1)
                link(tt(h[:, :, :], h[:, :, :], over(n3[:, :]), ALU.mult))

            def carry_over(k, row, op0, op1, none):
                w = width[k]
                dve.wait_ge(sem("carry_turned"), 2 * k + 1)
                link(dve.tensor_copy(rowa[0:w, :], bank[6][0:w, 0:P]))
                link(scan(rowb[0:w, :], row[0:w, :], rowa[0:w, :], none, op0, op1))
                link(dve.memset(rowc[0:w, 0:1], none))
                mark(dve.tensor_copy(rowc[0:w, 1:P], rowb[0:w, 0:P - 1]), "carry_scanned", k + 1)
                dve.wait_ge(sem("carry_turned"), 2 * k + 2)
                dve.wait_ge(sem("fix_fetched"), 16 * (k + 1))
                mark(tt(fix[:, 0:w], fix[:, 0:w], bank[7][:, 0:w], op1), "fix_ready", k + 1)
                dve.wait_ge(sem("fetched"), 16 * NT * (k + 1))

            def segment_scan(k, w, b, c, marks, op0, op1, src):
                o = orow(b, w)
                for f in range(w):
                    ins = scan(o[:, :, f], marks[:, cols(c)], src[:, :, f], carry[:, f:f + 1], op0, op1)
                ins.then_inc(sem("scan_steps"), 1)
                dve.wait_ge(sem("scan_steps"), NCH * k + c + 1)
                dve.tensor_copy(carry[:, 0:w], o[:, JC - 1, :]).then_inc(sem("scanned"), 1)
                dve.wait_ge(sem("scanned"), NCH * k + c + 1)

            def spread_rows(k, i, b, c, z):
                if isinstance(i, int) and b == 0:
                    dve.wait_ge(sem("first"), 16 * (k + 1))
                dve.wait_ge(sem(f"loaded{k}_{b}"), 32 * (i + 1))
                for f in range(F):
                    ins = scan(z[:, :, F + f], keep[:, cols(c)], z[:, :, F + f], carry_in[:, f:f + 1],
                               ALU.mult, ALU.add)
                ins.then_inc(sem(f"spread_steps{k}"), 1)
                dve.wait_ge(sem(f"spread_steps{k}"), c + 1)
                dve.tensor_copy(carry_in[:, :], z[:, JC - 1, F:2 * F]).then_inc(sem(f"spread_done{k}"), 1)
                dve.wait_ge(sem(f"spread_done{k}"), c + 1)

            def before_chunk(i, b, c, body):
                if b == 1:
                    body(i, 0, c - 1)
                elif not isinstance(i, int):
                    body(i - 1, 1, c - 1)

            dve.wait_ge(sem("x_loaded"), 16)
            norm_relu(0)
            mark(ts(h[:, :, :], h[:, :, :], 0.0, None, ALU.max), "table_ready", 1)
            fix_index()
            link(dve.memset(carry[:, :], -BIG))

            def max0(i, b, c):
                dve.wait_ge(sem("out_copied0"), NG * (c + 1))
                segment_scan(0, F, b, c, pen, ALU.add, ALU.max, orow(b, F))

            def body0(i, b, c):
                spread_rows(0, i, b, c, zrow(b, ZW))
                before_chunk(i, b, c, max0)
            chunks(dve, body0)
            max0(HALF - 1, 1, NCH - 1)
            carry_over(0, penkrow, ALU.add, ALU.max, -BIG)
            f0 = fetch[0]
            link(tt(f0, f0, along(b02[:, :]), ALU.add))
            link(tt(f0, f0, over(nohas[:, :]), ALU.add))
            link(tt(f0, f0, h[:, :, :], ALU.max))
            link(tt(x[:, :, :], x[:, :, :], f0, ALU.add))

            norm_relu(1)
            link(ts(h[:, :, :], h[:, :, :], 0.0, None, ALU.max))
            link(dve.tensor_copy(att3[:, :, 0:F], h[:, :, :]))
            temp = zin[:, :, :].rearrange("p b w -> p (b w)")[:, 0:NT * F].rearrange("p (t f) -> p t f", f=F)
            link(tt(temp, h[:, :, :], along(aw[:, 0:F]), ALU.mult))
            link(dve.tensor_reduce(att3[:, :, F], temp, AX.X, ALU.add))
            link(tt(temp, h[:, :, :], along(aw[:, F:2 * F]), ALU.mult))
            mark(dve.tensor_reduce(att3[:, :, F + 1], temp, AX.X, ALU.add), "table_ready", 2)
            dve.wait_ge(sem("score_copied"), NCH)
            dve.wait_ge(sem("spread1_loaded"), 16)
            dve.wait_ge(sem("first"), 32)
            link(scan(ea[:, 2], keep[:, :], ea[:, 1], fix[:, F + 1:F + 2], ALU.mult, ALU.add))
            link(tt(ea[:, 1], ea[:, 0], ea[:, 2], ALU.add))
            link(stt(ea[:, 0], ea[:, 1], LEAKY, ea[:, 1], ALU.mult, ALU.max))

            def running_max(out_, marks, row, turn, flip):
                r = (lambda a: a[:, ::-1]) if flip else (lambda a: a)
                last, dst, srcs, end = ((ea[:, out_, 0:1], slice(0, P - 1), slice(1, P), P - 1) if flip else
                                        (ea[:, out_, J - 1:J], slice(1, P), slice(0, P - 1), 0))
                link(scan(r(ea[:, out_]), r(marks), r(ea[:, 0]), -BIG, ALU.add, ALU.max))
                mark(dve.tensor_copy(c1[:, :], last), "max_end", turn + 1)
                dve.wait_ge(sem("max_turned"), 2 * turn + 1)
                link(dve.tensor_copy(rowa[0:1, :], bank[0][0:1, 0:P]))
                link(scan(r(rowb[0:1, :]), r(row), r(rowa[0:1, :]), -BIG, ALU.add, ALU.max))
                link(dve.memset(rowc[0:1, end:end + 1], -BIG))
                mark(dve.tensor_copy(rowc[0:1, dst], rowb[0:1, srcs]), "max_scanned", turn + 1)
                dve.wait_ge(sem("max_turned"), 2 * turn + 2)
                link(dve.tensor_copy(c2[:, :], bank[1][:, 0:1]))
                link(scan(r(ea[:, out_]), r(marks), r(ea[:, 0]), c2[:, 0:1], ALU.add, ALU.max))
            running_max(2, pen[:, :], penkrow[0:1, :], 0, False)
            running_max(3, ea[:, 5], bkrow[0:1, :], 1, True)
            link(tt(ea[:, 2], ea[:, 2], ea[:, 3], ALU.max))
            mark(tt(ea[:, 1], ea[:, 0], ea[:, 2], ALU.subtract), "logits")
            link(dve.memset(carry[:, :], 0.0))
            dve.wait_ge(sem("weights_ready"), 1)

            def body1(i, b, c):
                z, o = zrow(b, AW), orow(b, RW)
                dve.wait_ge(sem(f"loaded1_{b}"), 16 * (i + 1))
                if not isinstance(i, int):
                    dve.wait_ge(sem(f"stored{b}"), 16 * (HALF * 1 + i))
                tt(o[:, :, 0:F], z[:, :, 0:F], ea[:, 0, cols(c)].unsqueeze(2).broadcast_to([P, JC, F]), ALU.mult)
                ts(o[:, :, F], ea[:, 0, cols(c)], 1.0, None, ALU.mult).then_inc(sem("weighted"), 1)
                dve.wait_ge(sem("weighted"), c + 1)
                segment_scan(1, RW, b, c, keep, ALU.mult, ALU.add, o)
            chunks(dve, body1)
            carry_over(1, krow, ALU.mult, ALU.add, 0.0)
            f1 = fetch[1]
            link(ts(n2[:, :], has[:, :], -1.0, 1.0, ALU.mult, ALU.add))
            link(tt(n1[:, :], f1[:, :, F], has[:, :], ALU.mult))
            link(tt(n1[:, :], n1[:, :], n2[:, :], ALU.add))
            link(dve.reciprocal(n3[:, :], n1[:, :]))
            link(tt(n3[:, :], n3[:, :], has[:, :], ALU.mult))
            link(tt(f1[:, :, 0:F], f1[:, :, 0:F], over(n3[:, :]), ALU.mult))
            link(tt(x[:, :, :], x[:, :, :], f1[:, :, 0:F], ALU.add))

            vec = zin[:, :, :].rearrange("p b w -> p (b w)")[:, 0:3 * J].rearrange("p (j k) -> p j k", k=3)
            dve.wait_ge(sem("vec_loaded"), 32)
            link(tt(ea[:, 0], vec[:, :, 0], vec[:, :, 0], ALU.mult))
            link(tt(ea[:, 1], vec[:, :, 1], vec[:, :, 1], ALU.mult))
            link(tt(ea[:, 0], ea[:, 0], ea[:, 1], ALU.add))
            link(tt(ea[:, 1], vec[:, :, 2], vec[:, :, 2], ALU.mult))
            link(tt(ea[:, 0], ea[:, 0], ea[:, 1], ALU.add))
            mark(dve.reciprocal(ea[:, 4], ea[:, 0]), "norm2_ready")
            link(ts(ea[:, 3], ea[:, 3], TANH_GAIN, None, ALU.mult))
            dve.wait_ge(sem("rnorm_ready"), 1)
            link(tt(ea[:, 0], vec[:, :, 0], ea[:, 5], ALU.mult))
            link(tt(ea[:, 1], vec[:, :, 1], ea[:, 5], ALU.mult))
            mark(tt(ea[:, 2], vec[:, :, 2], ea[:, 5], ALU.mult), "vec_read")
            norm_relu(2)
            mark(ts(h[:, :, :], h[:, :, :], 0.0, None, ALU.max), "table_ready", 3)
            link(dve.memset(carry[:, :], 0.0))

            def unit(k, c, n):
                return ea[:, k, cols(c)].unsqueeze(2).broadcast_to([P, JC, n])

            def combine2(i, b, c):
                e, o = eo[b], orow(b, F)
                v = qtemp[:, 0:JC * 24].rearrange("p (j w) -> p j w", w=24)
                dve.wait_ge(sem("out_copied2"), NG * (c + 1))
                if not isinstance(i, int) :
                    dve.wait_ge(sem(f"stored{b}"), 16 * (HALF * 2 + i))
                tt(e[:, :, 0:16], e[:, :, 0:16], unit(3, c, 16), ALU.mult)
                for k in range(3):
                    ins = tt(v[:, :, 8 * k:8 * k + 8], e[:, :, 16:24], unit(k, c, 8), ALU.mult)
                ins.then_inc(sem("combine_steps2"), 1)
                dve.wait_ge(sem("combine_steps2"), 2 * c + 1)
                tt(v, v, e[:, :, 24:48], ALU.add).then_inc(sem("combine_steps2"), 1)
                dve.wait_ge(sem("combine_steps2"), 2 * c + 2)
                for k in range(3):
                    tt(o[:, :, 8 + k:F:3], v[:, :, 8 * k:8 * k + 8], e[:, :, 8:16], ALU.mult)
                ts(o[:, :, 0:8], e[:, :, 0:8], 1.0, None, ALU.mult).then_inc(sem("combined2"), 1)
                dve.wait_ge(sem("combined2"), c + 1)
                segment_scan(2, F, b, c, keep, ALU.mult, ALU.add, o)

            def body2(i, b, c):
                z = zrow(b, ZE)
                q = [qtemp[:, m * JC * 16:(m + 1) * JC * 16].rearrange("p (j w) -> p j w", w=16) for m in range(2)]
                spread_rows(2, i, b, c, z)
                dve.wait_ge(sem(f"gathered2_{b}"), 16 * JC * (i + 1))
                for half in range(2):
                    for k in range(3):
                        dst = z[:, :, 64:80] if k == 0 else q[k - 1]
                        ins = tt(dst[:, :, 8 * half:8 * half + 8], z[:, :, F * half + 8 + k:F * half + F:3],
                                 unit(k, c, 8), ALU.mult)
                ins.then_inc(sem("q_steps2"), 1)
                dve.wait_ge(sem("q_steps2"), 2 * c + 1)
                tt(z[:, :, 64:80], z[:, :, 64:80], q[0], ALU.add).then_inc(sem("q_steps2"), 1)
                dve.wait_ge(sem("q_steps2"), 2 * c + 2)
                tt(z[:, :, 64:80], z[:, :, 64:80], q[1], ALU.add).then_inc(sem("ready2"), 1)
                dve.wait_ge(sem("ready2"), c + 1)
                before_chunk(i, b, c, combine2)
                for g in range(NG):
                    n = c * NG + g
                    for a in range(7):
                        if a == 0:
                            dve.wait_ge(sem("relu2"), n + 1)
                            after(dve, sem("out2"), n - 1)
                        if a == 4:
                            dve.wait_ge(sem("dw_copied2"), n + 1)
                        dve.wait_ge(sem("block2"), 7 * n + a + 1)
                        tt(prod[:, g % 2, a, :], bank[block_bank(b, g, a)][:, :],
                           (hid if a < 4 else dw)[:, g % 2, :], ALU.mult).then_inc(sem("product2"), 1)
            chunks(dve, body2)
            combine2(HALF - 1, 1, NCH - 1)
            carry_over(2, krow, ALU.mult, ALU.add, 0.0)
            link(tt(fetch[2], fetch[2], over(has[:, :]), ALU.mult))
            link(tt(x[:, :, :], x[:, :, :], fetch[2], ALU.add))

            norm_relu(3)
            link(ts(h[:, :, :], h[:, :, :], 0.0, None, ALU.max))
            dve.wait_ge(sem("dinv_ready"), 1)
            mark(tt(h[:, :, :], h[:, :, :], over(dinv[:, :]), ALU.mult), "table_ready", 4)

            def convolve(k):
                link(dve.memset(carry[:, :], 0.0))

                def body(i, b, c):
                    dve.wait_ge(sem(f"gathered{k}_{b}"), 16 * JC * (i + 1))
                    if not isinstance(i, int):
                        dve.wait_ge(sem(f"stored{b}"), 16 * (HALF * k + i))
                    segment_scan(k, F, b, c, keep, ALU.mult, ALU.add, zrow(b, F))
                chunks(dve, body)
                carry_over(k, krow, ALU.mult, ALU.add, 0.0)
                link(tt(fetch[k], fetch[k], over(has[:, :]), ALU.mult))
                link(tt(fetch[k], fetch[k], h[:, :, :], ALU.add))
            convolve(3)
            mark(tt(scratch, fetch[3], over(dinv[:, :]), ALU.mult), "update3")
            for g in range(NT // G):
                dve.wait_ge(sem("out3"), g + 1)
                tt(h[:, g * G:(g + 1) * G, :], bank[4 + g % 2][:, 0:G * F].rearrange("p (j w) -> p j w", w=F),
                   over(dinv[:, g * G:(g + 1) * G]), ALU.mult).then_inc(sem("out_copied3"), 1)
            dve.wait_ge(sem("out_copied3"), NT // G)
            convolve(4)
            f4 = fetch[4]
            link(tt(f4, f4, over(dinv[:, :]), ALU.mult))
            link(tt(f4, f4, along(b32[:, :]), ALU.add))
            link(ts(f4, f4, 0.0, None, ALU.max))
            mark(tt(x[:, :, :], x[:, :, :], f4, ALU.add), "x_final")


def kernel(**inputs):
    import concourse.bacc as bacc
    from concourse.bass_utils import run_bass_kernel_spmd

    a = {k: np.asarray(v) for k, v in inputs.items()}
    pad = EP - E

    def padded(v, value):
        return np.concatenate([v, np.full((pad,) + v.shape[1:], value, v.dtype)])

    arrays = {
        "x": a["x"],
        "src": padded(a["src"].astype(np.int32), 0).reshape(P, J),
        "dst": np.concatenate([np.full(1, -1, np.int32), padded(a["dst"].astype(np.int32), N),
                               np.full(1, -2, np.int32)]),
        "a32": padded(a["edge_attr_32"], 0.0),
        "a10": padded(a["edge_attr_10"], 0.0),
        "a3": padded(a["edge_attr_3"], 1.0),
        "wgt": padded(a["edge_weight"], 0.0),
        "w01": a["L0_gnn_W1"], "w02": a["L0_gnn_W2"], "b01": a["L0_gnn_b1"].reshape(64, 1),
        "b02": np.tile(a["L0_gnn_b2"].reshape(1, F), (P, 1)),
        "aw": np.tile(a["L1_gnn_attn_w"].reshape(1, 2 * F), (P, 1)),
        "w31": a["L3_gnn_W1"], "w32": a["L3_gnn_W2"], "b31": a["L3_gnn_b1"].reshape(64, 1),
        "b32": np.tile(a["L3_gnn_b2"].reshape(1, F), (P, 1)),
    }
    w1rep = np.zeros((ZE, P), np.float32)
    w1rep[80:90] = np.tile(a["L2_gnn_W1"], (1, 8))
    arrays["w1rep"] = w1rep
    w2 = a["L2_gnn_W2"].reshape(16, 7, 16, 8)
    rows_of = lambda path, half: w2[:, path, 8 * half:8 * half + 8].transpose(1, 0, 2).reshape(P, 8)
    arrays["wa"] = np.stack([np.concatenate([rows_of(path, half) for path in paths], axis=1)
                             for paths in ((0, 2, 4), (1, 3, 6)) for half in range(2)], axis=1)
    arrays["wd"] = w2[:, 5].reshape(16, P)
    arrays["we"] = w2[:, 6].reshape(16, P)
    sel = np.zeros((ZE, 7, P), np.float32)
    for m in range(P):
        u, w = m // 16, m // 8
        for blk, col in enumerate((u, F + u, 64 + u, 72 + u)):
            sel[col, blk, m] = 1.0
        for k in range(3):
            sel[(8 + 3 * w + k) if w < 8 else (F + 8 + 3 * (w - 8) + k), 4 + k, m] = 1.0
    arrays["sel"] = sel
    r = np.arange(P)
    arrays["sumw"] = (r[:, None] % 8 == np.arange(8)[None]).astype(np.float32)
    arrays["ident"] = np.eye(P, dtype=np.float32)
    arrays["before"] = (r[:, None] < r[None]).astype(np.float32)
    arrays["dump"] = (EP + r).astype(np.float32)[:, None]
    arrays["dump_n"] = (EP + np.arange(NPAD)).astype(np.float32).reshape(P, NT)
    arrays["plimit"] = ((r + 1) * J).astype(np.float32)[:, None]
    arrays["iota"] = np.tile(r.astype(np.float32)[None], (P, 1))
    arrays = {k: np.ascontiguousarray(v) for k, v in arrays.items()}

    nc = bacc.Bacc("TRN2", target_bir_lowering=False, num_devices=1)
    d = {k: nc.dram_tensor("in_" + k, v.shape, mybir.dt.from_np(v.dtype), kind="ExternalInput").ap()
         for k, v in arrays.items()}
    out = nc.dram_tensor("out", (N, F), F32, kind="ExternalOutput").ap()
    graph_kernel(nc, d, out)
    got = run_bass_kernel_spmd(nc, [{"in_" + k: v for k, v in arrays.items()}], core_ids=[0])
    return got.results[0]["out"]
```

```python
from contextlib import ExitStack

import numpy as np
import concourse.bass as bass
from concourse import mybir

P = 128
N, E, F = 12500, 200000, 32
NP_REAL = 125
NT = N // NP_REAL
NPAD = P * NT
JC = 56
NCH = 28
J = JC * NCH
EP = P * J
HALF = NCH // 2
G = 4
NG = JC // G
V = 2 * G
NV = JC // V
ZW = 96
ZQ, ZS, ZV, ZA = 8, 24, 56, 80
ZE = 90
NA = 3 * P
NB = 3 * P + 16
WN = NA + 2 * NB
AW = 34
RW = 33
HC = 14
BIG = 1.0e38
EPS = 1e-5
TANH_GAIN = 1.593
PW_S, PW_V = 0.17677669529663687, 0.25
W121 = 1.5 ** 0.5
ALPHA = 2.0 ** 0.5 / 10.0 ** 0.5 / 4.0
LEAKY = 0.01

ALU = mybir.AluOpType
ACT = mybir.ActivationFunctionType
AX = mybir.AxisListType
F32 = mybir.dt.float32
I32 = mybir.dt.int32
BF16 = mybir.dt.bfloat16


def after(eng, sem, value):
    if isinstance(value, int) and value <= 0:
        return
    eng.wait_ge(sem, value)


class Steps:

    def __init__(self, eng, sem, base=0):
        self.eng, self.sem, self.base, self.k = eng, sem, base, 0

    def done(self, ins):
        self.k += 1
        ins.then_inc(self.sem, 1)
        return self.k

    def settle(self):
        after(self.eng, self.sem, self.base + self.k)


def graph_kernel(nc, d, out):
    with ExitStack() as ctx:
        def sb(name, shape, dt=F32):
            return ctx.enter_context(nc.sbuf_tensor(name, shape, dt))

        sems = {}

        def sem(name):
            if name not in sems:
                sems[name] = ctx.enter_context(nc.semaphore(name))
            return sems[name]

        def dram(name, shape, dt=F32):
            return nc.dram_tensor(name, shape, dt).ap()

        spread = dram("spread", (EP + NPAD, F))
        spread1 = dram("spread1", (EP + NPAD, 1))
        end_table = dram("end_table", (NPAD, 1), I32)
        table = {0: dram("table0", (NPAD, F)), 1: dram("table1", (NPAD, AW)),
                 2: dram("table2", (NPAD, F)), 3: dram("table3", (NPAD, F)),
                 4: dram("table4", (NPAD, F))}
        width = {0: F, 1: RW, 2: F, 3: F, 4: F}
        rows = {k: dram(f"rows{k}", (EP + P, width[k])) for k in width}
        stash = dram("stash", (EP, AW))

        x = sb("x", [P, NT, F])
        prod_f = sb("prod", [P, NT * F + J + 2 * P + NT])
        prod = prod_f[:, 0:4 * 768].rearrange("p (b w) -> p b w", b=4)
        h = prod_f[:, 0:NT * F].rearrange("p (t f) -> p t f", f=F)
        zero = prod_f[:, NT * F:NT * F + J]
        hot = prod_f[:, 0:HC * (P + NT)].bitcast(BF16).rearrange("p (k w) -> p k w", w=P + NT)
        fetched = sb("fetched", [P, NT * RW])
        att = sb("att", [P, NT * AW])
        zin = sb("zin", [P, 2, JC * ZW])
        zout = sb("zout", [P, 2, JC * RW])
        keep = sb("keep", [P, J])
        pen = sb("pen", [P, J])
        ea = sb("ea", [P, 6, J])
        dst0 = sb("dst0", [P, 1], I32)
        idx = sb("idx", [P, 2, JC], I32)
        start_idx = sb("start_idx", [P, NT], I32)
        end_idx = sb("end_idx", [P, NT], I32)
        fix_idx = sb("fix_idx", [P, 1], I32)
        fix_end = sb("fix_end", [P, 1], I32)
        has = sb("has", [P, NT])
        nohas = sb("nohas", [P, NT])
        dinv = sb("dinv", [P, NT])
        n1 = sb("n1", [P, NT])
        n2 = sb("n2", [P, NT])
        n3 = sb("n3", [P, NT])
        c1 = sb("c1", [P, 1])
        c2 = sb("c2", [P, 1])
        c3 = sb("c3", [P, 1])
        krow = sb("krow", [RW, P])
        penkrow = sb("penkrow", [RW, P])
        bkrow = sb("bkrow", [1, P])
        kcols = sb("kcols", [P, RW])
        rowa = sb("rowa", [RW, P])
        rowb = sb("rowb", [RW, P])
        rowc = sb("rowc", [RW, P])
        carry_in = sb("carry_in", [P, F])
        carry = sb("carry", [P, RW])
        fix = sb("fix", [P, AW])
        ident = sb("ident", [P, P])
        once = prod_f[:, NT * F + J:]
        before = once[:, 0:P]
        dump = sb("dump", [P, 1])
        dump_n = once[:, 2 * P:2 * P + NT]
        plimit = sb("plimit", [P, 1])
        iota_f = once[:, P:2 * P]
        iota_b = sb("iota_b", [P, P], BF16)
        w01 = sb("w01", [3 * F, 64])
        w02 = sb("w02", [64, F])
        b01 = sb("b01", [64, 1])
        b02 = sb("b02", [P, F])
        aw = sb("aw", [P, 2 * F])
        w31 = sb("w31", [F, 64])
        w32 = sb("w32", [64, F])
        b31 = sb("b31", [64, 1])
        b32 = sb("b32", [P, F])
        wz = [sb(f"wz{q}", [P, WN], BF16) for q in range(2)]
        ident_b = sb("ident_b", [P, P], BF16)
        tz = sb("tz", [P, 2, 768])
        hid = sb("hid", [P, 2, 512])
        dst_rows = sb("dst_rows", [P, JC * F])
        qtemp = sb("qtemp", [P, 2 * JC * 16])
        tz_b = tz[:, :, :].rearrange("p b w -> p (b w)").bitcast(BF16).rearrange(
            "p (b j s e) -> p b j s e", b=2, j=G, s=3)
        parts = ea[:, 4:6, :].rearrange("p a j -> p (a j)")[:, 0:2 * V * 192].bitcast(BF16).rearrange(
            "p (b j k f) -> p b j k f", b=2, j=3 * V, k=4)
        rest = pen[:, 0:V * ZW].rearrange("p (j f) -> p j f", f=32)
        w_f, w_sub = prod_f[:, 0:WN], prod_f[:, WN:WN + 2 * NB]
        w_rest = prod_f[:, WN + 2 * NB:2 * WN + 2 * NB]
        w121 = prod_f[:, 2 * WN + 2 * NB:2 * WN + 2 * NB + 1]
        eo = [t[:, 0:JC * 48].rearrange("p (j w) -> p j w", w=48) for t in (att, fetched)]

        psum = ctx.enter_context(nc.psum_tensor("psum", [P, 8 * 512], F32))
        bank = [psum[:, 512 * i:512 * (i + 1)] for i in range(8)]
        turned01 = bank[0].bitcast(BF16).rearrange("p (j w) -> p j w", j=G)
        turned2 = bank[1].bitcast(BF16)[:, 0:G * P].rearrange("p (j w) -> p j w", j=G)
        y = psum[:, 2 * 512:6 * 512].rearrange("p (j a w) -> p j a w", j=2, a=2)

        def zrow(b, w):
            return zin[:, b, 0:JC * w].rearrange("p (j w) -> p j w", w=w)

        def orow(b, w):
            return zout[:, b, 0:JC * w].rearrange("p (j w) -> p j w", w=w)

        def orow_flat(b, w):
            return zout[:, b, 0:JC * w]

        def hold(eng, semaphore, value):
            after(eng, semaphore, value)
            if not isinstance(value, int):
                eng.sem_inc(sem("gate"))

        def steps(eng, step, lags):
            for b in range(2):
                for s in range(NG):
                    step(0, b, b, s)
            with eng.Fori(1, HALF - 1) as i:
                for b in range(2):
                    for s in range(NG):
                        step(i, b, 2 * i + b, s)
            for b in range(2):
                for s in range(NG):
                    step(HALF - 1, b, NCH - 2 + b, s)
            for s in range(lags):
                step(HALF, 0, NCH, s)

        def behind(i, b, c, s, lag):
            if s >= lag:
                return None if isinstance(c, int) and c == NCH else (i, b, c, s - lag)
            if isinstance(c, int) and c == 0:
                return None
            return (i if b == 1 else i - 1, 1 - b, c - 1, s - lag + NG)

        def chunks(eng, body):
            for b in range(2):
                body(0, b, b)
            with eng.Fori(1, HALF) as i:
                for b in range(2):
                    body(i, b, 2 * i + b)

        def cols(c):
            return slice(c * JC, (c + 1) * JC) if isinstance(c, int) else bass.ds(c * JC, JC)

        consts = [(w01[:, :], d["w01"]), (w02[:, :], d["w02"]), (b01[:, :], d["b01"]), (b02[:, :], d["b02"]),
                  (aw[:, :], d["aw"]), (w31[:, :], d["w31"]), (w32[:, :], d["w32"]), (b31[:, :], d["b31"]),
                  (b32[:, :], d["b32"]), (w_f, d["w_f"]), (w_sub, d["w_sub"]), (w121, d["w121"]),
                  (ident[:, :], d["ident"]), (before, d["before"]), (dump[:, :], d["dump"]), (dump_n, d["dump_n"]),
                  (plimit[:, :], d["plimit"]), (iota_f, d["iota"])]
        fetch = {k: fetched[:, 0:NT * width[k]].rearrange("p (t w) -> p t w", w=width[k])
                 for k in width}
        att3 = att[:, :].rearrange("p (t w) -> p t w", w=AW)
        scratch = att[:, 0:NT * F].rearrange("p (t w) -> p t w", w=F)
        dst_i, prev_i, next_i = (fetched[:, 0:J].bitcast(I32), fetched[:, J:2 * J].bitcast(I32),
                                 zout[:, :, :].rearrange("p b w -> p (b w)")[:, 0:J].bitcast(I32))

        block = ctx.enter_context(nc.Block())

        @block.sync
        def _(sp):
            for dst, src in ((dst_i, d["dst"][1:1 + EP]), (prev_i, d["dst"][0:EP]),
                             (next_i, d["dst"][2:2 + EP])):
                sp.dma_start(dst, src.rearrange("(p j) -> p j", j=J)).then_inc(sem("dst_loaded"), 16)
            sp.wait_ge(sem("x_cleared"), 1)
            sp.dma_start(x[0:NP_REAL], d["x"].rearrange("(p t) f -> p t f", t=NT)
                         ).then_inc(sem("x_loaded"), 16)
            for dst, src in consts:
                sp.dma_start(dst, src).then_inc(sem("consts_loaded"), 16)
            sp.wait_ge(sem("zero_ready"), 1)
            sp.dma_start(spread1[0:EP].rearrange("(p j) w -> p (j w)", j=J), zero[:, :]
                         ).then_inc(sem("filled"), 16)
            for k in range(F):
                sp.dma_start(spread[0:EP].rearrange("(p c j) w -> p c (j w)", p=P, c=F)[:, k], zero[:, :]
                             ).then_inc(sem("filled"), 16)
            for k in width:
                sp.dma_start(rows[k][EP:EP + P], zero[:, 0:width[k]]).then_inc(sem("filled"), 16)
            sp.wait_ge(sem("end_idx_ready"), 1)
            sp.dma_start(end_table.rearrange("(p t) w -> p (t w)", t=NT), end_idx[:, :]
                         ).then_inc(sem("end_table_stored"), 16)

            def store_table(k, tile):
                if k == 4:
                    sp.wait_ge(sem("out_copied3"), NT // G)
                else:
                    sp.wait_ge(sem("table_ready"), k + 1)
                sp.dma_start(table[k].rearrange("(p t) w -> p (t w)", t=NT), tile
                             ).then_inc(sem("table_stored"), 16)

            def load_idx(k, b, c):
                sp.dma_start(idx[:, b], d["src"][:, cols(c)]).then_inc(sem(f"idx_loaded{b}"), 16)

            def store_rows(k, i, b, c):
                hold(sp, sem("scanned"), NCH * k + c + 1)
                sp.dma_start(rows[k][0:EP].rearrange("(p j) w -> p (j w)", j=J)[
                    :, wcols(c, width[k])], orow_flat(b, width[k])).then_inc(sem(f"stored{b}"), 16)

            def wcols(c, w):
                return slice(c * JC * w, (c + 1) * JC * w) if isinstance(c, int) else bass.ds(c * JC * w, JC * w)

            def later_store(k, i, b, c):
                if b == 1:
                    store_rows(k, i, 0, c - 1)
                elif not isinstance(i, int):
                    store_rows(k, i - 1, 1, c - 1)

            def spread_rows(b, c):
                return spread[0:EP].rearrange("(p j) w -> p j w", j=J)[:, cols(c), :]

            store_table(0, h[:, :, :].rearrange("p t f -> p (t f)"))

            def body0(i, b, c):
                hold(sp, sem("transposed0"), NG * (c - 1))
                load_idx(0, b, c)
                sp.dma_start(zrow(b, ZW)[:, :, 2 * F:3 * F],
                             d["a32"].rearrange("(p j) w -> p j w", j=J)[:, cols(c), :]
                             ).then_inc(sem(f"loaded0_{b}"), 16)
                if isinstance(i, int) and b == 0:
                    sp.wait_ge(sem("spread"), 16 * NT * 1)
                sp.dma_start(zrow(b, ZW)[:, :, F:2 * F], spread_rows(b, c)
                             ).then_inc(sem(f"loaded0_{b}"), 16)
                later_store(0, i, b, c)
            chunks(sp, body0)
            store_rows(0, HALF - 1, 1, NCH - 1)

            store_table(1, att[:, :])

            def body1(i, b, c):
                hold(sp, sem("score_copied"), c - 1)
                if not (isinstance(i, int)):
                    sp.wait_ge(sem(f"stashed{b}"), 16 * i)
                load_idx(1, b, c)
                if b == 1:
                    stash_rows(i, 0, c - 1)
                elif not isinstance(i, int):
                    stash_rows(i - 1, 1, c - 1)

            def stash_rows(i, b, c):
                hold(sp, sem(f"gathered1_{b}"), 16 * JC * (i + 1))
                sp.dma_start(stash.rearrange("(p j) w -> p (j w)", j=J)[:, wcols(c, AW)],
                             zin[:, b, 0:JC * AW]).then_inc(sem(f"stashed{b}"), 16)
            chunks(sp, body1)
            stash_rows(HALF - 1, 1, NCH - 1)
            sp.wait_ge(sem("spread"), 16 * NT * 2)
            sp.wait_ge(sem("table_ready"), 2)
            sp.dma_start(ea[:, 1], spread1[0:EP].rearrange("(p j) w -> p (j w)", j=J)
                         ).then_inc(sem("spread1_loaded"), 16)
            for b in range(2):
                sp.wait_ge(sem(f"stashed{b}"), 16 * HALF)

            def body1b(i, b, c):
                if isinstance(i, int) and b == 0:
                    sp.wait_ge(sem("score_copied"), NCH)
                hold(sp, sem("weighted"), c - 1)
                sp.dma_start(zin[:, b, 0:JC * AW],
                             stash.rearrange("(p j) w -> p (j w)", j=J)[:, wcols(c, AW)]
                             ).then_inc(sem(f"loaded1_{b}"), 16)
                later_store(1, i, b, c)
            chunks(sp, body1b)
            store_rows(1, HALF - 1, 1, NCH - 1)

            sp.wait_ge(sem("scanned"), 2 * NCH)
            sp.dma_start(zin[:, :, :].rearrange("p b w -> p (b w)")[:, 0:3 * J],
                         d["a3"].rearrange("(p j) w -> p (j w)", j=J)).then_inc(sem("vec_loaded"), 16)
            sp.dma_start(ea[:, 3], d["wgt"].rearrange("(p j) -> p j", j=J)).then_inc(sem("vec_loaded"), 16)
            store_table(2, att[:, 0:NT * F])
            sp.wait_ge(sem("vec_read"), 1)

            def body2(i, b, c):
                hold(sp, sem("spread_done2"), c)
                if isinstance(i, int) and b == 0:
                    sp.wait_ge(sem("spread"), 16 * NT * 3)
                sp.dma_start(dst_rows[:, :].rearrange("p (j w) -> p j w", w=F), spread_rows(b, c)
                             ).then_inc(sem("dst_rows_loaded"), 16)
                hold(sp, sem("split2"), NV * (c - 1))
                load_idx(2, b, c)
                sp.dma_start(zrow(b, ZW)[:, :, ZA:ZE],
                             d["a10"].rearrange("(p j) w -> p j w", j=J)[:, cols(c), :]
                             ).then_inc(sem(f"loaded2_{b}"), 16)
                if not isinstance(i, int):
                    store_rows(2, i - 1, b, c - 2)
            chunks(sp, body2)
            store_rows(2, HALF - 1, 0, NCH - 2)
            store_rows(2, HALF - 1, 1, NCH - 1)

            for k in (3, 4):
                store_table(k, h[:, :, :].rearrange("p t f -> p (t f)"))

                def body3(i, b, c):
                    hold(sp, sem("scanned"), NCH * k + c - 1)
                    load_idx(k, b, c)
                    later_store(k, i, b, c)
                chunks(sp, body3)
                store_rows(k, HALF - 1, 1, NCH - 1)

            sp.wait_ge(sem("x_final"), 1)
            sp.dma_start(out.rearrange("(p t) f -> p t f", t=NT), x[0:NP_REAL]).then_inc(sem("out_stored"), 16)
            sp.wait_ge(sem("out_stored"), 16)

        @block.gpsimd
        def _(pool):
            def take(dst, src, index):
                return pool.indirect_dma_start(out=dst, out_offset=None, in_=src,
                                               in_offset=bass.IndirectOffsetOnAxis(ap=index, axis=0))

            def put(dst, index, src):
                return pool.indirect_dma_start(out=dst, out_offset=bass.IndirectOffsetOnAxis(ap=index, axis=0),
                                               in_=src, in_offset=None)

            def gather(k, w, row_width, first=0):
                pool.wait_ge(sem("table_stored"), 16 * (k + 1))

                def body(i, b, c):
                    hold(pool, sem(f"idx_loaded{b}"), 16 * (HALF * k + i + 1))
                    for j in range(JC):
                        take(zrow(b, row_width)[:, j, first:first + w], table[k], idx[:, b, j:j + 1]
                             ).then_inc(sem(f"gathered{k}_{b}"), 16)
                chunks(pool, body)

            def fix_and_fetch(k):
                w = width[k]
                for b in range(2):
                    pool.wait_ge(sem(f"stored{b}"), 16 * HALF * (k + 1))
                take(fix[:, 0:w], rows[k], fix_idx[:, 0:1]).then_inc(sem("fix_fetched"), 16)
                pool.wait_ge(sem("fix_ready"), k + 1)
                put(rows[k], fix_idx[:, 0:1], fix[:, 0:w]).then_inc(sem("fix_stored"), 16)
                pool.wait_ge(sem("fix_stored"), 16 * (k + 1))
                for t in range(NT):
                    take(fetch[k][:, t, :], rows[k], end_idx[:, t:t + 1]).then_inc(sem("fetched"), 16)

            def spread_nodes(k, tile, where, first, w):
                pool.wait_ge(sem("table_ready"), k + 1)
                for t in range(NT):
                    put(where, start_idx[:, t:t + 1], tile(t)).then_inc(sem("spread"), 16)
                pool.wait_ge(sem("table_stored"), 16 * (k + 1))
                take(first, table[k], dst0[:, 0:1]).then_inc(sem("first"), 16)

            pool.wait_ge(sem("start_idx_ready"), 1)
            pool.wait_ge(sem("filled"), 16 * (1 + F + len(width)))
            pool.wait_ge(sem("end_table_stored"), 16)
            pool.wait_ge(sem("dst0_ready"), 1)
            take(fix_end[:, :], end_table, dst0[:, 0:1]).then_inc(sem("fix_end_fetched"), 16)
            spread_nodes(0, lambda t: h[:, t, :], spread, carry_in[:, :], F)
            gather(0, F, ZW)
            pool.wait_ge(sem("fix_idx_ready"), 1)
            fix_and_fetch(0)
            spread_nodes(1, lambda t: att3[:, t, F + 1:F + 2], spread1, fix[:, 0:AW], 1)
            gather(1, AW, AW)
            fix_and_fetch(1)
            spread_nodes(2, lambda t: scratch[:, t, :], spread, carry_in[:, :], F)
            pool.wait_ge(sem("vec_read"), 1)
            gather(2, F, ZW, ZS)
            fix_and_fetch(2)
            for k in (3, 4):
                gather(k, F, F)
                fix_and_fetch(k)

        @block.scalar
        def _(act):
            def copy(dst, src):
                return act.activation(dst, src, ACT.Copy)

            def root(k):
                act.wait_ge(sem("recip"), k + 1)
                act.activation(n3[:, :], n2[:, :], ACT.Sqrt).then_inc(sem("rstd"), 1)

            act.wait_ge(sem("deg_recip"), 1)
            act.activation(dinv[:, :], dinv[:, :], ACT.Sqrt).then_inc(sem("dinv_ready"), 1)
            root(0)
            act.wait_ge(sem("consts_loaded"), 16 * len(consts))

            def body0(i, b, c):
                for s in range(NG + 2):
                    n = c * NG + s
                    if s < NG:
                        act.wait_ge(sem("transposed0"), n + 1)
                        after(act, sem("hidden0"), n - 1)
                        copy(tz[0:ZW, s % 2, 0:512], bank[s % 2][0:ZW, :]).then_inc(sem("transposed_copied0"), 1)
                    if 1 <= s <= NG:
                        m, g = n - 1, s - 1
                        act.wait_ge(sem("hidden0"), m + 1)
                        after(act, sem("out0"), m - 1)
                        act.activation(hid[0:64, g % 2, :], bank[2 + g % 2][0:64, :], ACT.Relu,
                                       bias=b01[:, 0:1]).then_inc(sem("relu0"), 1)
                    if s >= 2:
                        m, g = n - 2, s - 2
                        act.wait_ge(sem("out0"), m + 1)
                        if g == 0:
                            after(act, sem("scanned"), c - 1)
                            if not isinstance(i, int):
                                act.wait_ge(sem(f"stored{b}"), 16 * (HALF * 0 + i))
                        copy(orow(b, F)[:, g * G:(g + 1) * G, :],
                             bank[4 + g % 2][:, 0:G * F].rearrange("p (j w) -> p j w", w=F)
                             ).then_inc(sem("out_copied0"), 1)
            chunks(act, body0)

            root(1)

            def body1(i, b, c):
                hold(act, sem(f"gathered1_{b}"), 16 * JC * (i + 1))
                copy(ea[:, 0, cols(c)], zrow(b, AW)[:, :, F]).then_inc(sem("score_copied"), 1)
            chunks(act, body1)
            act.wait_ge(sem("logits"), 1)
            act.activation(ea[:, 0], ea[:, 1], ACT.Exp).then_inc(sem("weights_ready"), 1)

            act.wait_ge(sem("norm2_ready"), 1)
            act.activation(ea[:, 5], ea[:, 4], ACT.Sqrt).then_inc(sem("rnorm_ready"), 1)
            root(2)

            def split_high(b, c, v):
                if v == 0:
                    act.wait_ge(sem("ready2"), c + 1)
                after(act, sem("transposed2"), 2 * (c * NV + v) - 2)
                z = zrow(b, ZW)[:, v * V:(v + 1) * V, :].rearrange("p j (s f) -> p (j s) f", s=3)
                copy(parts[:, (b + v) % 2, :, 0:4:3, :],
                     z.unsqueeze(2).broadcast_to([P, 3 * V, 2, 32])).then_inc(sem("split_high"), 1)

            def split_mid(b, c, v):
                act.wait_ge(sem("split_rest"), c * NV + v + 1)
                copy(parts[:, (b + v) % 2, :, 1, :], rest).then_inc(sem("split_mid"), 1)

            def next_split(i, b, c, s):
                if isinstance(c, int) and (c == NCH or (c == NCH - 1 and s >= NG - 2)):
                    return None
                v = s // 2 + 1
                return (b, c, v) if v < NV else (1 - b, c + 1, 0)

            def step2(i, b, c, s):
                nxt = next_split(i, b, c, s)
                if nxt and s % 2 == 0:
                    split_high(*nxt)
                elif nxt:
                    split_mid(*nxt)
                if behind(i, b, c, s, 0):
                    n = c * NG + s
                    act.wait_ge(sem("transposed2"), n + 1)
                    after(act, sem("column2"), G * (n - 1))
                    copy(tz_b[:, s % 2, :, 0:2, :].rearrange("p j s e -> p j (s e)"), turned01)
                    copy(tz_b[:, s % 2, :, 2, :], turned2).then_inc(sem("transposed_copied2"), 1)
                if at := behind(i, b, c, s, 1):
                    _, _, cc, g = at
                    for j in range(G):
                        act.wait_ge(sem("hidden2"), G * (cc * NG + g) + j + 1)
                        act.activation(hid[:, 0, 16 * j:16 * (j + 1)], y[:, j % 2, 1, 3 * P:NB], ACT.Relu
                                       ).then_inc(sem("relu2"), 1)
                if s == 2 and not (isinstance(c, int) and c in (0, NCH)):
                    tanh2(1 - b, c - 1)

            def tanh2(b, c):
                act.wait_ge(sem("summed2"), JC // 2 * (c + 1))
                act.activation(eo[b][:, :, 0:16], eo[b][:, :, 0:16], ACT.Tanh).then_inc(sem("tanh2"), 1)
            split_high(0, 0, 0)
            split_mid(0, 0, 0)
            steps(act, step2, 1)
            tanh2(1, NCH - 1)

            root(3)

            for g in range(NT // G):
                act.wait_ge(sem("transposed3"), g + 1)
                after(act, sem("hidden3"), g - 1)
                copy(tz[0:F, g % 2, 0:512], bank[g % 2][0:F, :]).then_inc(sem("transposed_copied3"), 1)
                act.wait_ge(sem("hidden3"), g + 1)
                after(act, sem("out3"), g - 1)
                act.activation(hid[0:64, g % 2, :], bank[2 + g % 2][0:64, :], ACT.Relu,
                               bias=b31[:, 0:1]).then_inc(sem("relu3"), 1)

        @block.tensor
        def _(pe):
            pe.wait_ge(sem("consts_loaded"), 16 * len(consts))

            def hist(i, b):
                hh = 2 * i + b
                pe.wait_ge(sem("hot"), hh + 1)
                for k in range(HC):
                    first = isinstance(i, int) and b == 0 and k == 0
                    ins = pe.matmul(bank[7][:, 0:NT], hot[:, b * HC + k, 0:P], hot[:, b * HC + k, P:P + NT],
                                    start=first, stop=False, skip_group_check=True)
                ins.then_inc(sem("hot_used"), 1)
            for b in range(2):
                hist(0, b)
            with pe.Fori(1, J // (2 * HC)) as i:
                for b in range(2):
                    hist(i, b)
            pe.wait_ge(sem("deg_scanned"), 1)
            pe.matmul(bank[6][:, 0:1], before[:, :], n1[:, NT - 1:NT], start=True, stop=True
                      ).then_inc(sem("base_ready"), 1)
            for m, (src, w) in enumerate(((kcols[:, 0:RW], RW), (fix[:, 0:RW], RW), (c3[:, :], 1))):
                pe.wait_ge(sem("marks_ready"), m + 1)
                pe.transpose(bank[m][0:w, 0:P], src, ident[:, :]).then_inc(sem("marks_turned"), 1)

            def turn_carry(k):
                w = width[k]
                pe.wait_ge(sem("scanned"), NCH * (k + 1))
                pe.transpose(bank[6][0:w, 0:P], carry[:, 0:w], ident[:, :]).then_inc(sem("carry_turned"), 1)
                pe.wait_ge(sem("carry_scanned"), k + 1)
                pe.transpose(bank[7][:, 0:w], rowc[0:w, :], ident[0:w, 0:w]).then_inc(sem("carry_turned"), 1)

            def body0(i, b, c):
                for s in range(NG + 2):
                    n = c * NG + s
                    if s < NG:
                        if s == 0:
                            pe.wait_ge(sem(f"gathered0_{b}"), 16 * JC * (i + 1))
                            pe.wait_ge(sem(f"loaded0_{b}"), 32 * (i + 1))
                            pe.wait_ge(sem("spread_done0"), c + 1)
                        after(pe, sem("transposed_copied0"), n - 1)
                        for j in range(G):
                            ins = pe.transpose(bank[s % 2][0:ZW, j * P:(j + 1) * P],
                                               zrow(b, ZW)[:, s * G + j, :], ident[:, :])
                        ins.then_inc(sem("transposed0"), 1)
                    if 1 <= s <= NG:
                        m, g = n - 1, s - 1
                        pe.wait_ge(sem("transposed_copied0"), m + 1)
                        after(pe, sem("relu0"), m - 1)
                        pe.matmul(bank[2 + g % 2][0:64, :], w01[:, :], tz[0:ZW, g % 2, 0:512],
                                  start=True, stop=True).then_inc(sem("hidden0"), 1)
                    if s >= 2:
                        m, g = n - 2, s - 2
                        pe.wait_ge(sem("relu0"), m + 1)
                        after(pe, sem("out_copied0"), m - 1)
                        for j in range(G):
                            ins = pe.matmul(bank[4 + g % 2][:, j * F:(j + 1) * F],
                                            hid[0:64, g % 2, j * P:(j + 1) * P], w02[:, :],
                                            start=True, stop=True)
                        ins.then_inc(sem("out0"), 1)
            chunks(pe, body0)
            turn_carry(0)
            for m in range(2):
                pe.wait_ge(sem("max_end"), m + 1)
                pe.transpose(bank[0][0:1, 0:P], c1[:, :], ident[:, :]).then_inc(sem("max_turned"), 1)
                pe.wait_ge(sem("max_scanned"), m + 1)
                pe.transpose(bank[1][:, 0:1], rowc[0:1, :], ident[0:1, 0:1]).then_inc(sem("max_turned"), 1)
            turn_carry(1)

            def step2(i, b, c, s):
                if behind(i, b, c, s, 0):
                    n = c * NG + s
                    if s % 2 == 0:
                        pe.wait_ge(sem("split2"), c * NV + s // 2 + 1)
                    after(pe, sem("transposed_copied2"), n)
                    for j in range(G):
                        for q in range(3):
                            to = turned01[:, j, q * P:(q + 1) * P] if q < 2 else turned2[:, j]
                            ins = pe.transpose(to, parts[:, (b + s // 2) % 2, 3 * ((s % 2) * G + j) + q].rearrange(
                                "p k f -> p (k f)"), ident_b[:, :])
                    ins.then_inc(sem("transposed2"), 1)
                if at := behind(i, b, c, s, 1):
                    _, _, cc, g = at
                    m = cc * NG + g
                    pe.wait_ge(sem("transposed_copied2"), m + 1)
                    for j in range(G):
                        after(pe, sem("product2"), G * m + j - 1)
                        rows_ = [tz_b[:, g % 2, j, q] for q in range(3)]
                        for r in range(2):
                            for q in range(2):
                                ins = pe.matmul(y[:, j % 2, 1, 0:NB], rows_[1 + r],
                                                wz[q][:, NA + r * NB:NA + (r + 1) * NB],
                                                start=(r == 0 and q == 0), stop=(r == 1 and q == 1))
                        ins.then_inc(sem("hidden2"), 1)
                        for q in range(2):
                            ins = pe.matmul(y[:, j % 2, 0, 0:NA], rows_[0], wz[q][:, 0:NA],
                                            start=(q == 0), stop=(q == 1))
                        ins.then_inc(sem("column2"), 1)
            pe.wait_ge(sem("weights2_ready"), 1)
            steps(pe, step2, 1)
            turn_carry(2)
            turn_carry(3)

            for g in range(NT // G):
                pe.wait_ge(sem("update3"), 1)
                after(pe, sem("transposed_copied3"), g - 1)
                for j in range(G):
                    ins = pe.transpose(bank[g % 2][0:F, j * P:(j + 1) * P], scratch[:, g * G + j, :], ident[:, :])
                ins.then_inc(sem("transposed3"), 1)
                pe.wait_ge(sem("transposed_copied3"), g + 1)
                after(pe, sem("relu3"), g - 1)
                pe.matmul(bank[2 + g % 2][0:64, :], w31[:, :], tz[0:F, g % 2, 0:512], start=True, stop=True
                          ).then_inc(sem("hidden3"), 1)
                pe.wait_ge(sem("relu3"), g + 1)
                after(pe, sem("out_copied3"), g - 1)
                for j in range(G):
                    ins = pe.matmul(bank[4 + g % 2][:, j * F:(j + 1) * F], hid[0:64, g % 2, j * P:(j + 1) * P],
                                    w32[:, :], start=True, stop=True)
                ins.then_inc(sem("out3"), 1)
            turn_carry(4)

        @block.vector
        def _(dve):
            order = [0]

            def link(ins):
                order[0] += 1
                ins.then_inc(sem("dve_order"), 1)
                dve.wait_ge(sem("dve_order"), order[0])

            def mark(ins, name, value=1):
                ins.then_inc(sem(name), 1)
                dve.wait_ge(sem(name), value)

            def over(t, w=F):
                return t.unsqueeze(2).broadcast_to([P, t.shape[1], w])

            def along(t, n=NT):
                return t.unsqueeze(1).broadcast_to([P, n, t.shape[1]])

            tt, ts, stt = dve.tensor_tensor, dve.tensor_scalar, dve.scalar_tensor_tensor
            scan = dve.tensor_tensor_scan

            mark(dve.memset(x[:, :, :], 0.0), "x_cleared")
            mark(dve.memset(zero[:, :], 0.0), "zero_ready")

            dve.wait_ge(sem("dst_loaded"), 48)
            mark(dve.tensor_copy(dst0[:, :], dst_i[:, 0:1]), "dst0_ready")
            link(tt(keep[:, :], dst_i, prev_i, ALU.is_equal))
            link(tt(ea[:, 4], dst_i, next_i, ALU.is_equal))
            link(ts(pen[:, :], keep[:, :], -1.0, BIG, ALU.add, ALU.mult))
            link(ts(ea[:, 5], ea[:, 4], -1.0, BIG, ALU.add, ALU.mult))
            link(dve.tensor_copy(ea[:, 0], dst_i))
            link(ts(prev_i, ea[:, 0], 1.0 / NT, None, ALU.mult))
            link(dve.tensor_copy(ea[:, 1], prev_i))
            link(stt(ea[:, 2], ea[:, 1], -float(NT), ea[:, 0], ALU.mult, ALU.add))
            link(ts(ea[:, 3], ea[:, 2], 0.0, None, ALU.is_lt))
            link(tt(ea[:, 1], ea[:, 1], ea[:, 3], ALU.subtract))
            link(stt(ea[:, 2], ea[:, 3], float(NT), ea[:, 2], ALU.mult, ALU.add))
            link(ts(ea[:, 3], ea[:, 2], float(NT), None, ALU.is_ge))
            link(tt(ea[:, 1], ea[:, 1], ea[:, 3], ALU.add))
            link(stt(ea[:, 2], ea[:, 3], -float(NT), ea[:, 2], ALU.mult, ALU.add))
            link(dve.tensor_reduce(c2[:, :], keep[:, :], AX.X, ALU.min))
            link(dve.tensor_reduce(c3[:, :], ea[:, 4], AX.X, ALU.min))
            mark(ts(kcols[:, :], zero[:, 0:RW], c2[:, 0:1], None, ALU.add), "marks_ready", 1)
            mark(ts(fix[:, 0:RW], kcols[:, :], -1.0, BIG, ALU.add, ALU.mult), "marks_ready", 2)
            mark(ts(c3[:, :], c3[:, :], -1.0, BIG, ALU.add, ALU.mult), "marks_ready", 3)

            dve.wait_ge(sem("consts_loaded"), 16 * len(consts))
            link(dve.tensor_copy(iota_b[:, :], iota_f[:, :]))
            link(dve.tensor_copy(ident_b[:, :], ident[:, :]))
            link(ts(w_f[:, 0:2 * P], w_f[:, 0:2 * P], ALPHA * PW_S, None, ALU.mult))
            link(ts(w_f[:, 2 * P:NA], w_f[:, 2 * P:NA], ALPHA * PW_V, None, ALU.mult))
            link(ts(w_f[:, 2 * P:NA], w_f[:, 2 * P:NA], w121, None, ALU.mult))
            link(ts(w_sub, w_sub, -ALPHA * PW_V * W121 / 3.0, None, ALU.mult))
            for r in range(2):
                v = w_f[:, NA + r * NB:NA + r * NB + 3 * P]
                link(stt(v, v, ALPHA * PW_V / 3.0 ** 0.5, w_sub[:, r * NB:r * NB + 3 * P], ALU.mult, ALU.add))
            link(dve.tensor_copy(wz[0][:, :], w_f))
            link(tt(w_rest, w_f, wz[0][:, :], ALU.subtract))
            link(dve.tensor_copy(wz[1][:, :], w_rest))
            link(tt(w_rest, w_rest, wz[1][:, :], ALU.subtract))
            link(dve.tensor_copy(wz[0][ZW:P, :], w_rest[ZW:P, :]))
            mark(dve.memset(wz[1][ZW:P, :], 0.0), "weights2_ready")

            def hist(i, b):
                hh = 2 * i + b
                after(dve, sem("hot_used"), hh - 1)
                for k in range(HC):
                    col = (hh * HC + k)
                    at = slice(col, col + 1) if isinstance(col, int) else bass.ds(col, 1)
                    ts(hot[:, b * HC + k, 0:P], iota_b[:, :], ea[:, 1, at], None, ALU.is_equal)
                    ins = ts(hot[:, b * HC + k, P:P + NT], iota_b[:, 0:NT], ea[:, 2, at], None, ALU.is_equal)
                ins.then_inc(sem("hot"), 1)
            for b in range(2):
                hist(0, b)
            with dve.Fori(1, J // (2 * HC)) as i:
                for b in range(2):
                    hist(i, b)

            dve.wait_ge(sem("hot_used"), J // HC)
            link(dve.tensor_copy(n2[:, :], bank[7][:, 0:NT]))
            link(ts(has[:, :], n2[:, :], 0.0, None, ALU.is_gt))
            link(ts(nohas[:, :], has[:, :], -1.0, BIG, ALU.add, ALU.mult))
            link(ts(n3[:, :], n2[:, :], 1.0, None, ALU.add))
            mark(dve.reciprocal(dinv[:, :], n3[:, :]), "deg_recip")
            link(ts(n3[:, :], n2[:, :], 0.0, 1.0, ALU.mult, ALU.add))
            mark(scan(n1[:, :], n3[:, :], n2[:, :], 0.0, ALU.mult, ALU.add), "deg_scanned")
            dve.wait_ge(sem("base_ready"), 1)
            link(dve.tensor_copy(c1[:, :], bank[6][:, 0:1]))
            link(ts(n1[:, :], n1[:, :], c1[:, 0:1], None, ALU.add))
            mark(ts(end_idx[:, :], n1[:, :], -1.0, 0.0, ALU.add, ALU.max), "end_idx_ready")
            link(tt(n1[:, :], n1[:, :], n2[:, :], ALU.subtract))
            link(tt(n1[:, :], n1[:, :], dump_n[:, :], ALU.subtract))
            link(tt(n1[:, :], n1[:, :], has[:, :], ALU.mult))
            mark(tt(start_idx[:, :], n1[:, :], dump_n[:, :], ALU.add), "start_idx_ready")
            dve.wait_ge(sem("marks_turned"), 3)
            link(dve.tensor_copy(krow[:, :], bank[0][0:RW, 0:P]))
            link(dve.tensor_copy(penkrow[:, :], bank[1][0:RW, 0:P]))
            link(dve.tensor_copy(bkrow[:, :], bank[2][0:1, 0:P]))

            def fix_index():
                dve.wait_ge(sem("fix_end_fetched"), 16)
                link(dve.tensor_copy(c1[:, :], fix_end[:, :]))
                link(ts(c2[:, :], c1[:, :], plimit[:, 0:1], None, ALU.is_lt))
                link(tt(c2[:, :], c2[:, :], keep[:, 0:1], ALU.mult))
                link(tt(c1[:, :], c1[:, :], dump[:, :], ALU.subtract))
                link(tt(c1[:, :], c1[:, :], c2[:, :], ALU.mult))
                mark(tt(fix_idx[:, :], c1[:, :], dump[:, :], ALU.add), "fix_idx_ready")

            def norm_relu(k):
                link(dve.tensor_reduce(n1[:, :], x[:, :, :], AX.X, ALU.add))
                link(ts(n1[:, :], n1[:, :], -1.0 / F, None, ALU.mult))
                link(tt(h[:, :, :], x[:, :, :], over(n1[:, :]), ALU.add))
                link(tt(scratch, h[:, :, :], h[:, :, :], ALU.mult))
                link(dve.tensor_reduce(n1[:, :], scratch, AX.X, ALU.add))
                link(ts(n1[:, :], n1[:, :], 1.0 / F, EPS, ALU.mult, ALU.add))
                mark(dve.reciprocal(n2[:, :], n1[:, :]), "recip", k + 1)
                dve.wait_ge(sem("rstd"), k + 1)
                link(tt(h[:, :, :], h[:, :, :], over(n3[:, :]), ALU.mult))

            def carry_over(k, row, op0, op1, none):
                w = width[k]
                dve.wait_ge(sem("carry_turned"), 2 * k + 1)
                link(dve.tensor_copy(rowa[0:w, :], bank[6][0:w, 0:P]))
                link(scan(rowb[0:w, :], row[0:w, :], rowa[0:w, :], none, op0, op1))
                link(dve.memset(rowc[0:w, 0:1], none))
                mark(dve.tensor_copy(rowc[0:w, 1:P], rowb[0:w, 0:P - 1]), "carry_scanned", k + 1)
                dve.wait_ge(sem("carry_turned"), 2 * k + 2)
                dve.wait_ge(sem("fix_fetched"), 16 * (k + 1))
                mark(tt(fix[:, 0:w], fix[:, 0:w], bank[7][:, 0:w], op1), "fix_ready", k + 1)
                dve.wait_ge(sem("fetched"), 16 * NT * (k + 1))

            def segment_scan(k, w, b, c, marks, op0, op1, src):
                for part in range(2):
                    segment_part(k, w, b, c, marks, op0, op1, src, part)

            def segment_part(k, w, b, c, marks, op0, op1, src, part):
                o = orow(b, w)
                if k == 2 and part == 0:
                    dve.wait_ge(sem("combined2"), c + 1)
                for f in range(part * (w // 2), w if part else w // 2):
                    ins = scan(o[:, :, f], marks[:, cols(c)], src[:, :, f], carry[:, f:f + 1], op0, op1)
                if part == 1:
                    ins.then_inc(sem("scan_steps"), 1)
                    dve.wait_ge(sem("scan_steps"), NCH * k + c + 1)
                    dve.tensor_copy(carry[:, 0:w], o[:, JC - 1, :]).then_inc(sem("scanned"), 1)
                    dve.wait_ge(sem("scanned"), NCH * k + c + 1)

            def spread_rows(k, i, b, c, z):
                for part in range(4):
                    spread_part(k, i, b, c, z, part)

            def spread_part(k, i, b, c, z, part):
                src = dst_rows[:, :].rearrange("p (j w) -> p j w", w=F) if k == 2 else z[:, :, F:2 * F]
                to = (lambda f: f if f < 8 else ZV - 8 + f) if k == 2 else (lambda f: F + f)
                if part == 0:
                    if isinstance(c, int) and c == 0:
                        dve.wait_ge(sem("first"), 16 * (k + 1))
                    if k == 2:
                        dve.wait_ge(sem("dst_rows_loaded"), 16 * (c + 1))
                        after(dve, sem("split2"), NV * (c - 1))
                    else:
                        dve.wait_ge(sem(f"loaded{k}_{b}"), 32 * (i + 1))
                for f in range(8 * part, 8 * part + 8):
                    ins = scan(z[:, :, to(f)], keep[:, cols(c)], src[:, :, f], carry_in[:, f:f + 1],
                               ALU.mult, ALU.add)
                if part == 3:
                    ins.then_inc(sem(f"spread_steps{k}"), 1)
                    dve.wait_ge(sem(f"spread_steps{k}"), c + 1)
                    if k == 2:
                        dve.tensor_copy(carry_in[:, 0:8], z[:, JC - 1, 0:8])
                        last = dve.tensor_copy(carry_in[:, 8:F], z[:, JC - 1, ZV:ZA])
                    else:
                        last = dve.tensor_copy(carry_in[:, :], z[:, JC - 1, F:2 * F])
                    last.then_inc(sem(f"spread_done{k}"), 1)
                    dve.wait_ge(sem(f"spread_done{k}"), c + 1)

            def before_chunk(i, b, c, body):
                if b == 1:
                    body(i, 0, c - 1)
                elif not isinstance(i, int):
                    body(i - 1, 1, c - 1)

            dve.wait_ge(sem("x_loaded"), 16)
            norm_relu(0)
            mark(ts(h[:, :, :], h[:, :, :], 0.0, None, ALU.max), "table_ready", 1)
            fix_index()
            link(dve.memset(carry[:, :], -BIG))

            def max0(i, b, c):
                dve.wait_ge(sem("out_copied0"), NG * (c + 1))
                segment_scan(0, F, b, c, pen, ALU.add, ALU.max, orow(b, F))

            def body0(i, b, c):
                spread_rows(0, i, b, c, zrow(b, ZW))
                before_chunk(i, b, c, max0)
            chunks(dve, body0)
            max0(HALF - 1, 1, NCH - 1)
            carry_over(0, penkrow, ALU.add, ALU.max, -BIG)
            f0 = fetch[0]
            link(tt(f0, f0, along(b02[:, :]), ALU.add))
            link(tt(f0, f0, over(nohas[:, :]), ALU.add))
            link(tt(f0, f0, h[:, :, :], ALU.max))
            link(tt(x[:, :, :], x[:, :, :], f0, ALU.add))

            norm_relu(1)
            link(ts(h[:, :, :], h[:, :, :], 0.0, None, ALU.max))
            link(dve.tensor_copy(att3[:, :, 0:F], h[:, :, :]))
            temp = zin[:, :, :].rearrange("p b w -> p (b w)")[:, 0:NT * F].rearrange("p (t f) -> p t f", f=F)
            link(tt(temp, h[:, :, :], along(aw[:, 0:F]), ALU.mult))
            link(dve.tensor_reduce(att3[:, :, F], temp, AX.X, ALU.add))
            link(tt(temp, h[:, :, :], along(aw[:, F:2 * F]), ALU.mult))
            mark(dve.tensor_reduce(att3[:, :, F + 1], temp, AX.X, ALU.add), "table_ready", 2)
            dve.wait_ge(sem("score_copied"), NCH)
            dve.wait_ge(sem("spread1_loaded"), 16)
            dve.wait_ge(sem("first"), 32)
            link(scan(ea[:, 2], keep[:, :], ea[:, 1], fix[:, F + 1:F + 2], ALU.mult, ALU.add))
            link(tt(ea[:, 1], ea[:, 0], ea[:, 2], ALU.add))
            link(stt(ea[:, 0], ea[:, 1], LEAKY, ea[:, 1], ALU.mult, ALU.max))

            def running_max(out_, marks, row, turn, flip):
                r = (lambda a: a[:, ::-1]) if flip else (lambda a: a)
                last, dst, srcs, end = ((ea[:, out_, 0:1], slice(0, P - 1), slice(1, P), P - 1) if flip else
                                        (ea[:, out_, J - 1:J], slice(1, P), slice(0, P - 1), 0))
                link(scan(r(ea[:, out_]), r(marks), r(ea[:, 0]), -BIG, ALU.add, ALU.max))
                mark(dve.tensor_copy(c1[:, :], last), "max_end", turn + 1)
                dve.wait_ge(sem("max_turned"), 2 * turn + 1)
                link(dve.tensor_copy(rowa[0:1, :], bank[0][0:1, 0:P]))
                link(scan(r(rowb[0:1, :]), r(row), r(rowa[0:1, :]), -BIG, ALU.add, ALU.max))
                link(dve.memset(rowc[0:1, end:end + 1], -BIG))
                mark(dve.tensor_copy(rowc[0:1, dst], rowb[0:1, srcs]), "max_scanned", turn + 1)
                dve.wait_ge(sem("max_turned"), 2 * turn + 2)
                link(dve.tensor_copy(c2[:, :], bank[1][:, 0:1]))
                link(scan(r(ea[:, out_]), r(marks), r(ea[:, 0]), c2[:, 0:1], ALU.add, ALU.max))
            running_max(2, pen[:, :], penkrow[0:1, :], 0, False)
            running_max(3, ea[:, 5], bkrow[0:1, :], 1, True)
            link(tt(ea[:, 2], ea[:, 2], ea[:, 3], ALU.max))
            mark(tt(ea[:, 1], ea[:, 0], ea[:, 2], ALU.subtract), "logits")
            link(dve.memset(carry[:, :], 0.0))
            dve.wait_ge(sem("weights_ready"), 1)

            def body1(i, b, c):
                z, o = zrow(b, AW), orow(b, RW)
                dve.wait_ge(sem(f"loaded1_{b}"), 16 * (i + 1))
                if not isinstance(i, int):
                    dve.wait_ge(sem(f"stored{b}"), 16 * (HALF * 1 + i))
                tt(o[:, :, 0:F], z[:, :, 0:F], ea[:, 0, cols(c)].unsqueeze(2).broadcast_to([P, JC, F]), ALU.mult)
                ts(o[:, :, F], ea[:, 0, cols(c)], 1.0, None, ALU.mult).then_inc(sem("weighted"), 1)
                dve.wait_ge(sem("weighted"), c + 1)
                segment_scan(1, RW, b, c, keep, ALU.mult, ALU.add, o)
            chunks(dve, body1)
            carry_over(1, krow, ALU.mult, ALU.add, 0.0)
            f1 = fetch[1]
            link(ts(n2[:, :], has[:, :], -1.0, 1.0, ALU.mult, ALU.add))
            link(tt(n1[:, :], f1[:, :, F], has[:, :], ALU.mult))
            link(tt(n1[:, :], n1[:, :], n2[:, :], ALU.add))
            link(dve.reciprocal(n3[:, :], n1[:, :]))
            link(tt(n3[:, :], n3[:, :], has[:, :], ALU.mult))
            link(tt(f1[:, :, 0:F], f1[:, :, 0:F], over(n3[:, :]), ALU.mult))
            link(tt(x[:, :, :], x[:, :, :], f1[:, :, 0:F], ALU.add))

            vec = zin[:, :, :].rearrange("p b w -> p (b w)")[:, 0:3 * J].rearrange("p (j k) -> p j k", k=3)
            dve.wait_ge(sem("vec_loaded"), 32)
            link(tt(ea[:, 0], vec[:, :, 0], vec[:, :, 0], ALU.mult))
            link(tt(ea[:, 1], vec[:, :, 1], vec[:, :, 1], ALU.mult))
            link(tt(ea[:, 0], ea[:, 0], ea[:, 1], ALU.add))
            link(tt(ea[:, 1], vec[:, :, 2], vec[:, :, 2], ALU.mult))
            link(tt(ea[:, 0], ea[:, 0], ea[:, 1], ALU.add))
            mark(dve.reciprocal(ea[:, 4], ea[:, 0]), "norm2_ready")
            link(ts(ea[:, 3], ea[:, 3], TANH_GAIN, None, ALU.mult))
            dve.wait_ge(sem("rnorm_ready"), 1)
            link(tt(ea[:, 0], vec[:, :, 0], ea[:, 5], ALU.mult))
            link(tt(ea[:, 1], vec[:, :, 1], ea[:, 5], ALU.mult))
            link(tt(ea[:, 2], vec[:, :, 2], ea[:, 5], ALU.mult))
            link(dve.memset(zrow(0, ZW)[:, :, ZE:ZW], 0.0))
            mark(dve.memset(zrow(1, ZW)[:, :, ZE:ZW], 0.0), "vec_read")
            norm_relu(2)
            link(ts(scratch[:, :, 0:8], h[:, :, 0:8], 0.0, None, ALU.max))
            mark(ts(scratch[:, :, 8:F].rearrange("p t (k u) -> p t k u", k=3),
                    h[:, :, 8:F].rearrange("p t (u k) -> p t k u", k=3), 0.0, None, ALU.max), "table_ready", 3)
            link(dve.memset(carry[:, :], 0.0))

            def unit(k, c, n):
                return ea[:, k, cols(c)].unsqueeze(2).broadcast_to([P, JC, n])

            def combine2(i, b, c, part):
                e, o = eo[b], orow(b, F)
                v = qtemp[:, 0:JC * 24].rearrange("p (j w) -> p j w", w=24)
                if part == 0:
                    dve.wait_ge(sem("tanh2"), c + 1)
                    if not (isinstance(c, int) and c < 2):
                        dve.wait_ge(sem(f"stored{b}"), 16 * (HALF * 2 + i))
                    tt(e[:, :, 0:16], e[:, :, 0:16], unit(3, c, 16), ALU.mult)
                    for k in range(3):
                        ins = tt(v[:, :, 8 * k:8 * k + 8], e[:, :, 16:24], unit(k, c, 8), ALU.mult)
                    ins.then_inc(sem("combine_steps2"), 1)
                elif part == 1:
                    dve.wait_ge(sem("combine_steps2"), 2 * c + 1)
                    tt(v, v, e[:, :, 24:48], ALU.add).then_inc(sem("combine_steps2"), 1)
                else:
                    dve.wait_ge(sem("combine_steps2"), 2 * c + 2)
                    for k in range(3):
                        tt(o[:, :, 8 + k:F:3], v[:, :, 8 * k:8 * k + 8], e[:, :, 8:16], ALU.mult)
                    ts(o[:, :, 0:8], e[:, :, 0:8], 1.0, None, ALU.mult).then_inc(sem("combined2"), 1)

            def project(i, b, c, part):
                z = zrow(b, ZW)
                q = z[:, :, ZQ:ZS].rearrange("p j (h u) -> p j h u", h=2)
                temp = [qtemp[:, m * JC * 16:(m + 1) * JC * 16].rearrange("p (j h u) -> p j h u", h=2, u=8)
                        for m in range(2)]
                if part == 0:
                    dve.wait_ge(sem(f"gathered2_{b}"), 16 * JC * (i + 1))
                    dve.wait_ge(sem(f"loaded2_{b}"), 16 * (i + 1))
                    for k in range(3):
                        both = z[:, :, ZS + 8 * (k + 1):ZS + 8 * (k + 1) + 48].rearrange(
                            "p j (h w) -> p j h w", h=2)[:, :, :, 0:8]
                        ins = tt((q, *temp)[k], both,
                                 ea[:, k, cols(c)].unsqueeze(2).unsqueeze(3).broadcast_to([P, JC, 2, 8]), ALU.mult)
                    ins.then_inc(sem("q_steps2"), 1)
                elif part == 1:
                    dve.wait_ge(sem("q_steps2"), 2 * c + 1)
                    tt(q, q, temp[0], ALU.add).then_inc(sem("q_steps2"), 1)
                else:
                    dve.wait_ge(sem("q_steps2"), 2 * c + 2)
                    tt(q, q, temp[1], ALU.add).then_inc(sem("ready2"), 1)

            def split_rest(b, c, v):
                after(dve, sem("split2"), c * NV + v)
                dve.wait_ge(sem("split_high"), c * NV + v + 1)
                tt(rest, zrow(b, ZW)[:, v * V:(v + 1) * V, :].rearrange("p j (s f) -> p (j s) f", s=3),
                   parts[:, (b + v) % 2, :, 0, :], ALU.subtract).then_inc(sem("split_rest"), 1)

            def split_low(b, c, v):
                dve.wait_ge(sem("split_mid"), c * NV + v + 1)
                tt(parts[:, (b + v) % 2, :, 2, :], rest, parts[:, (b + v) % 2, :, 1, :],
                   ALU.subtract).then_inc(sem("split2"), 1)

            def product(n, j):
                dve.wait_ge(sem("column2"), n + 1)
                dve.wait_ge(sem("relu2"), n + 1)
                tt(prod[:, j].rearrange("p (a o k) -> p a o k", a=2, k=16),
                   y[:, j % 2, :, 0:NA].rearrange("p a (o k) -> p a o k", k=16),
                   hid[:, 0, 16 * j:16 * (j + 1)].unsqueeze(1).unsqueeze(1).broadcast_to([P, 2, 24, 16]), ALU.mult
                   ).then_inc(sem("product2"), 1)

            def sum_pair(n, b, g, q):
                dve.wait_ge(sem("product2"), n)
                dve.tensor_reduce(eo[b][:, G * g + 2 * q:G * g + 2 * q + 2, :].rearrange("p j w -> p (j w)"),
                                  prod[:, 2 * q:2 * q + 2].rearrange("p j (o k) -> p (j o) k", k=16),
                                  AX.X, ALU.add).then_inc(sem("summed2"), 1)

            def step2(i, b, c, s):
                last = isinstance(c, int) and c >= NCH - 1
                if at := behind(i, b, c, s, 1):
                    _, bb, cc, g = at
                    for q in range(2):
                        n = G * (cc * NG + g) + 2 * q
                        after(dve, sem("summed2"), n // 2 - 1 if isinstance(n, int) else
                              2 * (cc * NG + g) + q - 1)
                        product(n, 2 * q)
                        if not (isinstance(cc, int) and cc == 0 and g == 0 and q == 0):
                            pg = (bb, g, 0) if q else ((bb, g - 1, 1) if g else (1 - bb, NG - 1, 1))
                            sum_pair(n, *pg)
                        product(n + 1, 2 * q + 1)
                if not (isinstance(c, int) and (c == NCH or (c == NCH - 1 and s >= NG - 2))):
                    v = s // 2 + 1
                    nxt = (b, c, v) if v < NV else (1 - b, c + 1, 0)
                    (split_rest if s % 2 == 0 else split_low)(*nxt)
                nb, ni = 1 - b, (i if b == 0 else i + 1)
                if not last and s < 4:
                    spread_part(2, ni, nb, c + 1, zrow(nb, ZW), s)
                if 9 <= s < 12 and not last:
                    project(ni, nb, c + 1, s - 9)
                if not (isinstance(c, int) and c in (0, NCH)):
                    pi, pb = (i if b == 1 else i - 1), 1 - b
                    if 4 <= s < 7:
                        combine2(pi, pb, c - 1, s - 4)
                    if s in (7, 8):
                        segment_part(2, F, pb, c - 1, keep, ALU.mult, ALU.add, orow(pb, F), s - 7)
            for part in range(4):
                spread_part(2, 0, 0, 0, zrow(0, ZW), part)
            for part in range(3):
                project(0, 0, 0, part)
            split_rest(0, 0, 0)
            split_low(0, 0, 0)
            steps(dve, step2, 1)
            sum_pair(J, 1, NG - 1, 1)
            for part in range(3):
                combine2(HALF - 1, 1, NCH - 1, part)
            for part in range(2):
                segment_part(2, F, 1, NCH - 1, keep, ALU.mult, ALU.add, orow(1, F), part)
            carry_over(2, krow, ALU.mult, ALU.add, 0.0)
            link(tt(fetch[2], fetch[2], over(has[:, :]), ALU.mult))
            link(tt(x[:, :, :], x[:, :, :], fetch[2], ALU.add))

            norm_relu(3)
            link(ts(h[:, :, :], h[:, :, :], 0.0, None, ALU.max))
            dve.wait_ge(sem("dinv_ready"), 1)
            mark(tt(h[:, :, :], h[:, :, :], over(dinv[:, :]), ALU.mult), "table_ready", 4)

            def convolve(k):
                link(dve.memset(carry[:, :], 0.0))

                def body(i, b, c):
                    dve.wait_ge(sem(f"gathered{k}_{b}"), 16 * JC * (i + 1))
                    if not isinstance(i, int):
                        dve.wait_ge(sem(f"stored{b}"), 16 * (HALF * k + i))
                    segment_scan(k, F, b, c, keep, ALU.mult, ALU.add, zrow(b, F))
                chunks(dve, body)
                carry_over(k, krow, ALU.mult, ALU.add, 0.0)
                link(tt(fetch[k], fetch[k], over(has[:, :]), ALU.mult))
                link(tt(fetch[k], fetch[k], h[:, :, :], ALU.add))
            convolve(3)
            mark(tt(scratch, fetch[3], over(dinv[:, :]), ALU.mult), "update3")
            for g in range(NT // G):
                dve.wait_ge(sem("out3"), g + 1)
                tt(h[:, g * G:(g + 1) * G, :], bank[4 + g % 2][:, 0:G * F].rearrange("p (j w) -> p j w", w=F),
                   over(dinv[:, g * G:(g + 1) * G]), ALU.mult).then_inc(sem("out_copied3"), 1)
            dve.wait_ge(sem("out_copied3"), NT // G)
            convolve(4)
            f4 = fetch[4]
            link(tt(f4, f4, over(dinv[:, :]), ALU.mult))
            link(tt(f4, f4, along(b32[:, :]), ALU.add))
            link(ts(f4, f4, 0.0, None, ALU.max))
            mark(tt(x[:, :, :], x[:, :, :], f4, ALU.add), "x_final")


def kernel(**inputs):
    import concourse.bacc as bacc
    from concourse.bass_utils import run_bass_kernel_spmd

    a = {k: np.asarray(v) for k, v in inputs.items()}
    pad = EP - E

    def padded(v, value):
        return np.concatenate([v, np.full((pad,) + v.shape[1:], value, v.dtype)])

    arrays = {
        "x": a["x"],
        "src": padded(a["src"].astype(np.int32), 0).reshape(P, J),
        "dst": np.concatenate([np.full(1, -1, np.int32), padded(a["dst"].astype(np.int32), N),
                               np.full(1, -2, np.int32)]),
        "a32": padded(a["edge_attr_32"], 0.0),
        "a10": padded(a["edge_attr_10"], 0.0),
        "a3": padded(a["edge_attr_3"], 1.0),
        "wgt": padded(a["edge_weight"], 0.0),
        "w01": a["L0_gnn_W1"], "w02": a["L0_gnn_W2"], "b01": a["L0_gnn_b1"].reshape(64, 1),
        "b02": np.tile(a["L0_gnn_b2"].reshape(1, F), (P, 1)),
        "aw": np.tile(a["L1_gnn_attn_w"].reshape(1, 2 * F), (P, 1)),
        "w31": a["L3_gnn_W1"], "w32": a["L3_gnn_W2"], "b31": a["L3_gnn_b1"].reshape(64, 1),
        "b32": np.tile(a["L3_gnn_b2"].reshape(1, F), (P, 1)),
    }
    w2 = a["L2_gnn_W2"].reshape(16, 7, 16, 8).transpose(1, 2, 3, 0)
    set0 = np.zeros((32, 3, 8, 16), np.float32)
    s_of = (slice(24, 32), slice(0, 8))
    for half in range(2):
        u = slice(8 * half, 8 * half + 8)
        set0[s_of[half]] = w2[(0, 2, 4), u].transpose(1, 0, 2, 3)
        set0[8 + 8 * half:16 + 8 * half] = w2[(1, 3, 6), u].transpose(1, 0, 2, 3)

    def vector_sets(path, hidden):
        sets = np.zeros((2, 32, NB), np.float32)
        for k in range(3):
            o = slice(k * P, (k + 1) * P)
            sets[0, 8 * k:8 * k + 8, o] = w2[path, 0:8].reshape(8, P)
            to = sets[0, 24:32] if k == 0 else sets[1, 8 * (k - 1):8 * k]
            to[:, o] = w2[path, 8:16].reshape(8, P)
        if hidden:
            sets[1, 16:26, 3 * P:] = a["L2_gnn_W1"]
        return np.concatenate(list(sets), axis=1)
    arrays["w_f"] = np.tile(np.concatenate([set0.reshape(32, NA), vector_sets(5, True)], axis=1), (4, 1))
    arrays["w_sub"] = np.tile(vector_sets(6, False), (4, 1))
    rows32 = np.arange(P) % 32
    arrays["w121"] = np.where((rows32 >= 8) & (rows32 < 24), W121, 1.0).astype(np.float32)[:, None]
    r = np.arange(P)
    arrays["ident"] = np.eye(P, dtype=np.float32)
    arrays["before"] = (r[:, None] < r[None]).astype(np.float32)
    arrays["dump"] = (EP + r).astype(np.float32)[:, None]
    arrays["dump_n"] = (EP + np.arange(NPAD)).astype(np.float32).reshape(P, NT)
    arrays["plimit"] = ((r + 1) * J).astype(np.float32)[:, None]
    arrays["iota"] = np.tile(r.astype(np.float32)[None], (P, 1))
    arrays = {k: np.ascontiguousarray(v) for k, v in arrays.items()}

    nc = bacc.Bacc("TRN2", target_bir_lowering=False, num_devices=1)
    d = {k: nc.dram_tensor("in_" + k, v.shape, mybir.dt.from_np(v.dtype), kind="ExternalInput").ap()
         for k, v in arrays.items()}
    out = nc.dram_tensor("out", (N, F), F32, kind="ExternalOutput").ap()
    graph_kernel(nc, d, out)
    got = run_bass_kernel_spmd(nc, [{"in_" + k: v for k, v in arrays.items()}], core_ids=[0])
    return got.results[0]["out"]
```

```python
from contextlib import ExitStack

import numpy as np
import concourse.bass as bass
from concourse import mybir

P = 128
N, E, F = 12500, 200000, 32
NP_REAL = 125
NT = N // NP_REAL
NPAD = P * NT
JC = 56
NCH = 28
J = JC * NCH
EP = P * J
HALF = NCH // 2
G = 4
NG = JC // G
V = 2 * G
NV = JC // V
ZW = 96
ZQ, ZS, ZV, ZA = 8, 24, 56, 80
ZE = 90
NA = 3 * P
NB = 3 * P + 16
WN = NA + 2 * NB
AW = 34
RW = 34
TAKES = 5
HC = 14
BIG = 1.0e38
EPS = 1e-5
TANH_GAIN = 1.593
PW_S, PW_V = 0.17677669529663687, 0.25
W121 = 1.5 ** 0.5
ALPHA = 2.0 ** 0.5 / 10.0 ** 0.5 / 4.0
LEAKY = 0.01

ALU = mybir.AluOpType
ACT = mybir.ActivationFunctionType
AX = mybir.AxisListType
F32 = mybir.dt.float32
I32 = mybir.dt.int32
BF16 = mybir.dt.bfloat16


def after(eng, sem, value):
    if isinstance(value, int) and value <= 0:
        return
    eng.wait_ge(sem, value)


def graph_kernel(nc, d, out):
    with ExitStack() as ctx:
        def sb(name, shape, dt=F32):
            return ctx.enter_context(nc.sbuf_tensor(name, shape, dt))

        sems = {}

        def sem(name):
            if name not in sems:
                sems[name] = ctx.enter_context(nc.semaphore(name))
            return sems[name]

        def dram(name, shape, dt=F32):
            return nc.dram_tensor(name, shape, dt).ap()

        spread = dram("spread", (EP + NPAD, F))
        spread1 = dram("spread1", (EP + NPAD, 1))
        end_table = dram("end_table", (NPAD, 1), I32)
        table = {0: dram("table0", (NPAD, F)), 1: dram("table1", (NPAD, AW)),
                 2: dram("table2", (NPAD, F)), 3: dram("table3", (NPAD, F)),
                 4: dram("table4", (NPAD, F))}
        width = {0: F, 1: RW, 2: F, 3: F, 4: F}
        rows = {k: dram(f"rows{k}", (EP + P, width[k])) for k in width}

        x = sb("x", [P, NT, F])
        prod_f = sb("prod", [P, NT * F + J + 2 * P + NT])
        prod = prod_f[:, 0:4 * 768].rearrange("p (b w) -> p b w", b=4)
        h = prod_f[:, 0:NT * F].rearrange("p (t f) -> p t f", f=F)
        zero = prod_f[:, NT * F:NT * F + J]
        fetched = sb("fetched", [P, NT * RW])
        hot = fetched[:, 0:HC * (P + NT)].bitcast(BF16).rearrange("p (k w) -> p k w", w=P + NT)
        att = sb("att", [P, NT * AW])
        zin = sb("zin", [P, 2, JC * ZW])
        zout = sb("zout", [P, 2, JC * RW])
        keep = sb("keep", [P, J])
        pen = sb("pen", [P, J])
        ea = sb("ea", [P, 6, J])
        dst0 = sb("dst0", [P, 1], I32)
        idx = sb("idx", [P, 2, JC], I32)
        start_idx = sb("start_idx", [P, NT], I32)
        end_idx = sb("end_idx", [P, NT], I32)
        fix_idx = sb("fix_idx", [P, 1], I32)
        fix_end = sb("fix_end", [P, 1], I32)
        has = sb("has", [P, NT])
        nohas = sb("nohas", [P, NT])
        dinv = sb("dinv", [P, NT])
        n1 = sb("n1", [P, NT])
        n2 = sb("n2", [P, NT])
        n3 = sb("n3", [P, NT])
        c1 = sb("c1", [P, 1])
        c2 = sb("c2", [P, 1])
        c3 = sb("c3", [P, 1])
        krow = sb("krow", [RW, P])
        penkrow = sb("penkrow", [RW, P])
        kcols = sb("kcols", [P, RW])
        rowa = sb("rowa", [RW, P])
        rowb = sb("rowb", [RW, P])
        rowc = sb("rowc", [RW, P])
        rowm = sb("rowm", [RW, P])
        decays = sb("decays", [RW, 2, P])
        fix_scale = sb("fix_scale", [P, 2])
        carry_in = sb("carry_in", [P, F])
        carry = sb("carry", [P, RW])
        fix = sb("fix", [P, AW])
        ident = sb("ident", [P, P])
        once = prod_f[:, NT * F + J:]
        before = once[:, 0:P]
        dump = sb("dump", [P, 1])
        dump_n = once[:, 2 * P:2 * P + NT]
        plimit = sb("plimit", [P, 1])
        iota_f = once[:, P:2 * P]
        iota_b = sb("iota_b", [P, P], BF16)
        w01 = sb("w01", [3 * F, 64])
        w02 = sb("w02", [64, F])
        b01 = sb("b01", [64, 1])
        b02 = sb("b02", [P, F])
        aw = sb("aw", [P, 2 * F])
        w31 = sb("w31", [F, 64])
        w32 = sb("w32", [64, F])
        b31 = sb("b31", [64, 1])
        b32 = sb("b32", [P, F])
        wz = [sb(f"wz{q}", [P, WN], BF16) for q in range(2)]
        ident_b = sb("ident_b", [P, P], BF16)
        tz = sb("tz", [P, 2, 768])
        hid = sb("hid", [P, 2, 512])
        dst_rows = sb("dst_rows", [P, JC * F])
        qtemp = sb("qtemp", [P, 2 * JC * 16])
        scales = qtemp[:, 0:4 * JC].rearrange("p (b a j) -> p b a j", b=2, a=2)
        peak = ea[:, 3:5, :].rearrange("p a j -> p (a j)")[:, 0:J + 1]
        tz_b = tz[:, :, :].rearrange("p b w -> p (b w)").bitcast(BF16).rearrange(
            "p (b j s e) -> p b j s e", b=2, j=G, s=3)
        parts = ea[:, 4:6, :].rearrange("p a j -> p (a j)")[:, 0:2 * V * 192].bitcast(BF16).rearrange(
            "p (b j k f) -> p b j k f", b=2, j=3 * V, k=4)
        rest = pen[:, 0:V * ZW].rearrange("p (j f) -> p j f", f=32)
        places = ea[:, 3, :].bitcast(BF16).rearrange("p (a j) -> p a j", a=2)
        w_f, w_sub = prod_f[:, 0:WN], prod_f[:, WN:WN + 2 * NB]
        w_rest = prod_f[:, WN + 2 * NB:2 * WN + 2 * NB]
        w121 = prod_f[:, 2 * WN + 2 * NB:2 * WN + 2 * NB + 1]
        eo = [t[:, 0:JC * 48].rearrange("p (j w) -> p j w", w=48) for t in (att, fetched)]

        psum = ctx.enter_context(nc.psum_tensor("psum", [P, 8 * 512], F32))
        bank = [psum[:, 512 * i:512 * (i + 1)] for i in range(8)]
        turned01 = bank[0].bitcast(BF16).rearrange("p (j w) -> p j w", j=G)
        turned2 = bank[1].bitcast(BF16)[:, 0:G * P].rearrange("p (j w) -> p j w", j=G)
        y = psum[:, 2 * 512:8 * 512].rearrange("p (j a w) -> p j a w", j=3, a=2)
        place = (0, 1, 0, 2)

        def zrow(b, w):
            return zin[:, b, 0:JC * w].rearrange("p (j w) -> p j w", w=w)

        def orow(b, w):
            return zout[:, b, 0:JC * w].rearrange("p (j w) -> p j w", w=w)

        def orow_flat(b, w):
            return zout[:, b, 0:JC * w]

        def hold(eng, semaphore, value):
            after(eng, semaphore, value)
            if not isinstance(value, int):
                eng.sem_inc(sem("gate"))

        def steps(eng, step, lags):
            for b in range(2):
                for s in range(NG):
                    step(0, b, b, s)
            with eng.Fori(1, HALF - 1) as i:
                for b in range(2):
                    for s in range(NG):
                        step(i, b, 2 * i + b, s)
            for b in range(2):
                for s in range(NG):
                    step(HALF - 1, b, NCH - 2 + b, s)
            for s in range(lags):
                step(HALF, 0, NCH, s)

        def behind(i, b, c, s, lag):
            if s >= lag:
                return None if isinstance(c, int) and c == NCH else (i, b, c, s - lag)
            if isinstance(c, int) and c == 0:
                return None
            return (i if b == 1 else i - 1, 1 - b, c - 1, s - lag + NG)

        def next_split(b, c, s):
            if isinstance(c, int) and (c == NCH or (c == NCH - 1 and s >= NG - 2)):
                return None
            v = s // 2 + 1
            return (b, c, v) if v < NV else (1 - b, c + 1, 0)

        def chunks(eng, body):
            for b in range(2):
                body(0, b, b)
            with eng.Fori(1, HALF) as i:
                for b in range(2):
                    body(i, b, 2 * i + b)

        def cols(c):
            return slice(c * JC, (c + 1) * JC) if isinstance(c, int) else bass.ds(c * JC, JC)

        consts = [(w01[:, :], d["w01"]), (w02[:, :], d["w02"]), (b01[:, :], d["b01"]), (b02[:, :], d["b02"]),
                  (aw[:, :], d["aw"]), (w31[:, :], d["w31"]), (w32[:, :], d["w32"]), (b31[:, :], d["b31"]),
                  (b32[:, :], d["b32"]), (w_f, d["w_f"]), (w_sub, d["w_sub"]), (w121, d["w121"]),
                  (ident[:, :], d["ident"]), (before, d["before"]), (dump[:, :], d["dump"]), (dump_n, d["dump_n"]),
                  (plimit[:, :], d["plimit"]), (iota_f, d["iota"])]
        fetch = {k: fetched[:, 0:NT * width[k]].rearrange("p (t w) -> p t w", w=width[k])
                 for k in width}
        att3 = att[:, :].rearrange("p (t w) -> p t w", w=AW)
        scratch = att[:, 0:NT * F].rearrange("p (t w) -> p t w", w=F)
        dst_i, prev_i = fetched[:, 0:J].bitcast(I32), fetched[:, J:2 * J].bitcast(I32)

        block = ctx.enter_context(nc.Block())

        @block.sync
        def _(sp):
            for dst, src in ((dst_i, d["dst"][1:1 + EP]), (prev_i, d["dst"][0:EP])):
                sp.dma_start(dst, src.rearrange("(p j) -> p j", j=J)).then_inc(sem("dst_loaded"), 16)
            sp.wait_ge(sem("x_cleared"), 1)
            sp.dma_start(x[0:NP_REAL], d["x"].rearrange("(p t) f -> p t f", t=NT)
                         ).then_inc(sem("x_loaded"), 16)
            for dst, src in consts:
                sp.dma_start(dst, src).then_inc(sem("consts_loaded"), 16)
            sp.wait_ge(sem("zero_ready"), 1)
            sp.dma_start(spread1[0:EP].rearrange("(p j) w -> p (j w)", j=J), zero[:, :]
                         ).then_inc(sem("filled"), 16)
            for k in range(F):
                sp.dma_start(spread[0:EP].rearrange("(p c j) w -> p c (j w)", p=P, c=F)[:, k], zero[:, :]
                             ).then_inc(sem("filled"), 16)
            for k in width:
                sp.dma_start(rows[k][EP:EP + P], zero[:, 0:width[k]]).then_inc(sem("filled"), 16)
            sp.wait_ge(sem("table_ready"), 1)
            sp.dma_start(table[0].rearrange("(p t) w -> p (t w)", t=NT), h[:, :, :].rearrange("p t f -> p (t f)")
                         ).then_inc(sem("table_stored"), 16)
            for b in range(2):
                sp.dma_start(idx[:, b], d["src"][:, cols(b)]).then_inc(sem(f"idx_loaded{b}"), 16)
            sp.wait_ge(sem("end_idx_ready"), 1)
            sp.dma_start(end_table.rearrange("(p t) w -> p (t w)", t=NT), end_idx[:, :]
                         ).then_inc(sem("end_table_stored"), 16)

            def store_table(k, tile):
                if k == 4:
                    sp.wait_ge(sem("out_copied3"), NT // G)
                else:
                    sp.wait_ge(sem("table_ready"), k + 1)
                sp.dma_start(table[k].rearrange("(p t) w -> p (t w)", t=NT), tile
                             ).then_inc(sem("table_stored"), 16)

            def load_idx(k, b, c):
                sp.dma_start(idx[:, b], d["src"][:, cols(c)]).then_inc(sem(f"idx_loaded{b}"), 16)

            def store_rows(k, i, b, c):
                hold(sp, sem("scanned"), NCH * k + c + 1)
                sp.dma_start(rows[k][0:EP].rearrange("(p j) w -> p (j w)", j=J)[
                    :, wcols(c, width[k])], orow_flat(b, width[k])).then_inc(sem(f"stored{b}"), 16)

            def wcols(c, w):
                return slice(c * JC * w, (c + 1) * JC * w) if isinstance(c, int) else bass.ds(c * JC * w, JC * w)

            def later_store(k, i, b, c):
                if b == 1:
                    store_rows(k, i, 0, c - 1)
                elif not isinstance(i, int):
                    store_rows(k, i - 1, 1, c - 1)

            def spread_rows(b, c):
                return spread[0:EP].rearrange("(p j) w -> p j w", j=J)[:, cols(c), :]

            def body0(i, b, c):
                hold(sp, sem("transposed0"), NG * (c - 1))
                if not isinstance(i, int):
                    load_idx(0, b, c)
                sp.dma_start(zrow(b, ZW)[:, :, 2 * F:3 * F],
                             d["a32"].rearrange("(p j) w -> p j w", j=J)[:, cols(c), :]
                             ).then_inc(sem(f"loaded0_{b}"), 16)
                if isinstance(i, int) and b == 0:
                    sp.wait_ge(sem("spread"), 16 * NT * 1)
                sp.dma_start(zrow(b, ZW)[:, :, F:2 * F], spread_rows(b, c)
                             ).then_inc(sem(f"loaded0_{b}"), 16)
                later_store(0, i, b, c)
            chunks(sp, body0)
            store_rows(0, HALF - 1, 1, NCH - 1)

            store_table(1, att[:, :])

            def body1(i, b, c):
                hold(sp, sem("weighted"), c - 1)
                load_idx(1, b, c)
                if isinstance(i, int) and b == 0:
                    sp.wait_ge(sem("spread"), 16 * NT * 2)
                    sp.wait_ge(sem("table_ready"), 2)
                    sp.dma_start(ea[:, 1], spread1[0:EP].rearrange("(p j) w -> p (j w)", j=J)
                                 ).then_inc(sem("spread1_loaded"), 16)
                later_store(1, i, b, c)
            chunks(sp, body1)
            store_rows(1, HALF - 1, 1, NCH - 1)

            sp.wait_ge(sem("scanned"), 2 * NCH)
            sp.dma_start(zin[:, :, :].rearrange("p b w -> p (b w)")[:, 0:3 * J],
                         d["a3"].rearrange("(p j) w -> p (j w)", j=J)).then_inc(sem("vec_loaded"), 16)
            sp.dma_start(ea[:, 3], d["wgt"].rearrange("(p j) -> p j", j=J)).then_inc(sem("vec_loaded"), 16)
            store_table(2, att[:, 0:NT * F])
            sp.wait_ge(sem("vec_read"), 1)

            def body2(i, b, c):
                hold(sp, sem("spread_done2"), c)
                if isinstance(i, int) and b == 0:
                    sp.wait_ge(sem("spread"), 16 * NT * 3)
                sp.dma_start(dst_rows[:, :].rearrange("p (j w) -> p j w", w=F), spread_rows(b, c)
                             ).then_inc(sem("dst_rows_loaded"), 16)
                hold(sp, sem("split2"), NV * (c - 1))
                load_idx(2, b, c)
                sp.dma_start(zrow(b, ZW)[:, :, ZA:ZE],
                             d["a10"].rearrange("(p j) w -> p j w", j=J)[:, cols(c), :]
                             ).then_inc(sem(f"loaded2_{b}"), 16)
                if not isinstance(i, int):
                    store_rows(2, i - 1, b, c - 2)
            chunks(sp, body2)
            store_rows(2, HALF - 1, 0, NCH - 2)
            store_rows(2, HALF - 1, 1, NCH - 1)

            for k in (3, 4):
                store_table(k, h[:, :, :].rearrange("p t f -> p (t f)"))

                def body3(i, b, c):
                    hold(sp, sem("scanned"), NCH * k + c - 1)
                    load_idx(k, b, c)
                    later_store(k, i, b, c)
                chunks(sp, body3)
                store_rows(k, HALF - 1, 1, NCH - 1)

            sp.wait_ge(sem("x_final"), 1)
            sp.dma_start(out.rearrange("(p t) f -> p t f", t=NT), x[0:NP_REAL]).then_inc(sem("out_stored"), 16)
            sp.wait_ge(sem("out_stored"), 16)

        @block.gpsimd
        def _(pool):
            def take(dst, src, index):
                return pool.indirect_dma_start(out=dst, out_offset=None, in_=src,
                                               in_offset=bass.IndirectOffsetOnAxis(ap=index, axis=0))

            def put(dst, index, src):
                return pool.indirect_dma_start(out=dst, out_offset=bass.IndirectOffsetOnAxis(ap=index, axis=0),
                                               in_=src, in_offset=None)

            def gather(k, w, row_width, between=None):
                pool.wait_ge(sem("table_stored"), 16 * (k + 1))

                def body(i, b, c):
                    hold(pool, sem(f"idx_loaded{b}"), 16 * (HALF * k + i + 1))
                    for j in range(JC):
                        take(zrow(b, row_width)[:, j, 0:w], table[k], idx[:, b, j:j + 1]
                             ).then_inc(sem(f"gathered{k}_{b}"), 16)
                for b in range(2):
                    body(0, b, b)
                if between:
                    between()
                with pool.Fori(1, HALF) as i:
                    for b in range(2):
                        body(i, b, 2 * i + b)

            def fix_and_fetch(k):
                w = width[k]
                for b in range(2):
                    pool.wait_ge(sem(f"stored{b}"), 16 * HALF * (k + 1))
                take(fix[:, 0:w], rows[k], fix_idx[:, 0:1]).then_inc(sem("fix_fetched"), 16)
                pool.wait_ge(sem("fix_ready"), k + 1)
                put(rows[k], fix_idx[:, 0:1], fix[:, 0:w]).then_inc(sem("fix_stored"), 16)
                pool.wait_ge(sem("fix_stored"), 16 * (k + 1))
                for t in range(NT):
                    take(fetch[k][:, t, :], rows[k], end_idx[:, t:t + 1]).then_inc(sem("fetched"), 16)

            def spread_nodes(k, tile, where, first, w):
                pool.wait_ge(sem("table_ready"), k + 1)
                for t in range(NT):
                    put(where, start_idx[:, t:t + 1], tile(t)).then_inc(sem("spread"), 16)
                pool.wait_ge(sem("table_stored"), 16 * (k + 1))
                take(first, table[k], dst0[:, 0:1]).then_inc(sem("first"), 16)

            def place_nodes():
                pool.wait_ge(sem("start_idx_ready"), 1)
                pool.wait_ge(sem("filled"), 16 * (1 + F + len(width)))
                pool.wait_ge(sem("end_table_stored"), 16)
                pool.wait_ge(sem("dst0_ready"), 1)
                take(fix_end[:, :], end_table, dst0[:, 0:1]).then_inc(sem("fix_end_fetched"), 16)
                spread_nodes(0, lambda t: h[:, t, :], spread, carry_in[:, :], F)
            gather(0, F, ZW, place_nodes)
            pool.wait_ge(sem("fix_idx_ready"), 1)
            fix_and_fetch(0)
            spread_nodes(1, lambda t: att3[:, t, F + 1:F + 2], spread1, fix[:, 0:AW], 1)
            gather(1, AW, AW)
            fix_and_fetch(1)
            spread_nodes(2, lambda t: scratch[:, t, :], spread, carry_in[:, :], F)
            pool.wait_ge(sem("vec_read"), 1)
            pool.wait_ge(sem("table_stored"), 16 * 3)

            def take_rows(i, b, c, first, last):
                if first == 0:
                    hold(pool, sem(f"idx_loaded{b}"), 16 * (HALF * 2 + i + 1))
                for j in range(first, min(last, JC)):
                    take(zrow(b, ZW)[:, j, ZS:ZS + F], table[2], idx[:, b, j:j + 1]
                         ).then_inc(sem(f"gathered2_{b}"), 16)

            def split_rest(b, c, v):
                hold(pool, sem("split2"), c * NV + v)
                hold(pool, sem("split_high"), c * NV + v + 1)
                pool.tensor_tensor(rest, zrow(b, ZW)[:, v * V:(v + 1) * V, :].rearrange(
                    "p j (s f) -> p (j s) f", s=3), parts[:, (b + v) % 2, :, 0, :], ALU.subtract
                    ).then_inc(sem("split_rest"), 1)

            def split_low(b, c, v):
                hold(pool, sem("split_mid"), c * NV + v + 1)
                pool.tensor_tensor(parts[:, (b + v) % 2, :, 2, :], rest, parts[:, (b + v) % 2, :, 1, :],
                                   ALU.subtract).then_inc(sem("split2"), 1)

            def step2(i, b, c, s):
                if s < -(-JC // TAKES) and not (isinstance(c, int) and c >= NCH - 1):
                    take_rows(i if b == 0 else i + 1, 1 - b, c + 1, TAKES * s, TAKES * (s + 1))
                if nxt := next_split(b, c, s):
                    (split_rest if s % 2 == 0 else split_low)(*nxt)
            take_rows(0, 0, 0, 0, JC)
            split_rest(0, 0, 0)
            split_low(0, 0, 0)
            steps(pool, step2, 0)
            fix_and_fetch(2)
            for k in (3, 4):
                gather(k, F, F)
                fix_and_fetch(k)

        @block.scalar
        def _(act):
            def copy(dst, src):
                return act.activation(dst, src, ACT.Copy)

            def root(k):
                act.wait_ge(sem("recip"), k + 1)
                act.activation(n3[:, :], n2[:, :], ACT.Sqrt).then_inc(sem("rstd"), 1)

            root(0)
            act.wait_ge(sem("deg_recip"), 1)
            act.activation(dinv[:, :], dinv[:, :], ACT.Sqrt).then_inc(sem("dinv_ready"), 1)
            act.wait_ge(sem("consts_loaded"), 16 * len(consts))

            def body0(i, b, c):
                for s in range(NG + 2):
                    n = c * NG + s
                    if s < NG:
                        act.wait_ge(sem("transposed0"), n + 1)
                        after(act, sem("hidden0"), n - 1)
                        copy(tz[0:ZW, s % 2, 0:512], bank[s % 2][0:ZW, :]).then_inc(sem("transposed_copied0"), 1)
                    if 1 <= s <= NG:
                        m, g = n - 1, s - 1
                        act.wait_ge(sem("hidden0"), m + 1)
                        after(act, sem("out0"), m - 1)
                        act.activation(hid[0:64, g % 2, :], bank[2 + g % 2][0:64, :], ACT.Relu,
                                       bias=b01[:, 0:1]).then_inc(sem("relu0"), 1)
                    if s >= 2:
                        m, g = n - 2, s - 2
                        act.wait_ge(sem("out0"), m + 1)
                        if g == 0:
                            after(act, sem("scanned"), c - 1)
                            if not isinstance(i, int):
                                act.wait_ge(sem(f"stored{b}"), 16 * (HALF * 0 + i))
                        copy(orow(b, F)[:, g * G:(g + 1) * G, :],
                             bank[4 + g % 2][:, 0:G * F].rearrange("p (j w) -> p j w", w=F)
                             ).then_inc(sem("out_copied0"), 1)
            chunks(act, body0)

            root(1)

            def body1(i, b, c):
                act.wait_ge(sem("logits"), c + 1)
                act.activation(scales[:, b], scales[:, b], ACT.Exp).then_inc(sem("weights_ready"), 1)
            chunks(act, body1)
            act.wait_ge(sem("row_logits"), 1)
            act.activation(decays[:, :, :], decays[:, :, :], ACT.Exp).then_inc(sem("decays_ready"), 1)
            act.wait_ge(sem("fix_logits"), 1)
            act.activation(fix_scale[:, :], fix_scale[:, :], ACT.Exp).then_inc(sem("fix_scale_ready"), 1)

            act.wait_ge(sem("norm2_ready"), 1)
            act.activation(ea[:, 5], ea[:, 4], ACT.Sqrt).then_inc(sem("rnorm_ready"), 1)
            root(2)

            def split_high(b, c, v):
                if v == 0:
                    act.wait_ge(sem("ready2"), c + 1)
                after(act, sem("transposed2"), 2 * (c * NV + v) - 2)
                z = zrow(b, ZW)[:, v * V:(v + 1) * V, :].rearrange("p j (s f) -> p (j s) f", s=3)
                copy(parts[:, (b + v) % 2, :, 0:4:3, :],
                     z.unsqueeze(2).broadcast_to([P, 3 * V, 2, 32])).then_inc(sem("split_high"), 1)

            def split_mid(b, c, v):
                act.wait_ge(sem("split_rest"), c * NV + v + 1)
                copy(parts[:, (b + v) % 2, :, 1, :], rest).then_inc(sem("split_mid"), 1)

            def step2(i, b, c, s):
                at = behind(i, b, c, s, 1)
                if at:
                    relu2(at, 0)
                    relu2(at, 1)
                if behind(i, b, c, s, 0):
                    n = c * NG + s
                    act.wait_ge(sem("transposed2"), n + 1)
                    after(act, sem("column2"), G * (n - 1))
                    copy(tz_b[:, s % 2, :, 0:2, :].rearrange("p j s e -> p j (s e)"), turned01)
                    copy(tz_b[:, s % 2, :, 2, :], turned2).then_inc(sem("transposed_copied2"), 1)
                if at:
                    relu2(at, 2)
                nxt = next_split(b, c, s)
                if nxt and s % 2 == 0:
                    split_high(*nxt)
                elif nxt:
                    split_mid(*nxt)
                if at:
                    relu2(at, 3)
                    _, _, cc, g = at
                    n = cc * NG + g
                    act.wait_ge(sem("relu2"), G * n + 4)
                    after(act, sem("summed2"), 2 * n)
                    act.wait_ge(sem("column2"), G * n + 4)
                    by_hidden = [t.rearrange("p a (o k) -> p a o k", k=16) for t in
                                 (prod[:, 3].rearrange("p (a o) -> p a o", a=2), y[:, place[3], :, 0:NA])]
                    for k in range(16):
                        ins = act.activation(by_hidden[0][:, :, :, k], by_hidden[1][:, :, :, k], ACT.Copy,
                                             scale=hid[:, 0, 48 + k:49 + k])
                    ins.then_inc(sem("act_product2"), 1)
                if s == 2 and not (isinstance(c, int) and c in (0, NCH)):
                    tanh2(1 - b, c - 1)

            def relu2(at, j):
                _, _, cc, g = at
                act.wait_ge(sem("hidden2"), G * (cc * NG + g) + j + 1)
                act.activation(hid[:, 0, 16 * j:16 * (j + 1)], y[:, place[j], 1, 3 * P:NB], ACT.Relu
                               ).then_inc(sem("relu2"), 1)

            def tanh2(b, c):
                act.wait_ge(sem("summed2"), JC // 2 * (c + 1))
                act.activation(eo[b][:, :, 0:16], eo[b][:, :, 0:16], ACT.Tanh).then_inc(sem("tanh2"), 1)
            split_high(0, 0, 0)
            split_mid(0, 0, 0)
            steps(act, step2, 1)
            tanh2(1, NCH - 1)

            root(3)

            for s in range(NT // G + 1):
                if s < NT // G:
                    act.wait_ge(sem("transposed3"), s + 1)
                    after(act, sem("hidden3"), s - 1)
                    copy(tz[0:F, s % 2, 0:512], bank[s % 2][0:F, :]).then_inc(sem("transposed_copied3"), 1)
                if s >= 1:
                    g = s - 1
                    act.wait_ge(sem("hidden3"), g + 1)
                    after(act, sem("out3"), g - 1)
                    act.activation(hid[0:64, g % 2, :], bank[2 + g % 2][0:64, :], ACT.Relu,
                                   bias=b31[:, 0:1]).then_inc(sem("relu3"), 1)

        @block.tensor
        def _(pe):
            pe.wait_ge(sem("consts_loaded"), 16 * len(consts))

            def hist(i, b):
                hh = 2 * i + b
                pe.wait_ge(sem("hot"), hh + 1)
                for k in range(HC):
                    first = isinstance(i, int) and b == 0 and k == 0
                    ins = pe.matmul(bank[7][:, 0:NT], hot[:, b * HC + k, 0:P], hot[:, b * HC + k, P:P + NT],
                                    start=first, stop=False, skip_group_check=True)
                ins.then_inc(sem("hot_used"), 1)
            for b in range(2):
                hist(0, b)
            with pe.Fori(1, J // (2 * HC)) as i:
                for b in range(2):
                    hist(i, b)
            pe.wait_ge(sem("deg_scanned"), 1)
            pe.matmul(bank[6][:, 0:1], before[:, :], n1[:, NT - 1:NT], start=True, stop=True
                      ).then_inc(sem("base_ready"), 1)
            for m, (src, w) in enumerate(((kcols[:, 0:RW], RW), (fix[:, 0:RW], RW))):
                pe.wait_ge(sem("marks_ready"), m + 1)
                pe.transpose(bank[m][0:w, 0:P], src, ident[:, :]).then_inc(sem("marks_turned"), 1)

            def turn_carry(k):
                w = width[k]
                pe.wait_ge(sem("scanned"), NCH * (k + 1))
                pe.transpose(bank[6][0:w, 0:P], carry[:, 0:w], ident[:, :]).then_inc(sem("carry_turned"), 1)
                pe.wait_ge(sem("carry_scanned"), k + 1)
                pe.transpose(bank[7][:, 0:w], rowc[0:w, :], ident[0:w, 0:w]).then_inc(sem("carry_turned"), 1)

            def body0(i, b, c):
                for s in range(NG + 2):
                    n = c * NG + s
                    if s < NG:
                        if s == 0:
                            pe.wait_ge(sem(f"gathered0_{b}"), 16 * JC * (i + 1))
                            pe.wait_ge(sem(f"loaded0_{b}"), 32 * (i + 1))
                            pe.wait_ge(sem("spread_done0"), c + 1)
                        after(pe, sem("transposed_copied0"), n - 1)
                        for j in range(G):
                            ins = pe.transpose(bank[s % 2][0:ZW, j * P:(j + 1) * P],
                                               zrow(b, ZW)[:, s * G + j, :], ident[:, :])
                        ins.then_inc(sem("transposed0"), 1)
                    if 1 <= s <= NG:
                        m, g = n - 1, s - 1
                        pe.wait_ge(sem("transposed_copied0"), m + 1)
                        after(pe, sem("relu0"), m - 1)
                        pe.matmul(bank[2 + g % 2][0:64, :], w01[:, :], tz[0:ZW, g % 2, 0:512],
                                  start=True, stop=True).then_inc(sem("hidden0"), 1)
                    if s >= 2:
                        m, g = n - 2, s - 2
                        pe.wait_ge(sem("relu0"), m + 1)
                        after(pe, sem("out_copied0"), m - 1)
                        for j in range(G):
                            ins = pe.matmul(bank[4 + g % 2][:, j * F:(j + 1) * F],
                                            hid[0:64, g % 2, j * P:(j + 1) * P], w02[:, :],
                                            start=True, stop=True)
                        ins.then_inc(sem("out0"), 1)
            chunks(pe, body0)
            turn_carry(0)
            pe.wait_ge(sem("max_end"), 1)
            pe.transpose(bank[5][0:RW, 0:P], kcols[:, :], ident[:, :]).then_inc(sem("max_turned"), 1)
            turn_carry(1)
            pe.transpose(bank[4][:, 0:RW], rowb[:, :], ident[0:RW, 0:RW]).then_inc(sem("max_turned"), 1)

            def step2(i, b, c, s):
                at = behind(i, b, c, s, 1)
                if at:
                    columns(at, 0)
                if behind(i, b, c, s, 0):
                    n = c * NG + s
                    if s % 2 == 0:
                        pe.wait_ge(sem("split2"), c * NV + s // 2 + 1)
                    after(pe, sem("transposed_copied2"), n)
                    for j in range(G):
                        for q in range(3):
                            to = turned01[:, j, q * P:(q + 1) * P] if q < 2 else turned2[:, j]
                            ins = pe.transpose(to, parts[:, (b + s // 2) % 2, 3 * ((s % 2) * G + j) + q].rearrange(
                                "p k f -> p (k f)"), ident_b[:, :])
                    ins.then_inc(sem("transposed2"), 1)
                if at:
                    columns(at, 1)

            def columns(at, half):
                _, _, cc, g = at
                m = cc * NG + g
                if half == 0:
                    pe.wait_ge(sem("transposed_copied2"), m + 1)
                for j in range(2 * half, 2 * half + 2):
                    if j == 3:
                        after(pe, sem("act_product2"), m)
                    else:
                        after(pe, sem("product2"), 3 * m + (0, -1, 1)[j])
                    rows_ = [tz_b[:, g % 2, j, q] for q in range(3)]
                    for r in range(2):
                        for q in range(2):
                            ins = pe.matmul(y[:, place[j], 1, 0:NB], rows_[1 + r],
                                            wz[q][:, NA + r * NB:NA + (r + 1) * NB],
                                            start=(r == 0 and q == 0), stop=(r == 1 and q == 1))
                    ins.then_inc(sem("hidden2"), 1)
                    for q in range(2):
                        ins = pe.matmul(y[:, place[j], 0, 0:NA], rows_[0], wz[q][:, 0:NA],
                                        start=(q == 0), stop=(q == 1))
                    ins.then_inc(sem("column2"), 1)
            pe.wait_ge(sem("weights2_ready"), 1)
            steps(pe, step2, 1)
            turn_carry(2)
            turn_carry(3)

            groups = NT // G
            pe.wait_ge(sem("update3"), 1)
            for s in range(groups + 2):
                if s < groups:
                    after(pe, sem("transposed_copied3"), s - 1)
                    for j in range(G):
                        ins = pe.transpose(bank[s % 2][0:F, j * P:(j + 1) * P], scratch[:, s * G + j, :],
                                           ident[:, :])
                    ins.then_inc(sem("transposed3"), 1)
                if 1 <= s <= groups:
                    g = s - 1
                    pe.wait_ge(sem("transposed_copied3"), g + 1)
                    after(pe, sem("relu3"), g - 1)
                    pe.matmul(bank[2 + g % 2][0:64, :], w31[:, :], tz[0:F, g % 2, 0:512], start=True, stop=True
                              ).then_inc(sem("hidden3"), 1)
                if s >= 2:
                    g = s - 2
                    pe.wait_ge(sem("relu3"), g + 1)
                    after(pe, sem("out_copied3"), g - 1)
                    for j in range(G):
                        ins = pe.matmul(bank[4 + g % 2][:, j * F:(j + 1) * F], hid[0:64, g % 2, j * P:(j + 1) * P],
                                        w32[:, :], start=True, stop=True)
                    ins.then_inc(sem("out3"), 1)
            turn_carry(4)

        @block.vector
        def _(dve):
            order = [0]

            def link(ins):
                order[0] += 1
                ins.then_inc(sem("dve_order"), 1)
                dve.wait_ge(sem("dve_order"), order[0])

            def mark(ins, name, value=1):
                ins.then_inc(sem(name), 1)
                dve.wait_ge(sem(name), value)

            def over(t, w=F):
                return t.unsqueeze(2).broadcast_to([P, t.shape[1], w])

            def along(t, n=NT):
                return t.unsqueeze(1).broadcast_to([P, n, t.shape[1]])

            tt, ts, stt = dve.tensor_tensor, dve.tensor_scalar, dve.scalar_tensor_tensor
            scan = dve.tensor_tensor_scan

            mark(dve.memset(x[:, :, :], 0.0), "x_cleared")
            mark(dve.memset(zero[:, :], 0.0), "zero_ready")

            dve.wait_ge(sem("dst_loaded"), 32)
            mark(dve.tensor_copy(dst0[:, :], dst_i[:, 0:1]), "dst0_ready")
            link(tt(keep[:, :], dst_i, prev_i, ALU.is_equal))
            link(ts(pen[:, :], keep[:, :], -1.0, BIG, ALU.add, ALU.mult))
            link(dve.tensor_copy(ea[:, 0], dst_i))
            link(ts(prev_i, ea[:, 0], 1.0 / NT, None, ALU.mult))
            link(dve.tensor_copy(ea[:, 1], prev_i))
            link(stt(ea[:, 2], ea[:, 1], -float(NT), ea[:, 0], ALU.mult, ALU.add))
            link(ts(ea[:, 3], ea[:, 2], 0.0, None, ALU.is_lt))
            link(tt(ea[:, 1], ea[:, 1], ea[:, 3], ALU.subtract))
            link(stt(ea[:, 2], ea[:, 3], float(NT), ea[:, 2], ALU.mult, ALU.add))
            link(ts(ea[:, 3], ea[:, 2], float(NT), None, ALU.is_ge))
            link(tt(ea[:, 1], ea[:, 1], ea[:, 3], ALU.add))
            link(stt(ea[:, 2], ea[:, 3], -float(NT), ea[:, 2], ALU.mult, ALU.add))
            link(dve.tensor_reduce(c2[:, :], keep[:, :], AX.X, ALU.min))
            mark(ts(kcols[:, :], zero[:, 0:RW], c2[:, 0:1], None, ALU.add), "marks_ready", 1)
            mark(ts(fix[:, 0:RW], kcols[:, :], -1.0, BIG, ALU.add, ALU.mult), "marks_ready", 2)

            dve.wait_ge(sem("consts_loaded"), 16 * len(consts))
            link(dve.tensor_copy(ident_b[:, :], ident[:, :]))
            link(ts(w_f[:, 0:2 * P], w_f[:, 0:2 * P], ALPHA * PW_S, None, ALU.mult))
            link(ts(w_f[:, 2 * P:NA], w_f[:, 2 * P:NA], ALPHA * PW_V, None, ALU.mult))
            link(ts(w_f[:, 2 * P:NA], w_f[:, 2 * P:NA], w121, None, ALU.mult))
            link(ts(w_sub, w_sub, -ALPHA * PW_V * W121 / 3.0, None, ALU.mult))
            for r in range(2):
                v = w_f[:, NA + r * NB:NA + r * NB + 3 * P]
                link(stt(v, v, ALPHA * PW_V / 3.0 ** 0.5, w_sub[:, r * NB:r * NB + 3 * P], ALU.mult, ALU.add))
            link(dve.tensor_copy(wz[0][:, :], w_f))
            link(tt(w_rest, w_f, wz[0][:, :], ALU.subtract))
            link(dve.tensor_copy(wz[1][:, :], w_rest))
            link(tt(w_rest, w_rest, wz[1][:, :], ALU.subtract))
            link(dve.tensor_copy(wz[0][ZW:P, :], w_rest[ZW:P, :]))
            mark(dve.memset(wz[1][ZW:P, :], 0.0), "weights2_ready")
            link(dve.tensor_copy(iota_b[:, :], iota_f[:, :]))
            for which in range(2):
                link(dve.tensor_copy(places[:, which], ea[:, 1 + which]))

            def norm_relu(k):
                link(dve.tensor_reduce(n1[:, :], x[:, :, :], AX.X, ALU.add))
                link(ts(n1[:, :], n1[:, :], -1.0 / F, None, ALU.mult))
                link(tt(h[:, :, :], x[:, :, :], over(n1[:, :]), ALU.add))
                link(tt(scratch, h[:, :, :], h[:, :, :], ALU.mult))
                link(dve.tensor_reduce(n1[:, :], scratch, AX.X, ALU.add))
                link(ts(n1[:, :], n1[:, :], 1.0 / F, EPS, ALU.mult, ALU.add))
                mark(dve.reciprocal(n2[:, :], n1[:, :]), "recip", k + 1)
                dve.wait_ge(sem("rstd"), k + 1)
                link(tt(h[:, :, :], h[:, :, :], over(n3[:, :]), ALU.mult))

            dve.wait_ge(sem("x_loaded"), 16)
            norm_relu(0)
            mark(ts(h[:, :, :], h[:, :, :], 0.0, None, ALU.max), "table_ready", 1)

            def hist(i, b):
                hh = 2 * i + b
                after(dve, sem("hot_used"), hh - 1)
                at = slice(hh * HC, (hh + 1) * HC) if isinstance(hh, int) else bass.ds(hh * HC, HC)
                for w, o, which in ((P, 0, 0), (NT, P, 1)):
                    ins = tt(hot[:, b * HC:(b + 1) * HC, o:o + w],
                             iota_b[:, 0:w].unsqueeze(1).broadcast_to([P, HC, w]),
                             places[:, which, at].unsqueeze(2).broadcast_to([P, HC, w]), ALU.is_equal)
                ins.then_inc(sem("hot"), 1)
            for b in range(2):
                hist(0, b)
            with dve.Fori(1, J // (2 * HC)) as i:
                for b in range(2):
                    hist(i, b)

            dve.wait_ge(sem("hot_used"), J // HC)
            link(dve.tensor_copy(n2[:, :], bank[7][:, 0:NT]))
            link(ts(has[:, :], n2[:, :], 0.0, None, ALU.is_gt))
            link(ts(nohas[:, :], has[:, :], -1.0, BIG, ALU.add, ALU.mult))
            link(ts(n3[:, :], n2[:, :], 1.0, None, ALU.add))
            mark(dve.reciprocal(dinv[:, :], n3[:, :]), "deg_recip")
            link(ts(n3[:, :], n2[:, :], 0.0, 1.0, ALU.mult, ALU.add))
            mark(scan(n1[:, :], n3[:, :], n2[:, :], 0.0, ALU.mult, ALU.add), "deg_scanned")
            dve.wait_ge(sem("base_ready"), 1)
            link(dve.tensor_copy(c1[:, :], bank[6][:, 0:1]))
            link(ts(n1[:, :], n1[:, :], c1[:, 0:1], None, ALU.add))
            mark(ts(end_idx[:, :], n1[:, :], -1.0, 0.0, ALU.add, ALU.max), "end_idx_ready")
            link(tt(n1[:, :], n1[:, :], n2[:, :], ALU.subtract))
            link(tt(n1[:, :], n1[:, :], dump_n[:, :], ALU.subtract))
            link(tt(n1[:, :], n1[:, :], has[:, :], ALU.mult))
            mark(tt(start_idx[:, :], n1[:, :], dump_n[:, :], ALU.add), "start_idx_ready")
            dve.wait_ge(sem("marks_turned"), 2)
            link(dve.tensor_copy(krow[:, :], bank[0][0:RW, 0:P]))
            link(dve.tensor_copy(penkrow[:, :], bank[1][0:RW, 0:P]))

            def fix_index():
                dve.wait_ge(sem("fix_end_fetched"), 16)
                link(dve.tensor_copy(c1[:, :], fix_end[:, :]))
                link(ts(c2[:, :], c1[:, :], plimit[:, 0:1], None, ALU.is_lt))
                link(tt(c2[:, :], c2[:, :], keep[:, 0:1], ALU.mult))
                link(tt(c1[:, :], c1[:, :], dump[:, :], ALU.subtract))
                link(tt(c1[:, :], c1[:, :], c2[:, :], ALU.mult))
                mark(tt(fix_idx[:, :], c1[:, :], dump[:, :], ALU.add), "fix_idx_ready")

            def carry_over(k, row, op0, op1, none):
                w = width[k]
                dve.wait_ge(sem("carry_turned"), 2 * k + 1)
                link(dve.tensor_copy(rowa[0:w, :], bank[6][0:w, 0:P]))
                link(scan(rowb[0:w, :], row[0:w, :], rowa[0:w, :], none, op0, op1))
                link(dve.memset(rowc[0:w, 0:1], none))
                mark(dve.tensor_copy(rowc[0:w, 1:P], rowb[0:w, 0:P - 1]), "carry_scanned", k + 1)
                dve.wait_ge(sem("carry_turned"), 2 * k + 2)
                dve.wait_ge(sem("fix_fetched"), 16 * (k + 1))
                mark(tt(fix[:, 0:w], fix[:, 0:w], bank[7][:, 0:w], op1), "fix_ready", k + 1)
                dve.wait_ge(sem("fetched"), 16 * NT * (k + 1))

            def segment_scan(k, w, b, c, marks, op0, op1, src):
                for part in range(2):
                    segment_part(k, w, b, c, marks, op0, op1, src, part)

            def segment_part(k, w, b, c, marks, op0, op1, src, part):
                o = orow(b, w)
                if k == 2 and part == 0:
                    dve.wait_ge(sem("combined2"), c + 1)
                for f in range(part * (w // 2), w if part else w // 2):
                    ins = scan(o[:, :, f], marks[:, cols(c)], src[:, :, f], carry[:, f:f + 1], op0, op1)
                if part == 1:
                    ins.then_inc(sem("scan_steps"), 1)
                    dve.wait_ge(sem("scan_steps"), NCH * k + c + 1)
                    dve.tensor_copy(carry[:, 0:w], o[:, JC - 1, :]).then_inc(sem("scanned"), 1)
                    dve.wait_ge(sem("scanned"), NCH * k + c + 1)

            def spread_rows(k, i, b, c, z):
                for part in range(4):
                    spread_part(k, i, b, c, z, part)

            def spread_part(k, i, b, c, z, part):
                src = dst_rows[:, :].rearrange("p (j w) -> p j w", w=F) if k == 2 else z[:, :, F:2 * F]
                to = (lambda f: f if f < 8 else ZV - 8 + f) if k == 2 else (lambda f: F + f)
                if part == 0:
                    if isinstance(c, int) and c == 0:
                        dve.wait_ge(sem("first"), 16 * (k + 1))
                    if k == 2:
                        dve.wait_ge(sem("dst_rows_loaded"), 16 * (c + 1))
                        after(dve, sem("split2"), NV * (c - 1))
                    else:
                        dve.wait_ge(sem(f"loaded{k}_{b}"), 32 * (i + 1))
                for f in range(8 * part, 8 * part + 8):
                    ins = scan(z[:, :, to(f)], keep[:, cols(c)], src[:, :, f], carry_in[:, f:f + 1],
                               ALU.mult, ALU.add)
                if part == 3:
                    ins.then_inc(sem(f"spread_steps{k}"), 1)
                    dve.wait_ge(sem(f"spread_steps{k}"), c + 1)
                    if k == 2:
                        dve.tensor_copy(carry_in[:, 0:8], z[:, JC - 1, 0:8])
                        last = dve.tensor_copy(carry_in[:, 8:F], z[:, JC - 1, ZV:ZA])
                    else:
                        last = dve.tensor_copy(carry_in[:, :], z[:, JC - 1, F:2 * F])
                    last.then_inc(sem(f"spread_done{k}"), 1)
                    dve.wait_ge(sem(f"spread_done{k}"), c + 1)

            def before_chunk(i, b, c, body):
                if b == 1:
                    body(i, 0, c - 1)
                elif not isinstance(i, int):
                    body(i - 1, 1, c - 1)

            fix_index()
            link(dve.memset(carry[:, :], -BIG))

            def max0(i, b, c):
                dve.wait_ge(sem("out_copied0"), NG * (c + 1))
                segment_scan(0, F, b, c, pen, ALU.add, ALU.max, orow(b, F))

            def body0(i, b, c):
                spread_rows(0, i, b, c, zrow(b, ZW))
                before_chunk(i, b, c, max0)
            chunks(dve, body0)
            max0(HALF - 1, 1, NCH - 1)
            carry_over(0, penkrow, ALU.add, ALU.max, -BIG)
            f0 = fetch[0]
            link(tt(f0, f0, along(b02[:, :]), ALU.add))
            link(tt(f0, f0, over(nohas[:, :]), ALU.add))
            link(tt(f0, f0, h[:, :, :], ALU.max))
            link(tt(x[:, :, :], x[:, :, :], f0, ALU.add))

            norm_relu(1)
            link(ts(h[:, :, :], h[:, :, :], 0.0, None, ALU.max))
            link(dve.tensor_copy(att3[:, :, 0:F], h[:, :, :]))
            temp = zin[:, :, :].rearrange("p b w -> p (b w)")[:, 0:NT * F].rearrange("p (t f) -> p t f", f=F)
            link(tt(temp, h[:, :, :], along(aw[:, 0:F]), ALU.mult))
            link(dve.tensor_reduce(att3[:, :, F], temp, AX.X, ALU.add))
            link(tt(temp, h[:, :, :], along(aw[:, F:2 * F]), ALU.mult))
            mark(dve.tensor_reduce(att3[:, :, F + 1], temp, AX.X, ALU.add), "table_ready", 2)
            dve.wait_ge(sem("spread1_loaded"), 16)
            dve.wait_ge(sem("first"), 32)
            link(scan(ea[:, 2], keep[:, :], ea[:, 1], fix[:, F + 1:F + 2], ALU.mult, ALU.add))
            link(dve.memset(carry[:, :], 0.0))
            link(dve.memset(peak[:, 0:1], -BIG))

            def body1(i, b, c):
                z, o, logit = zrow(b, AW), orow(b, RW), ea[:, 0, cols(c)]
                before_, after_ = peak[:, cols(c)], peak[:, slice(c * JC + 1, (c + 1) * JC + 1)
                                                         if isinstance(c, int) else bass.ds(c * JC + 1, JC)]
                first = peak[:, slice(c * JC, c * JC + 1) if isinstance(c, int) else bass.ds(c * JC, 1)]
                weight, decay = scales[:, b, 0], scales[:, b, 1]

                def step(ins, n):
                    ins.then_inc(sem("logit_steps"), 1)
                    dve.wait_ge(sem("logit_steps"), 4 * c + n)
                dve.wait_ge(sem(f"gathered1_{b}"), 16 * JC * (i + 1))
                step(tt(logit, z[:, :, F], ea[:, 2, cols(c)], ALU.add), 1)
                step(stt(logit, logit, LEAKY, logit, ALU.mult, ALU.max), 2)
                step(scan(after_, pen[:, cols(c)], logit, first, ALU.add, ALU.max), 3)
                tt(weight, logit, after_, ALU.subtract)
                step(tt(decay, before_, after_, ALU.subtract), 4)
                tt(decay, decay, pen[:, cols(c)], ALU.add).then_inc(sem("logits"), 1)
                if not isinstance(i, int):
                    dve.wait_ge(sem(f"stored{b}"), 16 * (HALF * 1 + i))
                dve.wait_ge(sem("weights_ready"), c + 1)
                ts(o[:, :, F], weight, 1.0, None, ALU.mult)
                ts(o[:, :, F + 1], after_, 1.0, None, ALU.mult)
                tt(o[:, :, 0:F], z[:, :, 0:F], weight.unsqueeze(2).broadcast_to([P, JC, F]), ALU.mult
                   ).then_inc(sem("weighted"), 1)
                dve.wait_ge(sem("weighted"), c + 1)
                for f in range(F + 1):
                    ins = scan(o[:, :, f], decay, o[:, :, f], carry[:, f:f + 1], ALU.mult, ALU.add)
                ins.then_inc(sem("scan_steps"), 1)
                dve.wait_ge(sem("scan_steps"), NCH + c + 1)
                dve.tensor_copy(carry[:, 0:F + 1], o[:, JC - 1, 0:F + 1]).then_inc(sem("scanned"), 1)
                dve.wait_ge(sem("scanned"), NCH + c + 1)
            chunks(dve, body1)

            mark(ts(kcols[:, :], zero[:, 0:RW], peak[:, J:J + 1], None, ALU.add), "max_end")
            dve.wait_ge(sem("max_turned"), 1)
            link(dve.tensor_copy(rowb[:, :], bank[5][0:RW, 0:P]))
            link(scan(rowm[:, :], penkrow[:, :], rowb[:, :], -BIG, ALU.add, ALU.max))
            link(tt(decays[:, 0, :], rowb[:, :], rowm[:, :], ALU.subtract))
            link(dve.memset(decays[:, 1, 0:1], -BIG))
            link(tt(decays[:, 1, 1:P], rowm[:, 0:P - 1], rowm[:, 1:P], ALU.subtract))
            mark(tt(decays[:, 1, 1:P], decays[:, 1, 1:P], penkrow[:, 1:P], ALU.add), "row_logits")
            link(dve.memset(rowb[:, 0:1], -BIG))
            link(dve.tensor_copy(rowb[:, 1:P], rowm[:, 0:P - 1]))
            link(dve.memset(rowc[:, 0:1], 0.0))
            dve.wait_ge(sem("carry_turned"), 3)
            link(dve.tensor_copy(rowa[:, :], bank[6][0:RW, 0:P]))
            dve.wait_ge(sem("decays_ready"), 1)
            link(tt(rowa[:, :], rowa[:, :], decays[:, 0, :], ALU.mult))
            link(scan(rowm[:, :], decays[:, 1, :], rowa[:, :], 0.0, ALU.mult, ALU.add))
            mark(dve.tensor_copy(rowc[:, 1:P], rowm[:, 0:P - 1]), "carry_scanned", 2)
            dve.wait_ge(sem("carry_turned"), 4)
            dve.wait_ge(sem("max_turned"), 2)
            dve.wait_ge(sem("fix_fetched"), 32)
            link(dve.tensor_copy(c1[:, :], bank[4][:, 0:1]))
            link(tt(c2[:, :], c1[:, :], fix[:, F + 1:F + 2], ALU.max))
            link(tt(fix_scale[:, 0:1], c1[:, :], c2[:, :], ALU.subtract))
            mark(tt(fix_scale[:, 1:2], fix[:, F + 1:F + 2], c2[:, :], ALU.subtract), "fix_logits")
            dve.wait_ge(sem("fix_scale_ready"), 1)
            link(ts(fix[:, 0:F + 1], fix[:, 0:F + 1], fix_scale[:, 1:2], None, ALU.mult))
            mark(stt(fix[:, 0:F + 1], bank[7][:, 0:F + 1], fix_scale[:, 0:1], fix[:, 0:F + 1], ALU.mult, ALU.add),
                 "fix_ready", 2)
            dve.wait_ge(sem("fetched"), 16 * NT * 2)
            f1 = fetch[1]
            link(ts(n2[:, :], has[:, :], -1.0, 1.0, ALU.mult, ALU.add))
            link(tt(n1[:, :], f1[:, :, F], has[:, :], ALU.mult))
            link(tt(n1[:, :], n1[:, :], n2[:, :], ALU.add))
            link(dve.reciprocal(n3[:, :], n1[:, :]))
            link(tt(n3[:, :], n3[:, :], has[:, :], ALU.mult))
            link(tt(f1[:, :, 0:F], f1[:, :, 0:F], over(n3[:, :]), ALU.mult))
            link(tt(x[:, :, :], x[:, :, :], f1[:, :, 0:F], ALU.add))

            vec = zin[:, :, :].rearrange("p b w -> p (b w)")[:, 0:3 * J].rearrange("p (j k) -> p j k", k=3)
            dve.wait_ge(sem("vec_loaded"), 32)
            link(tt(ea[:, 0], vec[:, :, 0], vec[:, :, 0], ALU.mult))
            link(tt(ea[:, 1], vec[:, :, 1], vec[:, :, 1], ALU.mult))
            link(tt(ea[:, 0], ea[:, 0], ea[:, 1], ALU.add))
            link(tt(ea[:, 1], vec[:, :, 2], vec[:, :, 2], ALU.mult))
            link(tt(ea[:, 0], ea[:, 0], ea[:, 1], ALU.add))
            mark(dve.reciprocal(ea[:, 4], ea[:, 0]), "norm2_ready")
            link(ts(ea[:, 3], ea[:, 3], TANH_GAIN, None, ALU.mult))
            dve.wait_ge(sem("rnorm_ready"), 1)
            link(tt(ea[:, 0], vec[:, :, 0], ea[:, 5], ALU.mult))
            link(tt(ea[:, 1], vec[:, :, 1], ea[:, 5], ALU.mult))
            link(tt(ea[:, 2], vec[:, :, 2], ea[:, 5], ALU.mult))
            link(dve.memset(zrow(0, ZW)[:, :, ZE:ZW], 0.0))
            mark(dve.memset(zrow(1, ZW)[:, :, ZE:ZW], 0.0), "vec_read")
            norm_relu(2)
            link(ts(scratch[:, :, 0:8], h[:, :, 0:8], 0.0, None, ALU.max))
            mark(ts(scratch[:, :, 8:F].rearrange("p t (k u) -> p t k u", k=3),
                    h[:, :, 8:F].rearrange("p t (u k) -> p t k u", k=3), 0.0, None, ALU.max), "table_ready", 3)
            link(dve.memset(carry[:, :], 0.0))

            def unit(k, c, n):
                return ea[:, k, cols(c)].unsqueeze(2).broadcast_to([P, JC, n])

            def combine2(i, b, c, part):
                e, o = eo[b], orow(b, F)
                v = qtemp[:, 0:JC * 24].rearrange("p (j w) -> p j w", w=24)
                if part == 0:
                    dve.wait_ge(sem("tanh2"), c + 1)
                    if not (isinstance(c, int) and c < 2):
                        dve.wait_ge(sem(f"stored{b}"), 16 * (HALF * 2 + i))
                    tt(e[:, :, 0:16], e[:, :, 0:16], unit(3, c, 16), ALU.mult)
                    for k in range(3):
                        ins = tt(v[:, :, 8 * k:8 * k + 8], e[:, :, 16:24], unit(k, c, 8), ALU.mult)
                    ins.then_inc(sem("combine_steps2"), 1)
                elif part == 1:
                    dve.wait_ge(sem("combine_steps2"), 2 * c + 1)
                    tt(v, v, e[:, :, 24:48], ALU.add).then_inc(sem("combine_steps2"), 1)
                else:
                    dve.wait_ge(sem("combine_steps2"), 2 * c + 2)
                    for k in range(3):
                        tt(o[:, :, 8 + k:F:3], v[:, :, 8 * k:8 * k + 8], e[:, :, 8:16], ALU.mult)
                    ts(o[:, :, 0:8], e[:, :, 0:8], 1.0, None, ALU.mult).then_inc(sem("combined2"), 1)

            def project(i, b, c, part):
                z = zrow(b, ZW)
                q = z[:, :, ZQ:ZS].rearrange("p j (h u) -> p j h u", h=2)
                temp = [qtemp[:, m * JC * 16:(m + 1) * JC * 16].rearrange("p (j h u) -> p j h u", h=2, u=8)
                        for m in range(2)]
                if part == 0:
                    dve.wait_ge(sem(f"gathered2_{b}"), 16 * JC * (i + 1))
                    dve.wait_ge(sem(f"loaded2_{b}"), 16 * (i + 1))
                    for k in range(3):
                        both = z[:, :, ZS + 8 * (k + 1):ZS + 8 * (k + 1) + 48].rearrange(
                            "p j (h w) -> p j h w", h=2)[:, :, :, 0:8]
                        ins = tt((q, *temp)[k], both,
                                 ea[:, k, cols(c)].unsqueeze(2).unsqueeze(3).broadcast_to([P, JC, 2, 8]), ALU.mult)
                    ins.then_inc(sem("q_steps2"), 1)
                elif part == 1:
                    dve.wait_ge(sem("q_steps2"), 2 * c + 1)
                    tt(q, q, temp[0], ALU.add).then_inc(sem("q_steps2"), 1)
                else:
                    dve.wait_ge(sem("q_steps2"), 2 * c + 2)
                    tt(q, q, temp[1], ALU.add).then_inc(sem("ready2"), 1)

            def product(n, j):
                dve.wait_ge(sem("column2"), G * n + j + 1)
                dve.wait_ge(sem("relu2"), G * n + j + 1)
                tt(prod[:, j].rearrange("p (a o k) -> p a o k", a=2, k=16),
                   y[:, place[j], :, 0:NA].rearrange("p a (o k) -> p a o k", k=16),
                   hid[:, 0, 16 * j:16 * (j + 1)].unsqueeze(1).unsqueeze(1).broadcast_to([P, 2, 24, 16]), ALU.mult
                   ).then_inc(sem("product2"), 1)

            def sum_pair(n, b, g, q):
                dve.wait_ge(sem("product2"), 3 * n + 2 + q)
                if q:
                    dve.wait_ge(sem("act_product2"), n + 1)
                dve.tensor_reduce(eo[b][:, G * g + 2 * q:G * g + 2 * q + 2, :].rearrange("p j w -> p (j w)"),
                                  prod[:, 2 * q:2 * q + 2].rearrange("p j (o k) -> p (j o) k", k=16),
                                  AX.X, ALU.add).then_inc(sem("summed2"), 1)

            def step2(i, b, c, s):
                last = isinstance(c, int) and c >= NCH - 1
                if at := behind(i, b, c, s, 1):
                    _, bb, cc, g = at
                    n = cc * NG + g
                    after(dve, sem("summed2"), 2 * n - 1)
                    product(n, 0)
                    if not (isinstance(cc, int) and cc == 0 and g == 0):
                        sum_pair(n - 1, bb if g else 1 - bb, (g - 1) % NG, 1)
                    product(n, 1)
                    after(dve, sem("summed2"), 2 * n)
                    product(n, 2)
                    sum_pair(n, bb, g, 0)
                nb, ni = 1 - b, (i if b == 0 else i + 1)
                if not last and s < 4:
                    spread_part(2, ni, nb, c + 1, zrow(nb, ZW), s)
                if s == 11 and not last:
                    for part in range(3):
                        project(ni, nb, c + 1, part)
                if not (isinstance(c, int) and c in (0, NCH)):
                    pi, pb = (i if b == 1 else i - 1), 1 - b
                    if 4 <= s < 7:
                        combine2(pi, pb, c - 1, s - 4)
                    if s in (7, 8):
                        segment_part(2, F, pb, c - 1, keep, ALU.mult, ALU.add, orow(pb, F), s - 7)
            for part in range(4):
                spread_part(2, 0, 0, 0, zrow(0, ZW), part)
            for part in range(3):
                project(0, 0, 0, part)
            steps(dve, step2, 1)
            sum_pair(NCH * NG - 1, 1, NG - 1, 1)
            for part in range(3):
                combine2(HALF - 1, 1, NCH - 1, part)
            for part in range(2):
                segment_part(2, F, 1, NCH - 1, keep, ALU.mult, ALU.add, orow(1, F), part)
            carry_over(2, krow, ALU.mult, ALU.add, 0.0)
            link(tt(fetch[2], fetch[2], over(has[:, :]), ALU.mult))
            link(tt(x[:, :, :], x[:, :, :], fetch[2], ALU.add))

            norm_relu(3)
            link(ts(h[:, :, :], h[:, :, :], 0.0, None, ALU.max))
            dve.wait_ge(sem("dinv_ready"), 1)
            mark(tt(h[:, :, :], h[:, :, :], over(dinv[:, :]), ALU.mult), "table_ready", 4)

            def convolve(k):
                link(dve.memset(carry[:, :], 0.0))

                def body(i, b, c):
                    dve.wait_ge(sem(f"gathered{k}_{b}"), 16 * JC * (i + 1))
                    if not isinstance(i, int):
                        dve.wait_ge(sem(f"stored{b}"), 16 * (HALF * k + i))
                    segment_scan(k, F, b, c, keep, ALU.mult, ALU.add, zrow(b, F))
                chunks(dve, body)
                carry_over(k, krow, ALU.mult, ALU.add, 0.0)
                link(tt(fetch[k], fetch[k], over(has[:, :]), ALU.mult))
                link(tt(fetch[k], fetch[k], h[:, :, :], ALU.add))
            convolve(3)
            mark(tt(scratch, fetch[3], over(dinv[:, :]), ALU.mult), "update3")
            for g in range(NT // G):
                dve.wait_ge(sem("out3"), g + 1)
                tt(h[:, g * G:(g + 1) * G, :], bank[4 + g % 2][:, 0:G * F].rearrange("p (j w) -> p j w", w=F),
                   over(dinv[:, g * G:(g + 1) * G]), ALU.mult).then_inc(sem("out_copied3"), 1)
            dve.wait_ge(sem("out_copied3"), NT // G)
            convolve(4)
            f4 = fetch[4]
            link(tt(f4, f4, over(dinv[:, :]), ALU.mult))
            link(tt(f4, f4, along(b32[:, :]), ALU.add))
            link(ts(f4, f4, 0.0, None, ALU.max))
            mark(tt(x[:, :, :], x[:, :, :], f4, ALU.add), "x_final")


def kernel(**inputs):
    import concourse.bacc as bacc
    from concourse.bass_utils import run_bass_kernel_spmd

    a = {k: np.asarray(v) for k, v in inputs.items()}
    pad = EP - E

    def padded(v, value):
        return np.concatenate([v, np.full((pad,) + v.shape[1:], value, v.dtype)])

    arrays = {
        "x": a["x"],
        "src": padded(a["src"].astype(np.int32), 0).reshape(P, J),
        "dst": np.concatenate([np.full(1, -1, np.int32), padded(a["dst"].astype(np.int32), N),
                               np.full(1, -2, np.int32)]),
        "a32": padded(a["edge_attr_32"], 0.0),
        "a10": padded(a["edge_attr_10"], 0.0),
        "a3": padded(a["edge_attr_3"], 1.0),
        "wgt": padded(a["edge_weight"], 0.0),
        "w01": a["L0_gnn_W1"], "w02": a["L0_gnn_W2"], "b01": a["L0_gnn_b1"].reshape(64, 1),
        "b02": np.tile(a["L0_gnn_b2"].reshape(1, F), (P, 1)),
        "aw": np.tile(a["L1_gnn_attn_w"].reshape(1, 2 * F), (P, 1)),
        "w31": a["L3_gnn_W1"], "w32": a["L3_gnn_W2"], "b31": a["L3_gnn_b1"].reshape(64, 1),
        "b32": np.tile(a["L3_gnn_b2"].reshape(1, F), (P, 1)),
    }
    w2 = a["L2_gnn_W2"].reshape(16, 7, 16, 8).transpose(1, 2, 3, 0)
    set0 = np.zeros((32, 3, 8, 16), np.float32)
    s_of = (slice(24, 32), slice(0, 8))
    for half in range(2):
        u = slice(8 * half, 8 * half + 8)
        set0[s_of[half]] = w2[(0, 2, 4), u].transpose(1, 0, 2, 3)
        set0[8 + 8 * half:16 + 8 * half] = w2[(1, 3, 6), u].transpose(1, 0, 2, 3)

    def vector_sets(path, hidden):
        sets = np.zeros((2, 32, NB), np.float32)
        for k in range(3):
            o = slice(k * P, (k + 1) * P)
            sets[0, 8 * k:8 * k + 8, o] = w2[path, 0:8].reshape(8, P)
            to = sets[0, 24:32] if k == 0 else sets[1, 8 * (k - 1):8 * k]
            to[:, o] = w2[path, 8:16].reshape(8, P)
        if hidden:
            sets[1, 16:26, 3 * P:] = a["L2_gnn_W1"]
        return np.concatenate(list(sets), axis=1)
    arrays["w_f"] = np.tile(np.concatenate([set0.reshape(32, NA), vector_sets(5, True)], axis=1), (4, 1))
    arrays["w_sub"] = np.tile(vector_sets(6, False), (4, 1))
    rows32 = np.arange(P) % 32
    arrays["w121"] = np.where((rows32 >= 8) & (rows32 < 24), W121, 1.0).astype(np.float32)[:, None]
    r = np.arange(P)
    arrays["ident"] = np.eye(P, dtype=np.float32)
    arrays["before"] = (r[:, None] < r[None]).astype(np.float32)
    arrays["dump"] = (EP + r).astype(np.float32)[:, None]
    arrays["dump_n"] = (EP + np.arange(NPAD)).astype(np.float32).reshape(P, NT)
    arrays["plimit"] = ((r + 1) * J).astype(np.float32)[:, None]
    arrays["iota"] = np.tile(r.astype(np.float32)[None], (P, 1))
    arrays = {k: np.ascontiguousarray(v) for k, v in arrays.items()}

    nc = bacc.Bacc("TRN2", target_bir_lowering=False, num_devices=1)
    d = {k: nc.dram_tensor("in_" + k, v.shape, mybir.dt.from_np(v.dtype), kind="ExternalInput").ap()
         for k, v in arrays.items()}
    out = nc.dram_tensor("out", (N, F), F32, kind="ExternalOutput").ap()
    graph_kernel(nc, d, out)
    got = run_bass_kernel_spmd(nc, [{"in_" + k: v for k, v in arrays.items()}], core_ids=[0])
    return got.results[0]["out"]
```
